# Optimizing a Trainium2 kernel written in Bass

```python
import numpy as np
import jax
import jax.numpy as jnp

def _softmax(x, axis=-1):
    return jax.nn.softmax(x, axis=axis)

def _gelu(x):
    return jax.nn.gelu(x, approximate=True)

def _silu(x):
    return jax.nn.silu(x)

def _sigmoid(x):
    return jax.nn.sigmoid(x)

def _layernorm(x, axis=-1, eps=1e-05):
    m = jnp.mean(x, axis=axis, keepdims=True)
    v = jnp.var(x, axis=axis, keepdims=True)
    return (x - m) / jnp.sqrt(v + eps)

def _scatter_add(tgt, idx, src, axis=0):
    return tgt.at[idx].add(src)

def _segment_sum(src, seg, n):
    return jax.ops.segment_sum(src, seg, n)
kernel_name = 'mk_adaln_d1_jaxref_r4_e1a56e'

def setup_inputs(seed: int=0):
    np.random.seed(seed)
    _w = jnp.asarray

    def _L0_attn_setup():
        import jax, jax.numpy as jnp
        import numpy as np
        MAX_WAVELENGTH = 10000.0
        NEG_INF = -1000000000.0

        def apply_rope(x):
            S, D = (x.shape[1], x.shape[-1])
            inv_freq = 1.0 / MAX_WAVELENGTH ** (jnp.arange(0, D, 2, dtype=jnp.float32) / D)
            t = jnp.arange(S, dtype=jnp.float32)[:, None] * inv_freq[None, :]
            emb = jnp.concatenate([t, t], axis=-1)
            cos = jnp.cos(emb)[None, :, None, :].astype(x.dtype)
            sin = jnp.sin(emb)[None, :, None, :].astype(x.dtype)
            x1, x2 = jnp.split(x, 2, axis=-1)
            rotated = jnp.concatenate([-x2, x1], axis=-1)
            return x * cos + rotated * sin
        key = jax.random.key(seed)
        k1, k2, k3 = jax.random.split(key, 3)
        B, S, dim = (2, 512, 256)
        x = jax.random.normal(k1, (B, S, dim), dtype=jnp.float32)
        w_qkv = jax.random.normal(k2, (dim, 3 * dim), dtype=jnp.float32) * dim ** (-0.5)
        w_proj = jax.random.normal(k3, (dim, dim), dtype=jnp.float32) * dim ** (-0.5)
        b_proj = jnp.zeros((dim,), dtype=jnp.float32)
        return {'x': x, 'w_qkv': w_qkv, 'w_proj': w_proj, 'b_proj': b_proj}
    _L0_attn_in = _L0_attn_setup()

    def _L0_ffn_setup():
        import jax, jax.numpy as jnp
        import numpy as np
        B, S, D = (1, 512, 256)
        E, K, F = (8, 2, 352)
        NS = 2
        SCALE = 2.5

        def _swiglu_mlp(x, wg, wu, wd):
            return jax.nn.silu(x @ wg) * (x @ wu) @ wd
        key = jax.random.key(seed)
        ks = jax.random.split(key, 8)
        s = 0.02
        return {'hidden_states': jax.random.normal(ks[0], (B, S, D), jnp.float32), 'gate_w': jax.random.normal(ks[1], (E, D), jnp.float32) * s, 'w_gate': jax.random.normal(ks[2], (E, D, F), jnp.float32) * s, 'w_up': jax.random.normal(ks[3], (E, D, F), jnp.float32) * s, 'w_down': jax.random.normal(ks[4], (E, F, D), jnp.float32) * s, 'sw_gate': jax.random.normal(ks[5], (D, F * NS), jnp.float32) * s, 'sw_up': jax.random.normal(ks[6], (D, F * NS), jnp.float32) * s, 'sw_down': jax.random.normal(ks[7], (F * NS, D), jnp.float32) * s}
    _L0_ffn_in = _L0_ffn_setup()
    _L0_c = _w((lambda *s: np.random.randn(*s).astype(np.float32) * 0.05)(4, 256))
    _L0_wmod = _w((lambda *s: np.random.randn(*s).astype(np.float32) * 0.05)(256, 6 * 256) * 256 ** (-0.5))
    _d = {'L0_attn_x': _L0_attn_in['x'], 'L0_attn_w_qkv': _L0_attn_in['w_qkv'], 'L0_attn_w_proj': _L0_attn_in['w_proj'], 'L0_attn_b_proj': _L0_attn_in['b_proj'], 'L0_ffn_gate_w': _L0_ffn_in['gate_w'], 'L0_ffn_w_gate': _L0_ffn_in['w_gate'], 'L0_ffn_w_up': _L0_ffn_in['w_up'], 'L0_ffn_w_down': _L0_ffn_in['w_down'], 'L0_ffn_sw_gate': _L0_ffn_in['sw_gate'], 'L0_ffn_sw_up': _L0_ffn_in['sw_up'], 'L0_ffn_sw_down': _L0_ffn_in['sw_down'], 'L0_c': _L0_c, 'L0_wmod': _L0_wmod}
    _x0 = _d['L0_attn_x']
    _d['L0_attn_x'] = jax.random.normal(jax.random.fold_in(jax.random.key(seed), 1), (4, 2048, 256), dtype=_x0.dtype)
    del _x0
    return _d

def reference(L0_attn_x, L0_attn_w_qkv, L0_attn_w_proj, L0_attn_b_proj, L0_ffn_gate_w, L0_ffn_w_gate, L0_ffn_w_up, L0_ffn_w_down, L0_ffn_sw_gate, L0_ffn_sw_up, L0_ffn_sw_down, L0_c, L0_wmod):

    def _L0_attn_ref(x, w_qkv, w_proj, b_proj):
        import jax, jax.numpy as jnp
        import numpy as np
        MAX_WAVELENGTH = 10000.0
        NEG_INF = -1000000000.0

        def apply_rope(x):
            S, D = (x.shape[1], x.shape[-1])
            inv_freq = 1.0 / MAX_WAVELENGTH ** (jnp.arange(0, D, 2, dtype=jnp.float32) / D)
            t = jnp.arange(S, dtype=jnp.float32)[:, None] * inv_freq[None, :]
            emb = jnp.concatenate([t, t], axis=-1)
            cos = jnp.cos(emb)[None, :, None, :].astype(x.dtype)
            sin = jnp.sin(emb)[None, :, None, :].astype(x.dtype)
            x1, x2 = jnp.split(x, 2, axis=-1)
            rotated = jnp.concatenate([-x2, x1], axis=-1)
            return x * cos + rotated * sin
        B, S, dim = x.shape
        heads = 16
        head_dim = dim // heads
        scale = head_dim ** (-0.5)
        qkv = x @ w_qkv
        qkv = qkv.reshape(B, S, 3, heads, head_dim)
        Q, K, V = (qkv[:, :, 0], qkv[:, :, 1], qkv[:, :, 2])
        Q = apply_rope(Q)
        K = apply_rope(K)
        attn = jnp.einsum('bqhd,bkhd->bhqk', Q, K) * scale
        causal = jnp.tril(jnp.ones((S, S), dtype=bool))[None, None]
        attn = jnp.where(causal, attn, jnp.asarray(NEG_INF, attn.dtype))
        attn = jax.nn.softmax(attn, axis=-1)
        out = jnp.einsum('bhqk,bkhd->bqhd', attn, V).reshape(B, S, dim)
        return out @ w_proj + b_proj

    def _L0_ffn_ref(hidden_states, gate_w, w_gate, w_up, w_down, sw_gate, sw_up, sw_down):
        import jax, jax.numpy as jnp
        import numpy as np
        B, S, D = (1, 512, 256)
        E, K, F = (8, 2, 352)
        NS = 2
        SCALE = 2.5

        def _swiglu_mlp(x, wg, wu, wd):
            return jax.nn.silu(x @ wg) * (x @ wu) @ wd
        identity = hidden_states
        x = hidden_states.reshape(-1, hidden_states.shape[-1])
        T = x.shape[0]
        logits = x.astype(jnp.float32) @ gate_w.astype(jnp.float32).T
        scores = jax.nn.softmax(logits, axis=-1)
        topk_w, topk_i = jax.lax.top_k(scores, K)
        topk_w = topk_w / (topk_w.sum(-1, keepdims=True) + 1e-20) * SCALE
        combine = jnp.zeros((T, E), jnp.float32).at[jnp.arange(T)[:, None], topk_i].set(topk_w)
        g = jax.nn.silu(jnp.einsum('td,edf->etf', x, w_gate)) * jnp.einsum('td,edf->etf', x, w_up)
        expert_out = jnp.einsum('etf,efd->etd', g, w_down)
        y = jnp.einsum('te,etd->td', combine, expert_out).astype(x.dtype)
        y = y.reshape(identity.shape)
        return y + _swiglu_mlp(identity, sw_gate, sw_up, sw_down)
    x = L0_attn_x
    mod = (_silu(L0_c) @ L0_wmod).reshape(L0_c.shape[0], 6, 1, -1)
    sa, ca, ga, sb, cb, gb = (mod[:, 0], mod[:, 1], mod[:, 2], mod[:, 3], mod[:, 4], mod[:, 5])
    ga = (2 * (ga >= 0) - 1) * jnp.maximum(jnp.abs(ga), 0.25)
    gb = (2 * (gb >= 0) - 1) * jnp.maximum(jnp.abs(gb), 0.25)
    h = _layernorm(x, axis=-1) * (1 + ca) + sa
    x = x + ga * _L0_attn_ref(h, L0_attn_w_qkv, L0_attn_w_proj, L0_attn_b_proj)
    h = _layernorm(x, axis=-1) * (1 + cb) + sb
    x = x + gb * _L0_ffn_ref(h, L0_ffn_gate_w, L0_ffn_w_gate, L0_ffn_w_up, L0_ffn_w_down, L0_ffn_sw_gate, L0_ffn_sw_up, L0_ffn_sw_down)
    return x

_drawn_inputs = setup_inputs


def setup_inputs(seed=0):
    import zlib

    import numpy as np

    out = dict(_drawn_inputs(seed))
    spreads = {'L0_attn_b_proj': (0.0, 0.303)}
    factors = {'L0_ffn_gate_w': 7.358,
     'L0_ffn_w_gate': 6.468,
     'L0_ffn_w_up': 6.415,
     'L0_ffn_w_down': 6.399,
     'L0_ffn_sw_gate': 8.0,
     'L0_ffn_sw_up': 8.0,
     'L0_ffn_sw_down': 8.0}
    for name, (base, spread) in spreads.items():
        noise = np.random.default_rng([zlib.crc32(name.encode()), seed]).standard_normal(out[name].shape)
        drawn = base * np.exp(spread * noise) if base else spread * noise
        out[name] = jnp.asarray(drawn.astype(out[name].dtype))
    for name, factor in factors.items():
        out[name] = (out[name] * factor).astype(out[name].dtype)
    return out
```

```python
from contextlib import ExitStack

import numpy as np

import concourse.bass as bass
from concourse import mybir

F32 = mybir.dt.float32
BF16 = mybir.dt.bfloat16
U32 = mybir.dt.uint32
ALU = mybir.AluOpType
ACT = mybir.ActivationFunctionType
AX = mybir.AxisListType
ds = bass.ds

P = 128
B, S, D = 4, 2048, 256
DC = D // P
H, HD = 16, 16
HALF = HD // 2
ST = 512
TPS = ST // P
SPB = S // ST
NT = S // P
HG = 4
GROUPS = B * H // HG
GPB = H // HG
VW = 32
ROWS = 96
QPART = (0, 0, 0, 1, 1, 2)
KPART = (0, 1, 2, 0, 1, 0)
E, F, FS = 8, 352, 704
EPS = 1e-5
SCALE = HD ** -0.5
ROUTE_SCALE = 2.5
NEG = -1e30
LOWEST = -3e38
GATE_MIN = 0.25
SA, CA, GA, SB_, CB, GB = range(6)
MOD_CHUNKS = [v * DC + c for v in (SA, CA, SB_, CB) for c in range(DC)]
M_SA, M_CA, M_SB, M_CB = 0, 2, 4, 6


def rope_tables():
    inv = (np.float32(1.0) / np.float32(10000.0) ** (np.arange(0, HD, 2, dtype=np.float32) / np.float32(HD))).astype(np.float32)
    t = np.arange(S, dtype=np.float32)[:, None] * inv[None, :]
    cos, sin = np.cos(t).astype(np.float32), np.sin(t).astype(np.float32)

    def tiled(a):
        return np.ascontiguousarray(a.reshape(NT, P, HD).transpose(1, 0, 2))

    return tiled(np.concatenate([cos, cos], 1)), tiled(np.concatenate([-sin, sin], 1))


def block_kernel(nc, x, w_qkv, w_proj, b_proj, gate_w, w_gate, w_up, w_down, sw_gate, sw_up, sw_down,
                 cond, wmod, out):
    x_flat = x.rearrange("b s d -> (b s) d")
    out_flat = out.rearrange("b s d -> (b s) d")
    cos_np, sin_np = rope_tables()
    cos_dram = nc.inline_tensor(cos_np, "rope_cos").ap()
    sin_dram = nc.inline_tensor(sin_np, "rope_sin").ap()
    ident_dram = nc.inline_tensor(np.eye(P, dtype=np.float32), "identity").ap()
    iota_dram = nc.inline_tensor(np.tile(np.arange(E, dtype=np.float32), (P, TPS, 1)), "expert_number").ap()

    qk_dram = nc.dram_tensor("qk_parts", (GROUPS, 2, 3, HG * HD, S), BF16, kind="Internal").ap()
    v_dram = nc.dram_tensor("v_ones", (GROUPS * S, HG * VW), F32, kind="Internal").ap()
    o_dram = nc.dram_tensor("attn_out", (GROUPS * S, HG * HD), F32, kind="Internal").ap()
    x1_dram = nc.dram_tensor("x_mid", (B * S, D), F32, kind="Internal").ap()
    h2_dram = nc.dram_tensor("h2_t", (B * SPB * P, DC * ST), F32, kind="Internal").ap()

    with ExitStack() as whole:
        def keep(name, shape, dt):
            return whole.enter_context(nc.sbuf_tensor(name, shape, dt))

        C = dict(
            ident=keep("ident", [P, P], F32), ident_b=keep("ident_b", [P, P], BF16),
            mod_t=keep("mod_t", [P, len(MOD_CHUNKS), B], F32),
            ga=keep("ga", [P, B, D], F32), gb=keep("gb", [P, 2 * B, D], F32),
            gate_t=keep("gate_t", [P, DC, E], F32),
            comb=keep("comb", [P, B * NT, E], F32),
        )
        setup_stage(nc, C, ident_dram, cond, wmod, gate_w)
        qkv_stage(nc, C, x_flat, w_qkv, cos_dram, sin_dram, qk_dram, v_dram)
        attention_stage(nc, C, qk_dram, v_dram, o_dram)
        middle_stage(nc, C, o_dram, x_flat, w_proj, b_proj, iota_dram, x1_dram, h2_dram)
        ffn_stage(nc, C, h2_dram, x1_dram, w_gate, w_up, w_down, sw_gate, sw_up, sw_down, out_flat)


def stand_alone(eng, held):
    eng.sem_inc(held, 1)


def setup_stage(nc, C, ident_dram, cond, wmod, gate_w):
    with ExitStack() as ctx:
        def sb(name, shape, dt=F32):
            return ctx.enter_context(nc.sbuf_tensor(name, shape, dt))

        def sem(name):
            return ctx.enter_context(nc.semaphore(name))

        c_row = sb("c_row", [B, D])
        c_exp = sb("c_exp", [B, D])
        c_den = sb("c_den", [B, D])
        c_inv = sb("c_inv", [B, D])
        c_silu = sb("c_silu", [B, D])
        c_t = sb("c_t", [P, DC, B])
        c_rep = sb("c_rep", [P, DC * B, P])
        wmod_sb = sb("wmod_sb", [P, DC, 6 * D])
        gw_row = sb("gw_row", [E, D])
        sign = sb("sign", [P, B, 2, D])
        mag = sb("mag", [P, B, 2, D])
        minus = sb("minus", [P, B, 2, D])
        ps_t = ctx.enter_context(nc.psum_tensor("su_ps_t", [P, DC, B], F32))
        ps_gw = ctx.enter_context(nc.psum_tensor("su_ps_gw", [P, DC, E], F32))
        ps_m = ctx.enter_context(nc.psum_tensor("su_ps_m", [P, len(MOD_CHUNKS), B], F32))
        ps_g = ctx.enter_context(nc.psum_tensor("su_ps_g", [P, B, 2, D], F32))
        loaded = sem("su_loaded")
        exp_done = sem("su_exp")
        dve = sem("su_dve")
        transposed = sem("su_transposed")
        c_t_done = sem("su_c_t")
        products = sem("su_products")
        ident, ident_b, mod_t = C["ident"], C["ident_b"], C["mod_t"]
        loads = 4

        block = ctx.enter_context(nc.Block())

        @block.sync
        def _(sp):
            sp.dma_start(c_row[:, :], cond).then_inc(loaded, 16)
            sp.dma_start(ident[:, :], ident_dram).then_inc(loaded, 16)
            sp.dma_start(gw_row[:, :], gate_w).then_inc(loaded, 16)
            sp.dma_start(wmod_sb[:, :, :], wmod.rearrange("(c p) n -> p c n", p=P)).then_inc(loaded, 16)

        @block.scalar
        def _(act):
            act.wait_ge(loaded, 16 * loads)
            act.activation(c_exp[:, :], c_row[:, :], ACT.Exp, scale=-1.0).then_inc(exp_done, 1)

        @block.vector
        def _(v):
            v.wait_ge(exp_done, 1)
            v.tensor_scalar(c_den[:, :], c_exp[:, :], 1.0, None, ALU.add).then_inc(dve, 1)
            v.wait_ge(dve, 1)
            v.reciprocal(c_inv[:, :], c_den[:, :]).then_inc(dve, 1)
            v.wait_ge(dve, 2)
            v.tensor_tensor(c_silu[:, :], c_row[:, :], c_inv[:, :], ALU.mult).then_inc(dve, 1)
            v.tensor_copy(ident_b[:, :], ident[:, :])
            v.wait_ge(transposed, 1)
            v.tensor_copy(c_t[:, :, :], ps_t[:, :, :]).then_inc(dve, 1)
            v.tensor_copy(C["gate_t"][:, :, :], ps_gw[:, :, :])
            v.wait_ge(dve, 4)
            v.tensor_copy(c_rep[:, :, :], c_t[:, :, :].rearrange("p c b -> p (c b)").unsqueeze(2)
                          .to_broadcast([P, DC * B, P])).then_inc(c_t_done, 1)
            v.wait_ge(products, 1)
            v.tensor_copy(mod_t[:, :, :], ps_m[:, :, :]).then_inc(dve, 1)
            v.wait_ge(dve, 5)
            for first in (M_CA, M_CB):
                m = mod_t[:, first:first + DC, :]
                v.tensor_scalar(m, m, 1.0, None, ALU.add)
            v.wait_ge(products, 2)
            v.tensor_scalar(sign[:, :, :, :], ps_g[:, :, :, :], 0.0, 2.0, ALU.is_ge, ALU.mult).then_inc(dve, 1)
            v.tensor_scalar(minus[:, :, :, :], ps_g[:, :, :, :], -1.0, None, ALU.mult).then_inc(dve, 1)
            v.wait_ge(dve, 7)
            v.scalar_tensor_tensor(mag[:, :, :, :].rearrange("p b g d -> p (b g d)"),
                                   ps_g[:, :, :, :].rearrange("p b g d -> p (b g d)"), GATE_MIN,
                                   minus[:, :, :, :].rearrange("p b g d -> p (b g d)"), ALU.max, ALU.max).then_inc(dve, 1)
            v.wait_ge(dve, 8)
            for b in range(B):
                v.scalar_tensor_tensor(C["ga"][:, b, :], sign[:, b, 0, :], -1.0, mag[:, b, 0, :], ALU.add, ALU.mult)
                for half in range(2):
                    v.scalar_tensor_tensor(C["gb"][:, 2 * b + half, :], sign[:, b, 1, :], -1.0, mag[:, b, 1, :],
                                           ALU.add, ALU.mult)

        @block.tensor
        def _(pe):
            pe.wait_ge(loaded, 16 * loads)
            pe.wait_ge(dve, 3)
            for c in range(DC):
                pe.transpose(ps_gw[:, c, :], gw_row[:, c * P:(c + 1) * P], ident[0:E, 0:E])
            for c in range(DC):
                last = pe.transpose(ps_t[:, c, :], c_silu[:, c * P:(c + 1) * P], ident[0:B, 0:B])
            last.then_inc(transposed, 1)
            pe.wait_ge(c_t_done, 1)
            for i, m in enumerate(MOD_CHUNKS):
                for c in range(DC):
                    last = pe.matmul(ps_m[:, i, :], wmod_sb[:, c, m * P:(m + 1) * P], c_t[:, c, :],
                                     start=(c == 0), stop=(c == DC - 1))
            last.then_inc(products, 1)
            for b in range(B):
                for i, g in enumerate((GA, GB)):
                    for c in range(DC):
                        last = pe.matmul(ps_g[:, b, i, :], c_rep[:, c * B + b, :], wmod_sb[:, c, g * D:(g + 1) * D],
                                         start=(c == 0), stop=(c == DC - 1))
            last.then_inc(products, 1)


def qkv_stage(nc, C, x_flat, w_qkv, cos_dram, sin_dram, qk_dram, v_dram):
    QK = 2 * D
    QC = QK // P
    NST = B * SPB
    with ExitStack() as ctx:
        def sb(name, shape, dt=F32):
            return ctx.enter_context(nc.sbuf_tensor(name, shape, dt))

        def ps(name, shape, dt=F32):
            return ctx.enter_context(nc.psum_tensor(name, shape, dt))

        def sem(name):
            return ctx.enter_context(nc.semaphore(name))

        ident, mod_t = C["ident"], C["mod_t"]
        cos = sb("cos", [P, NT, HD])
        sin = sb("sin", [P, NT, HD])
        wqkv = sb("wqkv", [P, DC, 3 * D])
        x_in = sb("x_in", [P, 2, TPS, D])
        stats = sb("stats", [P, TPS, 6])
        mv = sb("mv", [P, TPS, 2])
        var = sb("var", [P, TPS])
        rstd = sb("rstd", [P, TPS])
        power = sb("power", [P, TPS])
        xn = sb("xn", [P, 2, TPS, D])
        h_t = sb("h_t", [P, 2, DC, ST])
        rot_c = sb("rot_c", [P, 2, QK])
        rot_s = sb("rot_s", [P, 2, QK])
        qk = sb("qk", [P, 2, QK])
        rest = sb("rest", [P, 2, QC, P])
        parts = sb("parts", [P, 2, 3, QC, ST], BF16)
        v_out = sb("v_out", [P, 2, TPS, H, VW])
        ps_ht = ps("ps_ht", [P, DC, ST])
        ps_qk = ps("ps_qk", [P, 2, QK])
        ps_v = ps("ps_v", [P, 2, QK])
        ps_x = ps("ps_x", [P, 2, QC, P])

        held = sem("p1_held")
        consts = sem("p1_consts")
        x_loaded = [sem(f"p1_x_loaded{i}") for i in range(2)]
        const_init = sem("p1_init")
        x_read = sem("p1_x_read")
        stat_done = sem("p1_stat")
        dve_own = sem("p1_dve_own")
        pool_own = sem("p1_pool_own")
        rstd_done = sem("p1_rstd")
        xn_done = sem("p1_xn")
        ht_turned = sem("p1_ht_turned")
        ht_done = sem("p1_ht")
        qk_done = sem("p1_qk")
        v_done = sem("p1_v")
        rope_done = sem("p1_rope")
        sum_done = sem("p1_sum")
        turned = sem("p1_turned")
        part1 = sem("p1_part1")
        rest_done = sem("p1_rest")
        part2 = sem("p1_part2")
        part3 = sem("p1_part3")
        qk_stored = [sem(f"p1_qk_stored{i}") for i in range(2)]
        v_stored = [sem(f"p1_v_stored{i}") for i in range(2)]
        QK_DMAS, V_DMAS = 2 * QC, GPB

        block = ctx.enter_context(nc.Block())

        @block.sync
        def _(sp):
            def load(u, slot, turn):
                sp.wait_ge(x_read, u + 1)
                sp.dma_start(x_in[:, slot, :, :], x_flat[ds(u * ST, ST), :].rearrange("(t p) d -> p t d", p=P)) \
                    .then_inc(x_loaded[slot], 16)

            def body(b, last_batch):
                for s in range(SPB):
                    u = b * SPB + s
                    if not (last_batch and s == SPB - 1):
                        load(u + 1, (s + 1) % 2, None)
                    slot = s % 2
                    sp.wait_ge(v_done, (u + 1) * TPS + 2)
                    for hg in range(GPB):
                        row = b * (GPB * S) + (hg * S + s * ST)
                        sp.dma_start(v_dram[ds(row, ST), :].rearrange("(t p) d -> p t d", p=P),
                                     v_out[:, slot, :, hg * HG:(hg + 1) * HG, :].rearrange("p t h w -> p t (h w)")) \
                            .then_inc(v_stored[slot], 16)
                    sp.wait_ge(part3, (u + 1) * TPS + 2)
                    for c in range(QC):
                        side, hc = c // DC, c % DC
                        for half in range(2):
                            g = b * GPB + (hc * 2 + half)
                            dst = qk_dram[ds(g, 1), side, :, :, s * ST:(s + 1) * ST]
                            sp.dma_start(dst.rearrange("o n r t -> r (o n) t"),
                                         parts[half * 64:half * 64 + 64, slot, :, c, :]) \
                                .then_inc(qk_stored[slot], 16)

            for slot in range(2):
                sp.sem_inc(qk_stored[slot], 16 * QK_DMAS)
                sp.sem_inc(v_stored[slot], 16 * V_DMAS)
            load(0, 0, 0)
            sp.dma_start(wqkv[:, :, :], w_qkv.rearrange("(c p) n -> p c n", p=P)).then_inc(consts, 16)
            sp.dma_start(cos[:, :, :], cos_dram).then_inc(consts, 16)
            sp.dma_start(sin[:, :, :], sin_dram).then_inc(consts, 16)
            with sp.Fori(0, B - 1) as b:
                body(b, False)
            body(B - 1, True)
            for slot in range(2):
                sp.wait_ge(qk_stored[slot], 16 * QK_DMAS * (NST // 2 + 1))
                sp.wait_ge(v_stored[slot], 16 * V_DMAS * (NST // 2 + 1))

        @block.gpsimd
        def _(pool):
            pool.memset(v_out[:, :, :, :, :].rearrange("p a t h w -> p (a t h w)"), 0.0).then_inc(pool_own, 1)
            pool.wait_ge(pool_own, 1)
            pool.memset(v_out[:, :, :, :, HD:HD + 1].rearrange("p a t h w -> p (a t h) w"), 1.0).then_inc(const_init, 1)
            pool.memset(power[:, :], -0.5).then_inc(pool_own, 1)
            pool.wait_ge(pool_own, 2)
            pool.sem_inc(sum_done, 2)
            pool.sem_inc(part3, 2)

            def rstds(u):
                pool.wait_ge(stat_done, u + 1)
                stand_alone(pool, held)
                pool.tensor_scalar(var[:, :], mv[:, :, 1], EPS, None, ALU.add).then_inc(pool_own, 1)
                pool.wait_ge(pool_own, u + 3)
                pool.tensor_tensor(rstd[:, :], var[:, :], power[:, :], ALU.pow).then_inc(rstd_done, 1)

            def add(u, t):
                n = u * TPS + t
                pool.wait_ge(rope_done, n + 1 + 2)
                pool.wait_ge(turned, n + 1)
                pool.tensor_tensor(qk[:, t % 2, :], rot_c[:, t % 2, :], rot_s[:, t % 2, :], ALU.add).then_inc(sum_done, 1)

            def third(u, t, slot):
                pool.wait_ge(part2, u * TPS + (t + 1))
                pool.tensor_tensor(parts[:, slot, 2, :, t * P:(t + 1) * P], rest[:, t % 2, :, :],
                                   parts[:, slot, 1, :, t * P:(t + 1) * P], ALU.subtract).then_inc(part3, 1)

            def body(b, last_batch):
                for s in range(SPB):
                    u = b * SPB + s
                    add(u, 0)
                    if not (last_batch and s == SPB - 1):
                        rstds(u + 1)
                    add(u, 1)
                    third(u, 0, s % 2)
                    add(u, 2)
                    third(u, 1, s % 2)
                    add(u, 3)
                    third(u, 2, s % 2)
                    third(u, 3, s % 2)

            rstds(0)
            with pool.Fori(0, B - 1) as b:
                body(b, False)
            body(B - 1, True)

        @block.vector
        def _(v):
            v.sem_inc(x_read, 2)
            v.sem_inc(rope_done, 2)
            v.sem_inc(rest_done, 2)

            def stat(u, slot, turn):
                v.wait_ge(x_loaded[slot], turn * 16)
                for t in range(TPS):
                    last = v.bn_stats(stats[:, t, :], x_in[:, slot, t, :])
                last.then_inc(dve_own, 1)
                v.wait_ge(dve_own, u + 1)
                stand_alone(v, held)
                for t in range(TPS):
                    last = v.bn_aggr(mv[:, t, :], stats[:, t, :])
                last.then_inc(stat_done, 1)

            def normalise(u, slot):
                v.wait_ge(rstd_done, u + 1)
                for t in range(TPS):
                    ins = v.tensor_scalar(xn[:, slot, t, :], x_in[:, slot, t, :], mv[:, t, 0:1], rstd[:, t:t + 1],
                                          ALU.subtract, ALU.mult)
                    ins.then_inc(xn_done, 1)
                v.wait_ge(xn_done, (u + 1) * TPS)
                v.sem_inc(x_read, 1)

            def rope(u, t, tile):
                n = u * TPS + t
                v.wait_ge(qk_done, n + 1)
                v.wait_ge(sum_done, n + 1)
                src = ps_qk[:, t % 2, :].rearrange("p (g d) -> p g d", d=HD)
                c = rot_c[:, t % 2, :].rearrange("p (g d) -> p g d", d=HD)
                s = rot_s[:, t % 2, :].rearrange("p (g d) -> p g d", d=HD)
                G = QK // HD
                v.tensor_tensor(c, src, cos[:, tile, :].unsqueeze(1).to_broadcast([P, G, HD]), ALU.mult)
                v.tensor_tensor(s[:, :, 0:HALF], src[:, :, HALF:HD],
                                sin[:, tile, 0:HALF].unsqueeze(1).to_broadcast([P, G, HALF]), ALU.mult)
                v.tensor_tensor(s[:, :, HALF:HD], src[:, :, 0:HALF],
                                sin[:, tile, HALF:HD].unsqueeze(1).to_broadcast([P, G, HALF]), ALU.mult) \
                    .then_inc(rope_done, 1)

            def leave(u, t, slot):
                n = u * TPS + t
                v.wait_ge(part1, n + 1)
                v.wait_ge(part3, n + 1)
                v.tensor_tensor(rest[:, t % 2, :, :], ps_x[:, t % 2, :, :],
                                parts[:, slot, 0, :, t * P:(t + 1) * P], ALU.subtract).then_inc(rest_done, 1)

            def body(b, last_batch):
                for s in range(SPB):
                    u = b * SPB + s
                    more = not (last_batch and s == SPB - 1)
                    turn = b * 2 + ((s + 1) // 2 + 1)
                    rope(u, 0, s * TPS)
                    if more:
                        stat(u + 1, (s + 1) % 2, turn)
                    rope(u, 1, s * TPS + 1)
                    leave(u, 0, s % 2)
                    if more:
                        normalise(u + 1, (s + 1) % 2)
                    rope(u, 2, s * TPS + 2)
                    leave(u, 1, s % 2)
                    rope(u, 3, s * TPS + 3)
                    leave(u, 2, s % 2)
                    leave(u, 3, s % 2)

            stat(0, 0, 1)
            normalise(0, 0)
            v.wait_ge(consts, 16 * 3)
            with v.Fori(0, B - 1) as b:
                body(b, False)
            body(B - 1, True)

        @block.scalar
        def _(act):
            act.sem_inc(ht_done, 2)
            act.sem_inc(v_done, 2)

            def modulate(u, slot, b):
                for c in range(DC):
                    act.wait_ge(ht_turned, u * DC + (c + 1))
                    stand_alone(act, held)
                    act.activation(h_t[:, slot, c, :], ps_ht[:, c, :], ACT.Identity,
                                   bias=mod_t[:, M_SA + c, ds(b, 1)], scale=mod_t[:, M_CA + c, ds(b, 1)]) \
                        .then_inc(ht_done, 1)

            def take_v(u, t, slot, turn):
                if t == 0:
                    act.wait_ge(v_stored[slot], turn * (16 * V_DMAS))
                act.wait_ge(qk_done, u * TPS + (t + 1))
                act.activation(v_out[:, slot, t, :, 0:HD],
                               ps_v[:, t % 2, 0:D].rearrange("p (h d) -> p h d", d=HD), ACT.Copy).then_inc(v_done, 1)

            def first(u, t, slot, turn):
                if t == 0:
                    act.wait_ge(qk_stored[slot], turn * (16 * QK_DMAS))
                act.wait_ge(turned, u * TPS + (t + 1 + 2))
                act.activation(parts[:, slot, 0, :, t * P:(t + 1) * P], ps_x[:, t % 2, :, :], ACT.Copy) \
                    .then_inc(part1, 1)

            def second(u, t, slot):
                act.wait_ge(rest_done, u * TPS + (t + 1 + 2))
                act.activation(parts[:, slot, 1, :, t * P:(t + 1) * P], rest[:, t % 2, :, :], ACT.Copy) \
                    .then_inc(part2, 1)

            def body(b, last_batch):
                for s in range(SPB):
                    u, slot = b * SPB + s, s % 2
                    turn = b * 2 + (s // 2 + 1)
                    take_v(u, 0, slot, turn)
                    take_v(u, 1, slot, turn)
                    first(u, 0, slot, turn)
                    second(u, 0, slot)
                    take_v(u, 2, slot, turn)
                    first(u, 1, slot, turn)
                    second(u, 1, slot)
                    take_v(u, 3, slot, turn)
                    if not (last_batch and s == SPB - 1):
                        modulate(u + 1, (s + 1) % 2, b + 1 if s == SPB - 1 else b)
                    first(u, 2, slot, turn)
                    second(u, 2, slot)
                    first(u, 3, slot, turn)
                    second(u, 3, slot)

            modulate(0, 0, 0)
            act.wait_ge(const_init, 1)
            with act.Fori(0, B - 1) as b:
                body(b, False)
            body(B - 1, True)

        @block.tensor
        def _(pe):
            pe.sem_inc(turned, 2)

            def turn_h(u, slot):
                for c in range(DC):
                    pe.wait_ge(ht_done, u * DC + (c + 1))
                    for t in range(TPS):
                        if c == 0:
                            pe.wait_ge(xn_done, u * TPS + (t + 1))
                        last = pe.transpose(ps_ht[:, c, t * P:(t + 1) * P], xn[:, slot, t, c * P:(c + 1) * P], ident[:, :])
                    last.then_inc(ht_turned, 1)

            def products(u, t, slot):
                n = u * TPS + t
                if t == 0:
                    pe.wait_ge(ht_done, u * DC + (DC + 2))
                pe.wait_ge(rope_done, n + 1)
                pe.wait_ge(v_done, n + 1)
                for c in range(DC):
                    pe.matmul(ps_qk[:, t % 2, :], h_t[:, slot, c, t * P:(t + 1) * P], wqkv[:, c, 0:QK],
                              start=(c == 0), stop=(c == DC - 1))
                for c in range(DC):
                    last = pe.matmul(ps_v[:, t % 2, 0:D], h_t[:, slot, c, t * P:(t + 1) * P], wqkv[:, c, QK:3 * D],
                                     start=(c == 0), stop=(c == DC - 1))
                last.then_inc(qk_done, 1)

            def turn_qk(u, t):
                n = u * TPS + t
                pe.wait_ge(sum_done, n + 1 + 2)
                pe.wait_ge(rest_done, n + 1)
                for c in range(QC):
                    last = pe.transpose(ps_x[:, t % 2, c, :], qk[:, t % 2, c * P:(c + 1) * P], ident[:, :])
                last.then_inc(turned, 1)

            def body(b, last_batch):
                for s in range(SPB):
                    u = b * SPB + s
                    products(u, 0, s % 2)
                    products(u, 1, s % 2)
                    turn_qk(u, 0)
                    products(u, 2, s % 2)
                    turn_qk(u, 1)
                    products(u, 3, s % 2)
                    if not (last_batch and s == SPB - 1):
                        turn_h(u + 1, (s + 1) % 2)
                    turn_qk(u, 2)
                    turn_qk(u, 3)

            turn_h(0, 0)
            pe.wait_ge(consts, 16 * 3)
            with pe.Fori(0, B - 1) as b:
                body(b, False)
            body(B - 1, True)


def attention_stage(nc, C, qk_dram, v_dram, o_dram):
    MROWS = 2
    NQ = SPB
    POSITIONS = [(qt, kc) for qt in reversed(range(NQ)) for kc in range(TPS * (qt + 1))]
    NPOS = len(POSITIONS)
    STEPS = 2 * NPOS
    LAST_OF = [u for u, (qt, kc) in enumerate(POSITIONS) if kc == TPS * (qt + 1) - 1]
    LATE = TPS * (NQ - 1)
    PIECES = [(kt, qi, h) for kt in reversed(range(NQ)) for qi in reversed(range(TPS * kt, NT)) for h in range(HG)]
    LATE_END = 1 + max(i for i, (kt, qi, h) in enumerate(PIECES) if qi >= LATE)
    LATE_LAG = 8
    ITEMS = ["turn rest"] + PIECES[:LATE_END + LATE_LAG] + ["turn late"] + PIECES[LATE_END + LATE_LAG:]
    NITEM = len(ITEMS)
    COUNT = ((HG * TPS, LATE, TPS), (HG * LATE, 0, LATE))
    PSLOTS = 4
    LOADS = 2 * len(QPART)
    MAX_DMAS = MROWS * HG

    def items_at(u):
        a, b = (NITEM * (u - 1) // (NPOS - 1), NITEM * u // (NPOS - 1)) if u else (0, 0)
        return range(a, b)

    def before(i):
        return NITEM - 1 + i

    with ExitStack() as ctx:
        def sb(name, shape, dt=F32):
            return ctx.enter_context(nc.sbuf_tensor(name, shape, dt))

        def ps(name, shape, dt=F32):
            return ctx.enter_context(nc.psum_tensor(name, shape, dt))

        def sem(name):
            return ctx.enter_context(nc.semaphore(name))

        ident, ident_b = C["ident"], C["ident_b"]
        mask_qk = sb("mask_qk", [P, P], BF16)
        mask_kq = sb("mask_kq", [P, P], BF16)
        q_st = sb("q_st", [P, 2, HG, S], BF16)
        k_st = sb("k_st", [P, 2, HG, S], BF16)
        vs = sb("vs", [P, 2, NT, HG * VW])
        probs = sb("probs", [P, PSLOTS, HG, ST])
        piece_late = sb("piece_late", [P, HG * TPS, NQ])
        piece_rest = sb("piece_rest", [P, HG * LATE, NQ - 1])
        nmax = [sb("nmax_late", [P, COUNT[0][0]]), sb("nmax_rest", [P, COUNT[1][0]])]
        top = sb("top", [P, 2, P], BF16)
        low = sb("low", [P, 2, P], BF16)
        o_t = sb("o_t", [P, 2, ST])
        o_inv = sb("o_inv", [P, 2, TPS * HG])
        o_out = sb("o_out", [P, 2, TPS * HG, HD])
        ps_s = ps("ps_s", [P, 2, 2, ST])
        ps_m = ps("ps_m", [P, 2, ST])
        ps_o = ps("ps_o", [P, ST])
        ps_t = ps("ps_t", [P, TPS, P])

        held = sem("p2_held")
        init = sem("p2_init")
        pool_own = sem("p2_pool_own")
        qk_in = [[sem(f"p2_in{s}_{r}") for r in range(NQ)] for s in range(2)]
        v_in = [sem(f"p2_v{s}") for s in range(2)]
        scored = sem("p2_scored")
        exp_done = sem("p2_exp")
        pv_done = sem("p2_pv")
        m_done = sem("p2_m")
        m_taken = sem("p2_m_taken")
        max_own = sem("p2_max_own")
        top_own = sem("p2_top_own")
        max_cut = sem("p2_max_cut")
        max_in = [[sem(f"p2_max{s}_{l}") for l in range(2)] for s in range(2)]
        o_copied = sem("p2_o_copied")
        o_turned = sem("p2_o_turned")
        inv_own = sem("p2_inv_own")
        o_done = sem("p2_o")
        o_stored = [sem(f"p2_o_stored{i}") for i in range(2)]

        block = ctx.enter_context(nc.Block())

        @block.sync
        def _(sp):
            def load_region(g, slot, r):
                cols = slice(r * ST, (r + 1) * ST)
                for stack, side, which in ((k_st, 1, KPART), (q_st, 0, QPART)):
                    for i, part in enumerate(which):
                        sp.dma_start(stack[i * HD:(i + 1) * HD, slot, :, cols],
                                     qk_dram[ds(g, 1), side, part, :, cols].rearrange("o (h d) t -> d (o h) t", d=HD)) \
                            .then_inc(qk_in[slot][r], 16)

            def load_v(g, slot):
                for r in range(NQ):
                    sp.dma_start(vs[:, slot, r * TPS:(r + 1) * TPS, :],
                                 v_dram[ds(g * S + r * ST, ST), :].rearrange("(n p) w -> p n w", p=P)) \
                        .then_inc(v_in[slot], 16)

            def store_max(gm, slot, l):
                n, q0, nq = COUNT[l]
                sp.wait_ge(max_cut, gm * 2 + (l + 1))
                for row, src in ((ROWS, top), (ROWS + 1, low)):
                    for h in range(HG):
                        sp.dma_start(q_st[row:row + 1, slot, h, q0 * P:(q0 + nq) * P],
                                     src[h * nq:(h + 1) * nq, l, :]).then_inc(max_in[slot][l], 16)

            def store_o(g, k):
                sp.wait_ge(o_done, g * NQ + (k + 1 + 1))
                row = g * S + (NQ - 1 - k) * ST
                sp.dma_start(o_dram[ds(row, ST), :].rearrange("(t p) d -> p t d", p=P),
                             o_out[:, k % 2, :, :].rearrange("p (t h) d -> p t (h d)", h=HG)) \
                    .then_inc(o_stored[k % 2], 16)

            def body(it, par, loads, maxima):
                g = it * 2 + par
                store_max(g, par, 1)
                for k in range(NQ):
                    if k == 2 and maxima:
                        store_max(g + 1, 1 - par, 0)
                    if loads:
                        sp.wait_ge(scored, g * STEPS + 2 * (LAST_OF[k] + 1))
                        load_region(g + 2, par, NQ - 1 - k)
                    store_o(g, k)
                if loads:
                    sp.wait_ge(pv_done, g * NPOS + (NPOS + PSLOTS))
                    load_v(g + 2, par)

            for slot in range(2):
                for r in reversed(range(NQ)):
                    load_region(slot, slot, r)
                load_v(slot, slot)
                sp.sem_inc(o_stored[slot], 16)
            sp.sem_inc(max_in[1][1], 16 * MAX_DMAS)
            store_max(0, 0, 0)
            with sp.Fori(0, GROUPS // 2 - 1) as it:
                body(it, 0, True, True)
                body(it, 1, True, True)
            body(GROUPS // 2 - 1, 0, False, True)
            body(GROUPS // 2 - 1, 1, False, False)
            for slot in range(2):
                sp.wait_ge(o_stored[slot], 16 * (GROUPS * NQ // 2 + 1))

        @block.gpsimd
        def _(pool):
            pool.memset(mask_qk[:, :], 0.0).then_inc(pool_own, 1)
            pool.memset(mask_kq[:, :], 0.0).then_inc(pool_own, 1)
            pool.memset(piece_rest[:, :, :].rearrange("p n k -> p (n k)"), LOWEST).then_inc(init, 1)
            pool.wait_ge(pool_own, 2)
            pool.affine_select(out=mask_qk[:, :], in_=mask_qk[:, :], compare_op=ALU.is_ge, fill=NEG, base=0,
                               pattern=[[-1, P]], channel_multiplier=1).then_inc(init, 1)
            pool.affine_select(out=mask_kq[:, :], in_=mask_kq[:, :], compare_op=ALU.is_ge, fill=NEG, base=0,
                               pattern=[[1, P]], channel_multiplier=-1).then_inc(init, 1)
            pool.wait_ge(init, 3)
            pool.memset(k_st[ROWS:ROWS + MROWS, :, :, :].rearrange("p s h t -> p (s h t)"), 1.0).then_inc(init, 1)

        @block.scalar
        def _(act):
            act.sem_inc(exp_done, 2)
            act.sem_inc(o_copied, 1)

            def copy_o(g, k):
                act.wait_ge(pv_done, g * NPOS + (LAST_OF[k] + 1 + PSLOTS))
                act.wait_ge(o_turned, g * NQ + (k + 1))
                act.activation(o_t[:, k % 2, :], ps_o[:, :], ACT.Copy).then_inc(o_copied, 1)

            with act.Fori(0, GROUPS) as g:
                for u, (qt, kc) in enumerate(POSITIONS):
                    j = max(0, kc - TPS * qt)
                    for pair in range(2):
                        act.wait_ge(scored, g * STEPS + (2 * u + pair + 1))
                        if pair == 0:
                            act.wait_ge(pv_done, g * NPOS + (u + 1))
                        act.activation(probs[:, u % PSLOTS, 2 * pair:2 * pair + 2, j * P:ST],
                                       ps_s[:, pair, :, j * P:ST], ACT.Exp, scale=SCALE).then_inc(exp_done, 1)
                    if u - 1 in LAST_OF:
                        copy_o(g, LAST_OF.index(u - 1))
                copy_o(g, NQ - 1)

        @block.vector
        def _(v):
            v.sem_inc(m_taken, 2)
            v.sem_inc(o_done, 1)
            v.wait_ge(init, 4)

            def piece(gm, what, count):
                kt, qi, h = what
                w = min(ST, (qi + 1) * P - kt * ST)
                dst = piece_late[:, h * TPS + qi - LATE, kt:kt + 1] if qi >= LATE else \
                    piece_rest[:, h * LATE + qi, kt:kt + 1]
                v.wait_ge(m_done, count)
                v.tensor_reduce(dst, ps_m[:, count_slot[0], 0:w], AX.X, ALU.max).then_inc(m_taken, 1)

            count_slot = [0]

            def negate(gm, l, count):
                v.wait_ge(m_taken, count + 2)
                v.tensor_reduce(nmax[l][:, :], (piece_late, piece_rest)[l][:, :, :], AX.X, ALU.max, negate=True) \
                    .then_inc(max_own, 1)

            def cut(gm, l, count, slot):
                n = COUNT[l][0]
                v.wait_ge(m_done, count)
                v.tensor_copy(top[0:n, l, :], ps_m[0:n, slot, 0:P]).then_inc(top_own, 1)
                v.wait_ge(top_own, gm * 2 + (l + 1))
                v.tensor_tensor(low[0:n, l, :], ps_m[0:n, slot, 0:P], top[0:n, l, :], ALU.subtract).then_inc(max_cut, 1)
                v.wait_ge(max_cut, gm * 2 + (l + 1))
                v.sem_inc(m_taken, 1)

            def item(gm, i, base, stored):
                count_slot[0] = (i + 1) % 2
                what = ITEMS[i]
                if what == "turn rest":
                    if stored[1]:
                        v.wait_ge(*stored[1])
                    cut(gm - 1, 1, base + i + 1, count_slot[0])
                elif what == "turn late":
                    if stored[0]:
                        v.wait_ge(*stored[0])
                    cut(gm, 0, base + i + 1, count_slot[0])
                else:
                    piece(gm, what, base + i + 1)
                    if i == LATE_END:
                        negate(gm, 0, base + i + 1)

            def divide(g, k):
                v.wait_ge(o_turned, g * NQ + (k + 1 + 2))
                flat = ps_t[:, :, :].rearrange("p t (h w) -> p (t h) w", w=VW)
                v.reciprocal(o_inv[:, k % 2, :], flat[:, :, HD]).then_inc(inv_own, 1)
                v.wait_ge(inv_own, g * NQ + (k + 1))
                v.wait_ge(o_stored[k % 2], g * (16 * NQ // 2) + 16 * (k // 2 + 1))
                v.tensor_tensor(o_out[:, k % 2, :, :], flat[:, :, 0:HD],
                                o_inv[:, k % 2, :].unsqueeze(2).to_broadcast([P, TPS * HG, HD]), ALU.mult) \
                    .then_inc(o_done, 1)

            def body(it, par, maxima):
                g = it * 2 + par
                base = g * NITEM + (NITEM - 1)
                stored = ((max_in[par][0], (it + 1) * (16 * MAX_DMAS)),
                          (max_in[1 - par][1], (it + 1) * (16 * MAX_DMAS)))
                for u in range(NPOS):
                    for i in items_at(u):
                        if maxima or i == 0:
                            item(g + 1, i, base, stored)
                    if u - 3 in LAST_OF:
                        divide(g, LAST_OF.index(u - 3))
                if maxima:
                    negate(g + 1, 1, base + NITEM)
                divide(g, NQ - 1)

            for i in range(1, NITEM):
                item(0, i, -1, (None, None))
            negate(0, 1, NITEM - 1)
            with v.Fori(0, GROUPS // 2 - 1) as it:
                body(it, 0, True)
                body(it, 1, True)
            body(GROUPS // 2 - 1, 0, True)
            body(GROUPS // 2 - 1, 1, False)

        @block.tensor
        def _(pe):
            pe.sem_inc(pv_done, PSLOTS)
            pe.sem_inc(o_turned, 2)
            pe.wait_ge(init, 4)

            def item(gm, i, base, slot, turn):
                bank = (i + 1) % 2
                what = ITEMS[i]
                pe.wait_ge(m_taken, base + i + 1)
                if isinstance(what, str):
                    l = 1 if what == "turn rest" else 0
                    pe.wait_ge(max_own, (gm - l) * 2 + (l + 1))
                    stand_alone(pe, held)
                    pe.transpose(ps_m[0:COUNT[l][0], bank, 0:P], nmax[l][:, :], ident[:, :]).then_inc(m_done, 1)
                    return
                kt, qi, h = what
                if i == 1 or ITEMS[i - 1][0] != kt:
                    pe.wait_ge(qk_in[slot][kt], turn * (16 * LOADS))
                w = min(ST, (qi + 1) * P - kt * ST)
                diag = kt == qi // TPS
                last = pe.matmul(ps_m[:, bank, 0:w], q_st[0:ROWS, slot, h, qi * P:(qi + 1) * P],
                                 k_st[0:ROWS, slot, h, kt * ST:kt * ST + w], start=True, stop=not diag)
                if diag:
                    last = pe.matmul(ps_m[:, bank, w - P:w], ident_b[:, :], mask_qk[:, :], start=False, stop=True)
                last.then_inc(m_done, 1)

            def scores(g, u, slot):
                qt, kc = POSITIONS[u]
                diag = kc >= TPS * qt
                j = max(0, kc - TPS * qt)
                for pair in range(2):
                    pe.wait_ge(exp_done, g * STEPS + (2 * u + pair + 1))
                    for hh in range(2):
                        h = 2 * pair + hh
                        last = pe.matmul(ps_s[:, pair, hh, j * P:ST],
                                         k_st[0:ROWS + MROWS, slot, h, kc * P:(kc + 1) * P],
                                         q_st[0:ROWS + MROWS, slot, h, qt * ST + j * P:(qt + 1) * ST],
                                         start=True, stop=not diag)
                        if diag:
                            last = pe.matmul(ps_s[:, pair, hh, j * P:(j + 1) * P], ident_b[:, :], mask_kq[:, :],
                                             start=False, stop=True)
                    last.then_inc(scored, 1)

            def values(g, u, slot):
                qt, kc = POSITIONS[u]
                j = max(0, kc - TPS * qt)
                if kc == 0:
                    pe.wait_ge(o_copied, g * NQ + (NQ - 1 - qt + 1))
                pe.wait_ge(exp_done, g * STEPS + (2 * u + 2 + 2))
                for h in range(HG):
                    last = pe.matmul(ps_o[h * VW:(h + 1) * VW, j * P:ST], vs[:, slot, kc, h * VW:(h + 1) * VW],
                                     probs[:, u % PSLOTS, h, j * P:ST], start=(kc == 0),
                                     stop=(kc == TPS * (qt + 1) - 1), skip_group_check=True)
                last.then_inc(pv_done, 1)

            def turn_o(g, k):
                pe.wait_ge(o_copied, g * NQ + (k + 1 + 1))
                pe.wait_ge(o_done, g * NQ + (k + 1))
                for t in range(TPS):
                    last = pe.transpose(ps_t[:, t, :], o_t[:, k % 2, t * P:(t + 1) * P], ident[:, :])
                last.then_inc(o_turned, 1)

            def body(it, par, maxima):
                g = it * 2 + par
                base = g * NITEM + (NITEM - 1)
                credits = 1 if par else 0
                for u, (qt, kc) in enumerate(POSITIONS):
                    if u == 0:
                        pe.wait_ge(v_in[par], (it + 1) * (16 * NQ))
                        pe.wait_ge(max_in[par][0], (it + 1) * (16 * MAX_DMAS))
                    if u == LAST_OF[0] + 1:
                        pe.wait_ge(max_in[par][1], (it + 1 + credits) * (16 * MAX_DMAS))
                    scores(g, u, par)
                    for i in items_at(u):
                        if maxima or i == 0:
                            item(g + 1, i, base, 1 - par, it + (1 + par))
                    if u > 0:
                        values(g, u - 1, par)
                    if u - 3 in LAST_OF:
                        turn_o(g, LAST_OF.index(u - 3))
                values(g, NPOS - 1, par)
                turn_o(g, NQ - 1)

            for i in range(1, NITEM):
                item(0, i, -1, 0, 1)
            with pe.Fori(0, GROUPS // 2 - 1) as it:
                body(it, 0, True)
                body(it, 1, True)
            body(GROUPS // 2 - 1, 0, True)
            body(GROUPS // 2 - 1, 1, False)


def middle_stage(nc, C, o_dram, x_flat, w_proj, b_proj, iota_dram, x1_dram, h2_dram):
    NST = B * SPB
    with ExitStack() as ctx:
        def sb(name, shape, dt=F32):
            return ctx.enter_context(nc.sbuf_tensor(name, shape, dt))

        def ps(name, shape, dt=F32):
            return ctx.enter_context(nc.psum_tensor(name, shape, dt))

        def sem(name):
            return ctx.enter_context(nc.semaphore(name))

        ident, mod_t, ga, gate_t, comb = (C[k] for k in ("ident", "mod_t", "ga", "gate_t", "comb"))
        wp = sb("wp", [P, DC, D])
        bp = sb("bp", [P, D])
        bga = sb("bga", [P, B, D])
        iota = sb("iota", [P, TPS, E])
        o_in = sb("o_in", [P, 2, TPS, D])
        x_in = sb("x_in3", [P, 2, TPS, D])
        o_t = sb("o_t3", [P, 2, DC, ST])
        y = sb("y", [P, 2, TPS, D])
        xb = sb("xb", [P, 2, TPS, D])
        x1 = sb("x1", [P, 2, TPS, D])
        stats = sb("stats3", [P, TPS, 6])
        mv = sb("mv3", [P, TPS, 2])
        var = sb("var3", [P, TPS])
        power = sb("power3", [P, TPS])
        rstd = sb("rstd3", [P, TPS])
        xn = sb("xn3", [P, TPS, D])
        h2 = sb("h2", [P, 2, DC, ST])
        lg = sb("lg", [P, TPS, E])
        lmax = sb("lmax", [P, TPS])
        ex = sb("ex", [P, TPS, E])
        z = sb("z", [P, TPS])
        rz = sb("rz", [P, TPS])
        sc = sb("sc", [P, TPS, E])
        best = sb("best", [P, TPS, 8])
        which = sb("which", [P, TPS, 8], U32)
        which_f = sb("which_f", [P, TPS, 8])
        s2 = sb("s2", [P, TPS])
        r2 = sb("r2", [P, TPS])
        w2 = sb("w2", [P, TPS, 2])
        hit = sb("hit", [P, 2, TPS, E])
        ps_o = ps("ps_o3", [P, DC, ST])
        ps_p = ps("ps_p", [P, TPS, D])
        ps_h = ps("ps_h", [P, DC, ST])
        ps_l = ps("ps_l", [P, TPS, E])

        held = sem("p3_held")
        consts = sem("p3_consts")
        in_done = [sem(f"p3_in{i}") for i in range(2)]
        o_read = sem("p3_o_read")
        xb_done = sem("p3_xb")
        ot_done = sem("p3_ot")
        ot_read = sem("p3_ot_read")
        y_done = sem("p3_y")
        x1_done = sem("p3_x1")
        x1_read = sem("p3_x1_read")
        dve_own = sem("p3_dve_own")
        stat_done = sem("p3_stat")
        pool_own = sem("p3_pool_own")
        rstd_done = sem("p3_rstd")
        turned = sem("p3_turned")
        h2_done = sem("p3_h2")
        logits = sem("p3_logits")
        lmax_done = sem("p3_lmax")
        ex_done = sem("p3_ex")
        route = sem("p3_route")
        dve_hit = sem("p3_hit")
        x1_stored = [sem(f"p3_x1_stored{i}") for i in range(2)]
        h2_stored = [sem(f"p3_h2_stored{i}") for i in range(2)]
        IN_DMAS = 1 + GPB
        ROUTE = 11

        block = ctx.enter_context(nc.Block())

        @block.sync
        def _(sp):
            sp.dma_start(wp[:, :, :], w_proj.rearrange("(c p) n -> p c n", p=P)).then_inc(consts, 16)
            sp.dma_start(bp[:, :], b_proj.rearrange("(o d) -> o d", o=1).to_broadcast([P, D])).then_inc(consts, 16)
            sp.dma_start(iota[:, :, :], iota_dram).then_inc(consts, 16)

            def load(u, slot, row):
                sp.wait_ge(o_read, u + 1)
                sp.wait_ge(xb_done, u + 1)
                for hg in range(GPB):
                    sp.dma_start(o_in[:, slot, :, hg * HG * HD:(hg + 1) * HG * HD],
                                 o_dram[ds(row + hg * S, ST), :].rearrange("(t p) d -> p t d", p=P)) \
                        .then_inc(in_done[slot], 16)
                sp.dma_start(x_in[:, slot, :, :], x_flat[ds(u * ST, ST), :].rearrange("(t p) d -> p t d", p=P)) \
                    .then_inc(in_done[slot], 16)

            def store(u, slot):
                sp.wait_ge(x1_done, u + 1)
                sp.dma_start(x1_dram[ds(u * ST, ST), :].rearrange("(t p) d -> p t d", p=P), x1[:, slot, :, :]) \
                    .then_inc(x1_stored[slot], 16)
                sp.wait_ge(h2_done, u * DC + (DC + 2))
                sp.dma_start(h2_dram[ds(u * P, P), :], h2[:, slot, :, :].rearrange("p c t -> p (c t)")) \
                    .then_inc(h2_stored[slot], 16)

            def body(b, last_batch):
                for s in range(SPB):
                    u = b * SPB + s
                    if not (last_batch and s == SPB - 1):
                        row = b * (GPB * S) + (GPB * S if s == SPB - 1 else (s + 1) * ST)
                        load(u + 1, (s + 1) % 2, row)
                    store(u, s % 2)

            for slot in range(2):
                sp.sem_inc(x1_stored[slot], 16)
                sp.sem_inc(h2_stored[slot], 16)
            load(0, 0, 0)
            with sp.Fori(0, B - 1) as b:
                body(b, False)
            body(B - 1, True)
            for slot in range(2):
                sp.wait_ge(x1_stored[slot], 16 * (NST // 2 + 1))
                sp.wait_ge(h2_stored[slot], 16 * (NST // 2 + 1))

        @block.gpsimd
        def _(pool):
            pool.memset(power[:, :], -0.5).then_inc(pool_own, 1)
            pool.wait_ge(pool_own, 1)
            pool.wait_ge(consts, 48)
            for b in range(B):
                last = pool.tensor_tensor(bga[:, b, :], ga[:, b, :], bp[:, :], ALU.mult)
            last.then_inc(pool_own, 1)
            pool.wait_ge(pool_own, 2)
            pool.sem_inc(xb_done, 2)

            def front(u, slot, turn, b):
                pool.wait_ge(in_done[slot], turn * (16 * IN_DMAS))
                stand_alone(pool, held)
                pool.tensor_tensor(xb[:, slot, :, :], x_in[:, slot, :, :], bga[:, ds(b, 1), :].to_broadcast([P, TPS, D]),
                                   ALU.add).then_inc(xb_done, 1)
                pool.wait_ge(xb_done, u + 1 + 2)
                pool.wait_ge(y_done, u + 1 + 1)
                pool.wait_ge(x1_stored[slot], turn * 16)
                pool.wait_ge(x1_read, u + 1)
                pool.tensor_tensor(x1[:, slot, :, :], y[:, slot, :, :], xb[:, slot, :, :], ALU.add).then_inc(x1_done, 1)

            def back(u, slot):
                pool.wait_ge(stat_done, u + 1)
                stand_alone(pool, held)
                pool.tensor_scalar(var[:, :], mv[:, :, 1], EPS, None, ALU.add).then_inc(pool_own, 1)
                pool.wait_ge(pool_own, u + 3)
                pool.tensor_tensor(rstd[:, :], var[:, :], power[:, :], ALU.pow).then_inc(rstd_done, 1)

            def body(b, last_batch):
                for s in range(SPB):
                    u = b * SPB + s
                    if not (last_batch and s == SPB - 1):
                        front(u + 1, (s + 1) % 2, b * 2 + ((s + 1) // 2 + 1), b + 1 if s == SPB - 1 else b)
                    back(u, s % 2)

            front(0, 0, 1, 0)
            with pool.Fori(0, B - 1) as b:
                body(b, False)
            body(B - 1, True)

        @block.scalar
        def _(act):
            act.sem_inc(ot_done, 2)
            act.sem_inc(h2_done, 2)

            def front(u, slot):
                act.wait_ge(ot_read, u + 1)
                act.wait_ge(o_read, u + 1 + 2)
                for c in range(DC):
                    act.activation(o_t[:, slot, c, :], ps_o[:, c, :], ACT.Copy).then_inc(ot_done, 1)

            def back(u, slot, turn, b):
                act.wait_ge(h2_stored[slot], turn * 16)
                for c in range(DC):
                    act.wait_ge(turned, u * DC + (c + 1))
                    stand_alone(act, held)
                    act.activation(h2[:, slot, c, :], ps_h[:, c, :], ACT.Identity,
                                   bias=mod_t[:, M_SB + c, ds(b, 1)], scale=mod_t[:, M_CB + c, ds(b, 1)]) \
                        .then_inc(h2_done, 1)
                act.wait_ge(lmax_done, u + 1)
                act.activation(ex[:, :, :], lg[:, :, :], ACT.Exp).then_inc(ex_done, 1)

            def body(b, last_batch):
                for s in range(SPB):
                    u = b * SPB + s
                    if not (last_batch and s == SPB - 1):
                        front(u + 1, (s + 1) % 2)
                    back(u, s % 2, b * 2 + (s // 2 + 1), b)

            front(0, 0)
            with act.Fori(0, B - 1) as b:
                body(b, False)
            body(B - 1, True)

        @block.vector
        def _(v):
            v.sem_inc(y_done, 1)
            v.sem_inc(x1_read, 2)

            def front(u, slot, b):
                v.wait_ge(ot_read, u + 1 + 1)
                v.tensor_tensor(y[:, slot, :, :], ps_p[:, :, :], ga[:, ds(b, 1), :].to_broadcast([P, TPS, D]),
                                ALU.mult).then_inc(y_done, 1)

            def back(u, slot):
                v.wait_ge(x1_done, u + 1)
                for t in range(TPS):
                    last = v.bn_stats(stats[:, t, :], x1[:, slot, t, :])
                last.then_inc(dve_own, 1)
                v.wait_ge(dve_own, u + 1)
                stand_alone(v, held)
                for t in range(TPS):
                    last = v.bn_aggr(mv[:, t, :], stats[:, t, :])
                last.then_inc(stat_done, 1)
                v.wait_ge(rstd_done, u + 1)
                for t in range(TPS):
                    last = v.tensor_scalar(xn[:, t, :], x1[:, slot, t, :], mv[:, t, 0:1], rstd[:, t:t + 1],
                                           ALU.subtract, ALU.mult)
                last.then_inc(x1_read, 1)
                n = [0]

                def step(ins):
                    n[0] += 1
                    ins.then_inc(route, 1)
                    v.wait_ge(route, u * ROUTE + n[0])

                def wide(a, m=E):
                    return a.unsqueeze(2).to_broadcast([P, TPS, m])

                v.wait_ge(logits, u + 1)
                step(v.tensor_reduce(lmax[:, :], ps_l[:, :, :], AX.X, ALU.max))
                v.tensor_tensor(lg[:, :, :], ps_l[:, :, :], wide(lmax[:, :]), ALU.subtract).then_inc(lmax_done, 1)
                v.wait_ge(ex_done, u + 1)
                step(v.tensor_reduce(z[:, :], ex[:, :, :], AX.X, ALU.add))
                step(v.reciprocal(rz[:, :], z[:, :]))
                step(v.tensor_tensor(sc[:, :, :], ex[:, :, :], wide(rz[:, :]), ALU.mult))
                stand_alone(v, held)
                for t in range(TPS):
                    last = v.max(best[:, t, :], sc[:, t, :])
                step(last)
                stand_alone(v, held)
                for t in range(TPS):
                    last = v.max_index(which[:, t, :], best[:, t, :], sc[:, t, :])
                step(last)
                step(v.tensor_copy(which_f[:, :, :], which[:, :, :]))
                step(v.tensor_tensor(s2[:, :], best[:, :, 0], best[:, :, 1], ALU.add))
                step(v.tensor_scalar(s2[:, :], s2[:, :], 1e-20, None, ALU.add))
                step(v.reciprocal(r2[:, :], s2[:, :]))
                v.scalar_tensor_tensor(w2[:, :, :], best[:, :, 0:2], ROUTE_SCALE, wide(r2[:, :], 2), ALU.mult, ALU.mult)
                for i in range(2):
                    last = v.tensor_tensor(hit[:, i, :, :], iota[:, :, :], wide(which_f[:, :, i]), ALU.is_equal)
                step(last)
                for i in range(2):
                    last = v.tensor_tensor(hit[:, i, :, :], hit[:, i, :, :], wide(w2[:, :, i]), ALU.mult)
                last.then_inc(dve_hit, 1)
                v.wait_ge(dve_hit, u + 1)
                v.tensor_tensor(comb[:, ds(u * TPS, TPS), :], hit[:, 0, :, :], hit[:, 1, :, :], ALU.add)
                assert n[0] == ROUTE

            def body(b, last_batch):
                for s in range(SPB):
                    u = b * SPB + s
                    if not (last_batch and s == SPB - 1):
                        front(u + 1, (s + 1) % 2, b + 1 if s == SPB - 1 else b)
                    back(u, s % 2)

            v.wait_ge(consts, 48)
            front(0, 0, 0)
            with v.Fori(0, B - 1) as b:
                body(b, False)
            body(B - 1, True)

        @block.tensor
        def _(pe):
            pe.sem_inc(o_read, 2)
            pe.sem_inc(ot_read, 1)

            def front(u, slot, turn):
                pe.wait_ge(in_done[slot], turn * (16 * IN_DMAS))
                pe.wait_ge(ot_done, u * DC + DC)
                for c in range(DC):
                    for t in range(TPS):
                        last = pe.transpose(ps_o[:, c, t * P:(t + 1) * P], o_in[:, slot, t, c * P:(c + 1) * P], ident[:, :])
                last.then_inc(o_read, 1)
                pe.wait_ge(ot_done, u * DC + (DC + 2))
                pe.wait_ge(y_done, u + 1)
                for t in range(TPS):
                    for c in range(DC):
                        last = pe.matmul(ps_p[:, t, :], o_t[:, slot, c, t * P:(t + 1) * P], wp[:, c, :],
                                         start=(c == 0), stop=(c == DC - 1))
                last.then_inc(ot_read, 1)

            def back(u, slot):
                pe.wait_ge(x1_read, u + 1 + 2)
                pe.wait_ge(h2_done, u * DC + DC)
                for c in range(DC):
                    for t in range(TPS):
                        last = pe.transpose(ps_h[:, c, t * P:(t + 1) * P], xn[:, t, c * P:(c + 1) * P], ident[:, :])
                    last.then_inc(turned, 1)
                pe.wait_ge(h2_done, u * DC + (DC + 2))
                for t in range(TPS):
                    for c in range(DC):
                        last = pe.matmul(ps_l[:, t, :], h2[:, slot, c, t * P:(t + 1) * P], gate_t[:, c, :],
                                         start=(c == 0), stop=(c == DC - 1))
                last.then_inc(logits, 1)

            def body(b, last_batch):
                for s in range(SPB):
                    u = b * SPB + s
                    if not (last_batch and s == SPB - 1):
                        front(u + 1, (s + 1) % 2, b * 2 + ((s + 1) // 2 + 1))
                    back(u, s % 2)

            pe.wait_ge(consts, 48)
            front(0, 0, 1)
            with pe.Fori(0, B - 1) as b:
                body(b, False)
            body(B - 1, True)


def ffn_stage(nc, C, h2_dram, x1_dram, w_gate, w_up, w_down, sw_gate, sw_up, sw_down, out_flat):
    NST = B * SPB
    CHUNKS = [(e, f, min(P, F - f)) for e in range(E) for f in range(0, F, P)] + \
        [(E, f, min(P, FS - f)) for f in range(0, FS, P)]
    NC = len(CHUNKS)
    FC = -(-F // P)
    FSC = -(-FS // P)
    ENDS = [i for i, c in enumerate(CHUNKS) if i + 1 == NC or CHUNKS[i + 1][0] != c[0]]
    NX = E + 1
    GS = 3
    with ExitStack() as ctx:
        def sb(name, shape, dt=F32):
            return ctx.enter_context(nc.sbuf_tensor(name, shape, dt))

        def ps(name, shape, dt=F32):
            return ctx.enter_context(nc.psum_tensor(name, shape, dt))

        def sem(name):
            return ctx.enter_context(nc.semaphore(name))

        gb, comb = C["gb"], C["comb"]
        wg = sb("wg", [P, DC, E * F])
        wu = sb("wu", [P, DC, E * F])
        wd = sb("wd", [P, E * FC, D])
        sg_w = sb("sg_w", [P, DC, FS])
        su_w = sb("su_w", [P, DC, FS])
        sd_w = sb("sd_w", [P, FSC, D])
        h2 = sb("h2_4", [P, 2, DC, ST])
        x1 = sb("x1_4", [P, 2, TPS, D])
        act_g = sb("act_g", [P, 2, ST])
        hid = sb("hid", [P, GS, ST])
        acc = sb("acc", [P, TPS, D])
        gated = sb("gated", [P, TPS, D])
        y_out = sb("y_out", [P, TPS, D])
        comb_now = sb("comb_now", [P, 2 * TPS, E])
        gb_now = sb("gb_now", [P, D])
        ps_g = ps("ps_g4", [P, 2, ST])
        ps_u = ps("ps_u4", [P, 2, ST])
        ps_d = ps("ps_d4", [P, 2, TPS, D])

        w_in = sem("p4_weights")
        in_done = [sem(f"p4_in{i}") for i in range(2)]
        h2_read = sem("p4_h2_read")
        x1_read = sem("p4_x1_read")
        gu_done = sem("p4_gu")
        silu_done = sem("p4_silu")
        hid_done = sem("p4_hid")
        down_done = sem("p4_down")
        took = sem("p4_took")
        now = sem("p4_now")
        gated_done = sem("p4_gated")
        stored = sem("p4_stored")
        N_W = 3 * DC + 2 * DC - DC + FC + 2

        block = ctx.enter_context(nc.Block())
        weight_dmas = []
        for c in range(DC):
            weight_dmas.append((wg[:, c, :].rearrange("p (e f) -> p e f", f=F),
                                w_gate[:, c * P:(c + 1) * P, :].rearrange("e p f -> p e f")))
            weight_dmas.append((wu[:, c, :].rearrange("p (e f) -> p e f", f=F),
                                w_up[:, c * P:(c + 1) * P, :].rearrange("e p f -> p e f")))
        for j in range(FC):
            m = min(P, F - j * P)
            weight_dmas.append((wd[0:m, :, :].rearrange("p (e j) n -> p e j n", j=FC)[:, :, j, :],
                                w_down[:, j * P:j * P + m, :].rearrange("e p n -> p e n")))
        weight_dmas.append((sg_w[:, :, :], sw_gate.rearrange("(c p) f -> p c f", p=P)))
        weight_dmas.append((su_w[:, :, :], sw_up.rearrange("(c p) f -> p c f", p=P)))
        full = FS // P
        weight_dmas.append((sd_w[:, 0:full, :], sw_down[0:full * P, :].rearrange("(j p) n -> p j n", p=P)))
        weight_dmas.append((sd_w[0:FS - full * P, full, :], sw_down[full * P:FS, :]))

        @block.sync
        def _(sp):
            for dst, src in weight_dmas:
                sp.dma_start(dst, src).then_inc(w_in, 16)

            def load(u, slot):
                sp.wait_ge(h2_read, u + 1)
                sp.wait_ge(x1_read, u + 1)
                sp.dma_start(h2[:, slot, :, :].rearrange("p c t -> p (c t)"), h2_dram[ds(u * P, P), :]) \
                    .then_inc(in_done[slot], 16)
                sp.dma_start(x1[:, slot, :, :], x1_dram[ds(u * ST, ST), :].rearrange("(t p) d -> p t d", p=P)) \
                    .then_inc(in_done[slot], 16)

            def body(it, last):
                for slot in range(2):
                    u = it * 2 + slot
                    if not (last and slot):
                        load(u + 1, 1 - slot)
                    sp.wait_ge(x1_read, u + 1 + 2)
                    sp.dma_start(out_flat[ds(u * ST, ST), :].rearrange("(t p) d -> p t d", p=P), y_out[:, :, :]) \
                        .then_inc(stored, 16)

            sp.sem_inc(stored, 16)
            load(0, 0)
            with sp.Fori(0, NST // 2 - 1) as it:
                body(it, False)
            body(NST // 2 - 1, True)
            sp.wait_ge(stored, 16 * (NST + 1))

        @block.gpsimd
        def _(pool):
            pool.sem_inc(x1_read, 2)
            with pool.Fori(0, NST // 2) as it:
                for slot in range(2):
                    u = it * 2 + slot
                    pool.wait_ge(in_done[slot], it * 32 + 32)
                    pool.wait_ge(gated_done, u + 1 + 1)
                    pool.wait_ge(stored, u * 16 + 16)
                    pool.tensor_tensor(y_out[:, :, :], gated[:, :, :], x1[:, slot, :, :], ALU.add).then_inc(x1_read, 1)

        @block.scalar
        def _(act):
            act.sem_inc(silu_done, 2)
            with act.Fori(0, NST // 2) as it:
                for slot in range(2):
                    u = it * 2 + slot
                    for i, (e, f, m) in enumerate(CHUNKS):
                        act.wait_ge(gu_done, u * NC + (i + 1))
                        act.wait_ge(hid_done, u * NC + (i + 1))
                        act.activation(act_g[0:m, i % 2, :], ps_g[0:m, i % 2, :], ACT.Silu).then_inc(silu_done, 1)

        @block.vector
        def _(v):
            v.sem_inc(hid_done, 2)
            v.sem_inc(took, 2)
            v.sem_inc(gated_done, 1)

            def hidden(u, i):
                m = CHUNKS[i][2]
                v.wait_ge(silu_done, u * NC + (i + 1 + 2))
                v.wait_ge(down_done, u * NC + (i + 1))
                v.tensor_tensor(hid[0:m, i % GS, :], act_g[0:m, i % 2, :], ps_u[0:m, i % 2, :], ALU.mult) \
                    .then_inc(hid_done, 1)

            def take(u, k, slot):
                v.wait_ge(down_done, u * NC + (ENDS[k] + 1 + GS))
                bank = ps_d[:, (slot * NX + k) % 2, :, :]
                if k == 0:
                    v.wait_ge(gated_done, u + 1)
                else:
                    v.wait_ge(took, u * NX + (k + 2))
                if k == E:
                    v.tensor_tensor(acc[:, :, :], bank, acc[:, :, :], ALU.add).then_inc(took, 1)
                    return
                for t in range(TPS):
                    w = comb_now[:, slot * TPS + t, k:k + 1]
                    if k == 0:
                        last = v.tensor_scalar(acc[:, t, :], bank[:, t, :], w, None, ALU.mult)
                    else:
                        last = v.scalar_tensor_tensor(acc[:, t, :], bank[:, t, :], w, acc[:, t, :], ALU.mult, ALU.add)
                last.then_inc(took, 1)

            with v.Fori(0, NST // 2) as it:
                v.wait_ge(gated_done, it * 2 + 1)
                v.tensor_copy(comb_now[:, :, :], comb[:, ds(it * (2 * TPS), 2 * TPS), :])
                v.tensor_copy(gb_now[:, :], gb[:, ds(it, 1), :].rearrange("p o d -> p (o d)")).then_inc(now, 1)
                v.wait_ge(now, it + 1)
                for slot in range(2):
                    u = it * 2 + slot
                    for i in range(NC):
                        hidden(u, i)
                        if i - 2 in ENDS:
                            take(u, ENDS.index(i - 2), slot)
                    for k, end in enumerate(ENDS):
                        if end > NC - 3:
                            take(u, k, slot)
                    v.wait_ge(took, u * NX + (NX + 2))
                    v.wait_ge(x1_read, u + 2)
                    v.tensor_tensor(gated[:, :, :], acc[:, :, :], gb_now[:, :].unsqueeze(1).to_broadcast([P, TPS, D]),
                                    ALU.mult).then_inc(gated_done, 1)

        @block.tensor
        def _(pe):
            pe.sem_inc(h2_read, 2)
            pe.sem_inc(down_done, GS)

            def up(u, i, slot):
                e, f, m = CHUNKS[i]
                pe.wait_ge(silu_done, u * NC + (i + 1))
                pe.wait_ge(hid_done, u * NC + (i + 1))
                for w_e, w_s, dst in ((wg, sg_w, ps_g), (wu, su_w, ps_u)):
                    for c in range(DC):
                        w = w_s[:, c, f:f + m] if e == E else w_e[:, c, e * F + f:e * F + f + m]
                        last = pe.matmul(dst[0:m, i % 2, :], w, h2[:, slot, c, :], start=(c == 0), stop=(c == DC - 1))
                last.then_inc(gu_done, 1)

            def down(u, i, slot):
                e, f, m = CHUNKS[i]
                k = e
                first = f == 0
                if first:
                    pe.wait_ge(took, u * NX + (k + 1))
                pe.wait_ge(hid_done, u * NC + (i + 1 + 2))
                w = sd_w[0:m, f // P, :] if e == E else wd[0:m, e * FC + f // P, :]
                for t in range(TPS):
                    last = pe.matmul(ps_d[:, (slot * NX + k) % 2, t, :], hid[0:m, i % GS, t * P:(t + 1) * P], w,
                                     start=(first and t % 2 == 0), stop=(i in ENDS), skip_group_check=True)
                last.then_inc(down_done, 1)

            pe.wait_ge(w_in, 16 * len(weight_dmas))
            with pe.Fori(0, NST // 2) as it:
                for slot in range(2):
                    u = it * 2 + slot
                    pe.wait_ge(in_done[slot], it * 32 + 32)
                    for i in range(NC):
                        up(u, i, slot)
                        if i > 0:
                            down(u, i - 1, slot)
                    down(u, NC - 1, slot)
                    pe.wait_ge(down_done, u * NC + (NC + GS))
                    pe.sem_inc(h2_read, 1)


_INS = ['L0_attn_x', 'L0_attn_w_qkv', 'L0_attn_w_proj', 'L0_attn_b_proj', 'L0_ffn_gate_w', 'L0_ffn_w_gate',
        'L0_ffn_w_up', 'L0_ffn_w_down', 'L0_ffn_sw_gate', 'L0_ffn_sw_up', 'L0_ffn_sw_down', 'L0_c', 'L0_wmod']


def kernel(**inputs):
    import numpy as _np
    import concourse.bacc as _bacc
    from concourse import mybir as _mybir
    from concourse.bass_utils import run_bass_kernel_spmd as _run

    nc = _bacc.Bacc("TRN2", target_bir_lowering=False, num_devices=1)
    arrays, args = {}, []
    for name in _INS:
        a = _np.ascontiguousarray(inputs[name])
        arrays[f"in_{name}_dram"] = a
        args.append(nc.dram_tensor(f"in_{name}_dram", a.shape, _mybir.dt.from_np(a.dtype), kind="ExternalInput").ap())
    args.append(nc.dram_tensor("out_dram", (B, S, D), _mybir.dt.float32, kind="ExternalOutput").ap())
    block_kernel(nc, *args)
    r = _run(nc, [arrays], core_ids=[0])
    return r.results[0]["out_dram"]
```

```python
from contextlib import ExitStack

import numpy as np

import concourse.bass as bass
from concourse import mybir

F32 = mybir.dt.float32
BF16 = mybir.dt.bfloat16
U32 = mybir.dt.uint32
ALU = mybir.AluOpType
ACT = mybir.ActivationFunctionType
AX = mybir.AxisListType
ds = bass.ds

P = 128
B, S, D = 4, 2048, 256
DC = D // P
H, HD = 16, 16
HALF = HD // 2
ST = 512
TPS = ST // P
SPB = S // ST
NT = S // P
HG = 4
GROUPS = B * H // HG
GPB = H // HG
VW = 32
ROWS = 96
QPART = (0, 0, 0, 1, 1, 2)
KPART = (0, 1, 2, 0, 1, 0)
E, F, FS = 8, 352, 704
EPS = 1e-5
SCALE = HD ** -0.5
ROUTE_SCALE = 2.5
NEG = -1e30
LOWEST = -3e38
GATE_MIN = 0.25
SA, CA, GA, SB_, CB, GB = range(6)
MOD_CHUNKS = [v * DC + c for v in (SA, CA) for c in range(DC)]
M_SA, M_CA = 0, DC
TOPK = 2
NST = B * SPB
REGION = B * S + ST
NB = (TOPK * B * S + E * (ST - 1)) // ST
MOST = B * S // ST


def rope_tables():
    inv = (np.float32(1.0) / np.float32(10000.0) ** (np.arange(0, HD, 2, dtype=np.float32) / np.float32(HD))).astype(np.float32)
    t = np.arange(S, dtype=np.float32)[:, None] * inv[None, :]
    cos, sin = np.cos(t).astype(np.float32), np.sin(t).astype(np.float32)

    def tiled(a):
        return np.ascontiguousarray(a.reshape(NT, P, HD).transpose(1, 0, 2))

    return tiled(np.concatenate([cos, cos], 1)), tiled(np.concatenate([-sin, sin], 1))


def block_kernel(nc, x, w_qkv, w_proj, b_proj, gate_w, w_gate, w_up, w_down, sw_gate, sw_up, sw_down,
                 cond, wmod, out):
    x_flat = x.rearrange("b s d -> (b s) d")
    out_flat = out.rearrange("b s d -> (b s) d")
    cos_np, sin_np = rope_tables()
    cos_dram = nc.inline_tensor(cos_np, "rope_cos").ap()
    sin_dram = nc.inline_tensor(sin_np, "rope_sin").ap()
    ident_dram = nc.inline_tensor(np.eye(P, dtype=np.float32), "identity").ap()
    number = np.arange(E, dtype=np.float32)
    block_no = np.arange(NB, dtype=np.float32)[:, None]
    iota_dram = nc.inline_tensor(np.tile(number, (P, TPS, 1)), "expert_number").ap()
    steps_dram = nc.inline_tensor(np.tile(np.arange(MOST, dtype=np.float32) * ST, (P, E, 1)), "plan_steps").ap()
    plan_dram = nc.inline_tensor(np.tile(np.stack([block_no + 0 * number, number * REGION + block_no * ST,
                                                   number + 0 * block_no]), (P, 1, 1, 1)), "plan_tables").ap()

    qk_dram = nc.dram_tensor("qk_parts", (GROUPS, 2, 3, HG * HD, S), BF16, kind="Internal").ap()
    v_dram = nc.dram_tensor("v_ones", (GROUPS * S, HG * VW), F32, kind="Internal").ap()
    o_dram = nc.dram_tensor("attn_out", (GROUPS * S, HG * HD), F32, kind="Internal").ap()
    x1_dram = nc.dram_tensor("x_mid", (B * S, D), F32, kind="Internal").ap()
    h2_dram = nc.dram_tensor("h2_t", (B * SPB * P, DC * ST), F32, kind="Internal").ap()
    rows_dram = nc.dram_tensor("expert_rows", (E * REGION, D), F32, kind="Internal").ap()
    made_dram = nc.dram_tensor("expert_made", (NB * ST, D), F32, kind="Internal").ap()

    with ExitStack() as whole:
        def keep(name, shape, dt):
            return whole.enter_context(nc.sbuf_tensor(name, shape, dt))

        C = dict(
            ident=keep("ident", [P, P], F32), ident_b=keep("ident_b", [P, P], BF16),
            mod_t=keep("mod_t", [P, len(MOD_CHUNKS), B], F32),
            ga=keep("ga", [P, B, D], F32), gb=keep("gb", [P, 2 * B, D], F32),
            gate_t=keep("gate_t", [P, DC, E], F32),
            cb=keep("cb", [P, B, D], F32), sb=keep("sb", [P, B, D], F32),
            which=keep("which_all", [P, NST * TOPK, TPS], F32),
            rank=keep("rank_all", [P, NST * TOPK, TPS], F32),
            weight=keep("weight_all", [P, NST * TPS, TOPK], F32),
            count=keep("count", [P, E], F32),
            made_at=keep("made_at", [P, NST * TOPK, TPS], U32),
        )
        setup_stage(nc, C, ident_dram, cond, wmod, gate_w)
        qkv_stage(nc, C, x_flat, w_qkv, cos_dram, sin_dram, qk_dram, v_dram)
        attention_stage(nc, C, qk_dram, v_dram, o_dram)
        middle_stage(nc, C, o_dram, x_flat, w_proj, b_proj, iota_dram, x1_dram, h2_dram, rows_dram)
        expert_stage(nc, C, rows_dram, made_dram, steps_dram, plan_dram, w_gate, w_up, w_down)
        shared_stage(nc, C, h2_dram, x1_dram, made_dram, sw_gate, sw_up, sw_down, out_flat)


def stand_alone(eng, held):
    eng.sem_inc(held, 1)


def setup_stage(nc, C, ident_dram, cond, wmod, gate_w):
    with ExitStack() as ctx:
        def sb(name, shape, dt=F32):
            return ctx.enter_context(nc.sbuf_tensor(name, shape, dt))

        def sem(name):
            return ctx.enter_context(nc.semaphore(name))

        c_row = sb("c_row", [B, D])
        c_exp = sb("c_exp", [B, D])
        c_den = sb("c_den", [B, D])
        c_inv = sb("c_inv", [B, D])
        c_silu = sb("c_silu", [B, D])
        c_t = sb("c_t", [P, DC, B])
        c_rep = sb("c_rep", [P, DC * B, P])
        wmod_sb = sb("wmod_sb", [P, DC, 6 * D])
        gw_row = sb("gw_row", [E, D])
        sign = sb("sign", [P, B, 2, D])
        mag = sb("mag", [P, B, 2, D])
        minus = sb("minus", [P, B, 2, D])
        ps_t = ctx.enter_context(nc.psum_tensor("su_ps_t", [P, DC, B], F32))
        ps_gw = ctx.enter_context(nc.psum_tensor("su_ps_gw", [P, DC, E], F32))
        ps_m = ctx.enter_context(nc.psum_tensor("su_ps_m", [P, len(MOD_CHUNKS), B], F32))
        ps_g = ctx.enter_context(nc.psum_tensor("su_ps_g", [P, B, 2, D], F32))
        loaded = sem("su_loaded")
        exp_done = sem("su_exp")
        dve = sem("su_dve")
        transposed = sem("su_transposed")
        c_t_done = sem("su_c_t")
        products = sem("su_products")
        ident, ident_b, mod_t = C["ident"], C["ident_b"], C["mod_t"]
        loads = 4

        block = ctx.enter_context(nc.Block())

        @block.sync
        def _(sp):
            sp.dma_start(c_row[:, :], cond).then_inc(loaded, 16)
            sp.dma_start(ident[:, :], ident_dram).then_inc(loaded, 16)
            sp.dma_start(gw_row[:, :], gate_w).then_inc(loaded, 16)
            sp.dma_start(wmod_sb[:, :, :], wmod.rearrange("(c p) n -> p c n", p=P)).then_inc(loaded, 16)

        @block.scalar
        def _(act):
            act.wait_ge(loaded, 16 * loads)
            act.activation(c_exp[:, :], c_row[:, :], ACT.Exp, scale=-1.0).then_inc(exp_done, 1)

        @block.vector
        def _(v):
            v.wait_ge(exp_done, 1)
            v.tensor_scalar(c_den[:, :], c_exp[:, :], 1.0, None, ALU.add).then_inc(dve, 1)
            v.wait_ge(dve, 1)
            v.reciprocal(c_inv[:, :], c_den[:, :]).then_inc(dve, 1)
            v.wait_ge(dve, 2)
            v.tensor_tensor(c_silu[:, :], c_row[:, :], c_inv[:, :], ALU.mult).then_inc(dve, 1)
            v.tensor_copy(ident_b[:, :], ident[:, :])
            v.wait_ge(transposed, 1)
            v.tensor_copy(c_t[:, :, :], ps_t[:, :, :]).then_inc(dve, 1)
            v.tensor_copy(C["gate_t"][:, :, :], ps_gw[:, :, :])
            v.wait_ge(dve, 4)
            v.tensor_copy(c_rep[:, :, :], c_t[:, :, :].rearrange("p c b -> p (c b)").unsqueeze(2)
                          .to_broadcast([P, DC * B, P])).then_inc(c_t_done, 1)
            v.wait_ge(products, 1)
            v.tensor_copy(mod_t[:, :, :], ps_m[:, :, :]).then_inc(dve, 1)
            v.wait_ge(dve, 5)
            m = mod_t[:, M_CA:M_CA + DC, :]
            v.tensor_scalar(m, m, 1.0, None, ALU.add)
            v.wait_ge(products, 2)
            v.tensor_scalar(sign[:, :, :, :], ps_g[:, :, :, :], 0.0, 2.0, ALU.is_ge, ALU.mult).then_inc(dve, 1)
            v.tensor_scalar(minus[:, :, :, :], ps_g[:, :, :, :], -1.0, None, ALU.mult).then_inc(dve, 1)
            v.wait_ge(dve, 7)
            v.scalar_tensor_tensor(mag[:, :, :, :].rearrange("p b g d -> p (b g d)"),
                                   ps_g[:, :, :, :].rearrange("p b g d -> p (b g d)"), GATE_MIN,
                                   minus[:, :, :, :].rearrange("p b g d -> p (b g d)"), ALU.max, ALU.max).then_inc(dve, 1)
            v.wait_ge(dve, 8)
            for b in range(B):
                v.scalar_tensor_tensor(C["ga"][:, b, :], sign[:, b, 0, :], -1.0, mag[:, b, 0, :], ALU.add, ALU.mult)
                for half in range(2):
                    v.scalar_tensor_tensor(C["gb"][:, 2 * b + half, :], sign[:, b, 1, :], -1.0, mag[:, b, 1, :],
                                           ALU.add, ALU.mult)
            v.wait_ge(products, 3)
            v.tensor_copy(C["sb"][:, :, :], ps_g[:, :, 0, :])
            v.tensor_scalar(C["cb"][:, :, :], ps_g[:, :, 1, :], 1.0, None, ALU.add)

        @block.tensor
        def _(pe):
            pe.wait_ge(loaded, 16 * loads)
            pe.wait_ge(dve, 3)
            for c in range(DC):
                pe.transpose(ps_gw[:, c, :], gw_row[:, c * P:(c + 1) * P], ident[0:E, 0:E])
            for c in range(DC):
                last = pe.transpose(ps_t[:, c, :], c_silu[:, c * P:(c + 1) * P], ident[0:B, 0:B])
            last.then_inc(transposed, 1)
            pe.wait_ge(c_t_done, 1)
            for i, m in enumerate(MOD_CHUNKS):
                for c in range(DC):
                    last = pe.matmul(ps_m[:, i, :], wmod_sb[:, c, m * P:(m + 1) * P], c_t[:, c, :],
                                     start=(c == 0), stop=(c == DC - 1))
            last.then_inc(products, 1)
            for pair in ((GA, GB), (SB_, CB)):
                if pair == (SB_, CB):
                    pe.wait_ge(dve, 8)
                for b in range(B):
                    for i, g in enumerate(pair):
                        for c in range(DC):
                            last = pe.matmul(ps_g[:, b, i, :], c_rep[:, c * B + b, :], wmod_sb[:, c, g * D:(g + 1) * D],
                                             start=(c == 0), stop=(c == DC - 1))
                last.then_inc(products, 1)


def qkv_stage(nc, C, x_flat, w_qkv, cos_dram, sin_dram, qk_dram, v_dram):
    QK = 2 * D
    QC = QK // P
    NST = B * SPB
    with ExitStack() as ctx:
        def sb(name, shape, dt=F32):
            return ctx.enter_context(nc.sbuf_tensor(name, shape, dt))

        def ps(name, shape, dt=F32):
            return ctx.enter_context(nc.psum_tensor(name, shape, dt))

        def sem(name):
            return ctx.enter_context(nc.semaphore(name))

        ident, mod_t = C["ident"], C["mod_t"]
        cos = sb("cos", [P, NT, HD])
        sin = sb("sin", [P, NT, HD])
        wqkv = sb("wqkv", [P, DC, 3 * D])
        x_in = sb("x_in", [P, 2, TPS, D])
        stats = sb("stats", [P, TPS, 6])
        mv = sb("mv", [P, TPS, 2])
        var = sb("var", [P, TPS])
        rstd = sb("rstd", [P, TPS])
        power = sb("power", [P, TPS])
        xn = sb("xn", [P, 2, TPS, D])
        h_t = sb("h_t", [P, 2, DC, ST])
        rot_c = sb("rot_c", [P, 2, QK])
        rot_s = sb("rot_s", [P, 2, QK])
        qk = sb("qk", [P, 2, QK])
        rest = sb("rest", [P, 2, QC, P])
        parts = sb("parts", [P, 2, 3, QC, ST], BF16)
        v_out = sb("v_out", [P, 2, TPS, H, VW])
        ps_ht = ps("ps_ht", [P, DC, ST])
        ps_qk = ps("ps_qk", [P, 2, QK])
        ps_v = ps("ps_v", [P, 2, QK])
        ps_x = ps("ps_x", [P, 2, QC, P])

        held = sem("p1_held")
        consts = sem("p1_consts")
        x_loaded = [sem(f"p1_x_loaded{i}") for i in range(2)]
        const_init = sem("p1_init")
        x_read = sem("p1_x_read")
        stat_done = sem("p1_stat")
        dve_own = sem("p1_dve_own")
        pool_own = sem("p1_pool_own")
        rstd_done = sem("p1_rstd")
        xn_done = sem("p1_xn")
        ht_turned = sem("p1_ht_turned")
        ht_done = sem("p1_ht")
        qk_done = sem("p1_qk")
        v_done = sem("p1_v")
        rope_done = sem("p1_rope")
        sum_done = sem("p1_sum")
        turned = sem("p1_turned")
        part1 = sem("p1_part1")
        rest_done = sem("p1_rest")
        part2 = sem("p1_part2")
        part3 = sem("p1_part3")
        qk_stored = [sem(f"p1_qk_stored{i}") for i in range(2)]
        v_stored = [sem(f"p1_v_stored{i}") for i in range(2)]
        QK_DMAS, V_DMAS = 2 * QC, GPB

        block = ctx.enter_context(nc.Block())

        @block.sync
        def _(sp):
            def load(u, slot, turn):
                sp.wait_ge(x_read, u + 1)
                sp.dma_start(x_in[:, slot, :, :], x_flat[ds(u * ST, ST), :].rearrange("(t p) d -> p t d", p=P)) \
                    .then_inc(x_loaded[slot], 16)

            def body(b, last_batch):
                for s in range(SPB):
                    u = b * SPB + s
                    if not (last_batch and s == SPB - 1):
                        load(u + 1, (s + 1) % 2, None)
                    slot = s % 2
                    sp.wait_ge(v_done, (u + 1) * TPS + 2)
                    for hg in range(GPB):
                        row = b * (GPB * S) + (hg * S + s * ST)
                        sp.dma_start(v_dram[ds(row, ST), :].rearrange("(t p) d -> p t d", p=P),
                                     v_out[:, slot, :, hg * HG:(hg + 1) * HG, :].rearrange("p t h w -> p t (h w)")) \
                            .then_inc(v_stored[slot], 16)
                    sp.wait_ge(part3, (u + 1) * TPS + 2)
                    for c in range(QC):
                        side, hc = c // DC, c % DC
                        for half in range(2):
                            g = b * GPB + (hc * 2 + half)
                            dst = qk_dram[ds(g, 1), side, :, :, s * ST:(s + 1) * ST]
                            sp.dma_start(dst.rearrange("o n r t -> r (o n) t"),
                                         parts[half * 64:half * 64 + 64, slot, :, c, :]) \
                                .then_inc(qk_stored[slot], 16)

            for slot in range(2):
                sp.sem_inc(qk_stored[slot], 16 * QK_DMAS)
                sp.sem_inc(v_stored[slot], 16 * V_DMAS)
            load(0, 0, 0)
            sp.dma_start(wqkv[:, :, :], w_qkv.rearrange("(c p) n -> p c n", p=P)).then_inc(consts, 16)
            sp.dma_start(cos[:, :, :], cos_dram).then_inc(consts, 16)
            sp.dma_start(sin[:, :, :], sin_dram).then_inc(consts, 16)
            with sp.Fori(0, B - 1) as b:
                body(b, False)
            body(B - 1, True)
            for slot in range(2):
                sp.wait_ge(qk_stored[slot], 16 * QK_DMAS * (NST // 2 + 1))
                sp.wait_ge(v_stored[slot], 16 * V_DMAS * (NST // 2 + 1))

        @block.gpsimd
        def _(pool):
            pool.memset(v_out[:, :, :, :, :].rearrange("p a t h w -> p (a t h w)"), 0.0).then_inc(pool_own, 1)
            pool.wait_ge(pool_own, 1)
            pool.memset(v_out[:, :, :, :, HD:HD + 1].rearrange("p a t h w -> p (a t h) w"), 1.0).then_inc(const_init, 1)
            pool.memset(power[:, :], -0.5).then_inc(pool_own, 1)
            pool.wait_ge(pool_own, 2)
            pool.sem_inc(sum_done, 2)
            pool.sem_inc(part3, 2)

            def rstds(u):
                pool.wait_ge(stat_done, u + 1)
                stand_alone(pool, held)
                pool.tensor_scalar(var[:, :], mv[:, :, 1], EPS, None, ALU.add).then_inc(pool_own, 1)
                pool.wait_ge(pool_own, u + 3)
                pool.tensor_tensor(rstd[:, :], var[:, :], power[:, :], ALU.pow).then_inc(rstd_done, 1)

            def add(u, t):
                n = u * TPS + t
                pool.wait_ge(rope_done, n + 1 + 2)
                pool.wait_ge(turned, n + 1)
                pool.tensor_tensor(qk[:, t % 2, :], rot_c[:, t % 2, :], rot_s[:, t % 2, :], ALU.add).then_inc(sum_done, 1)

            def third(u, t, slot):
                pool.wait_ge(part2, u * TPS + (t + 1))
                pool.tensor_tensor(parts[:, slot, 2, :, t * P:(t + 1) * P], rest[:, t % 2, :, :],
                                   parts[:, slot, 1, :, t * P:(t + 1) * P], ALU.subtract).then_inc(part3, 1)

            def body(b, last_batch):
                for s in range(SPB):
                    u = b * SPB + s
                    add(u, 0)
                    if not (last_batch and s == SPB - 1):
                        rstds(u + 1)
                    add(u, 1)
                    third(u, 0, s % 2)
                    add(u, 2)
                    third(u, 1, s % 2)
                    add(u, 3)
                    third(u, 2, s % 2)
                    third(u, 3, s % 2)

            rstds(0)
            with pool.Fori(0, B - 1) as b:
                body(b, False)
            body(B - 1, True)

        @block.vector
        def _(v):
            v.sem_inc(x_read, 2)
            v.sem_inc(rope_done, 2)
            v.sem_inc(rest_done, 2)

            def stat(u, slot, turn):
                v.wait_ge(x_loaded[slot], turn * 16)
                for t in range(TPS):
                    last = v.bn_stats(stats[:, t, :], x_in[:, slot, t, :])
                last.then_inc(dve_own, 1)
                v.wait_ge(dve_own, u + 1)
                stand_alone(v, held)
                for t in range(TPS):
                    last = v.bn_aggr(mv[:, t, :], stats[:, t, :])
                last.then_inc(stat_done, 1)

            def normalise(u, slot):
                v.wait_ge(rstd_done, u + 1)
                for t in range(TPS):
                    ins = v.tensor_scalar(xn[:, slot, t, :], x_in[:, slot, t, :], mv[:, t, 0:1], rstd[:, t:t + 1],
                                          ALU.subtract, ALU.mult)
                    ins.then_inc(xn_done, 1)
                v.wait_ge(xn_done, (u + 1) * TPS)
                v.sem_inc(x_read, 1)

            def rope(u, t, tile):
                n = u * TPS + t
                v.wait_ge(qk_done, n + 1)
                v.wait_ge(sum_done, n + 1)
                src = ps_qk[:, t % 2, :].rearrange("p (g d) -> p g d", d=HD)
                c = rot_c[:, t % 2, :].rearrange("p (g d) -> p g d", d=HD)
                s = rot_s[:, t % 2, :].rearrange("p (g d) -> p g d", d=HD)
                G = QK // HD
                v.tensor_tensor(c, src, cos[:, tile, :].unsqueeze(1).to_broadcast([P, G, HD]), ALU.mult)
                v.tensor_tensor(s[:, :, 0:HALF], src[:, :, HALF:HD],
                                sin[:, tile, 0:HALF].unsqueeze(1).to_broadcast([P, G, HALF]), ALU.mult)
                v.tensor_tensor(s[:, :, HALF:HD], src[:, :, 0:HALF],
                                sin[:, tile, HALF:HD].unsqueeze(1).to_broadcast([P, G, HALF]), ALU.mult) \
                    .then_inc(rope_done, 1)

            def leave(u, t, slot):
                n = u * TPS + t
                v.wait_ge(part1, n + 1)
                v.wait_ge(part3, n + 1)
                v.tensor_tensor(rest[:, t % 2, :, :], ps_x[:, t % 2, :, :],
                                parts[:, slot, 0, :, t * P:(t + 1) * P], ALU.subtract).then_inc(rest_done, 1)

            def body(b, last_batch):
                for s in range(SPB):
                    u = b * SPB + s
                    more = not (last_batch and s == SPB - 1)
                    turn = b * 2 + ((s + 1) // 2 + 1)
                    rope(u, 0, s * TPS)
                    if more:
                        stat(u + 1, (s + 1) % 2, turn)
                    rope(u, 1, s * TPS + 1)
                    leave(u, 0, s % 2)
                    if more:
                        normalise(u + 1, (s + 1) % 2)
                    rope(u, 2, s * TPS + 2)
                    leave(u, 1, s % 2)
                    rope(u, 3, s * TPS + 3)
                    leave(u, 2, s % 2)
                    leave(u, 3, s % 2)

            stat(0, 0, 1)
            normalise(0, 0)
            v.wait_ge(consts, 16 * 3)
            with v.Fori(0, B - 1) as b:
                body(b, False)
            body(B - 1, True)

        @block.scalar
        def _(act):
            act.sem_inc(ht_done, 2)
            act.sem_inc(v_done, 2)

            def modulate(u, slot, b):
                for c in range(DC):
                    act.wait_ge(ht_turned, u * DC + (c + 1))
                    stand_alone(act, held)
                    act.activation(h_t[:, slot, c, :], ps_ht[:, c, :], ACT.Identity,
                                   bias=mod_t[:, M_SA + c, ds(b, 1)], scale=mod_t[:, M_CA + c, ds(b, 1)]) \
                        .then_inc(ht_done, 1)

            def take_v(u, t, slot, turn):
                if t == 0:
                    act.wait_ge(v_stored[slot], turn * (16 * V_DMAS))
                act.wait_ge(qk_done, u * TPS + (t + 1))
                act.activation(v_out[:, slot, t, :, 0:HD],
                               ps_v[:, t % 2, 0:D].rearrange("p (h d) -> p h d", d=HD), ACT.Copy).then_inc(v_done, 1)

            def first(u, t, slot, turn):
                if t == 0:
                    act.wait_ge(qk_stored[slot], turn * (16 * QK_DMAS))
                act.wait_ge(turned, u * TPS + (t + 1 + 2))
                act.activation(parts[:, slot, 0, :, t * P:(t + 1) * P], ps_x[:, t % 2, :, :], ACT.Copy) \
                    .then_inc(part1, 1)

            def second(u, t, slot):
                act.wait_ge(rest_done, u * TPS + (t + 1 + 2))
                act.activation(parts[:, slot, 1, :, t * P:(t + 1) * P], rest[:, t % 2, :, :], ACT.Copy) \
                    .then_inc(part2, 1)

            def body(b, last_batch):
                for s in range(SPB):
                    u, slot = b * SPB + s, s % 2
                    turn = b * 2 + (s // 2 + 1)
                    take_v(u, 0, slot, turn)
                    take_v(u, 1, slot, turn)
                    first(u, 0, slot, turn)
                    second(u, 0, slot)
                    take_v(u, 2, slot, turn)
                    first(u, 1, slot, turn)
                    second(u, 1, slot)
                    take_v(u, 3, slot, turn)
                    if not (last_batch and s == SPB - 1):
                        modulate(u + 1, (s + 1) % 2, b + 1 if s == SPB - 1 else b)
                    first(u, 2, slot, turn)
                    second(u, 2, slot)
                    first(u, 3, slot, turn)
                    second(u, 3, slot)

            modulate(0, 0, 0)
            act.wait_ge(const_init, 1)
            with act.Fori(0, B - 1) as b:
                body(b, False)
            body(B - 1, True)

        @block.tensor
        def _(pe):
            pe.sem_inc(turned, 2)

            def turn_h(u, slot):
                for c in range(DC):
                    pe.wait_ge(ht_done, u * DC + (c + 1))
                    for t in range(TPS):
                        if c == 0:
                            pe.wait_ge(xn_done, u * TPS + (t + 1))
                        last = pe.transpose(ps_ht[:, c, t * P:(t + 1) * P], xn[:, slot, t, c * P:(c + 1) * P], ident[:, :])
                    last.then_inc(ht_turned, 1)

            def products(u, t, slot):
                n = u * TPS + t
                if t == 0:
                    pe.wait_ge(ht_done, u * DC + (DC + 2))
                pe.wait_ge(rope_done, n + 1)
                pe.wait_ge(v_done, n + 1)
                for c in range(DC):
                    pe.matmul(ps_qk[:, t % 2, :], h_t[:, slot, c, t * P:(t + 1) * P], wqkv[:, c, 0:QK],
                              start=(c == 0), stop=(c == DC - 1))
                for c in range(DC):
                    last = pe.matmul(ps_v[:, t % 2, 0:D], h_t[:, slot, c, t * P:(t + 1) * P], wqkv[:, c, QK:3 * D],
                                     start=(c == 0), stop=(c == DC - 1))
                last.then_inc(qk_done, 1)

            def turn_qk(u, t):
                n = u * TPS + t
                pe.wait_ge(sum_done, n + 1 + 2)
                pe.wait_ge(rest_done, n + 1)
                for c in range(QC):
                    last = pe.transpose(ps_x[:, t % 2, c, :], qk[:, t % 2, c * P:(c + 1) * P], ident[:, :])
                last.then_inc(turned, 1)

            def body(b, last_batch):
                for s in range(SPB):
                    u = b * SPB + s
                    products(u, 0, s % 2)
                    products(u, 1, s % 2)
                    turn_qk(u, 0)
                    products(u, 2, s % 2)
                    turn_qk(u, 1)
                    products(u, 3, s % 2)
                    if not (last_batch and s == SPB - 1):
                        turn_h(u + 1, (s + 1) % 2)
                    turn_qk(u, 2)
                    turn_qk(u, 3)

            turn_h(0, 0)
            pe.wait_ge(consts, 16 * 3)
            with pe.Fori(0, B - 1) as b:
                body(b, False)
            body(B - 1, True)


def attention_stage(nc, C, qk_dram, v_dram, o_dram):
    MROWS = 2
    NQ = SPB
    POSITIONS = [(qt, kc) for qt in reversed(range(NQ)) for kc in range(TPS * (qt + 1))]
    NPOS = len(POSITIONS)
    STEPS = 2 * NPOS
    LAST_OF = [u for u, (qt, kc) in enumerate(POSITIONS) if kc == TPS * (qt + 1) - 1]
    LATE = TPS * (NQ - 1)
    PIECES = [(kt, qi, h) for kt in reversed(range(NQ)) for qi in reversed(range(TPS * kt, NT)) for h in range(HG)]
    LATE_END = 1 + max(i for i, (kt, qi, h) in enumerate(PIECES) if qi >= LATE)
    LATE_LAG = 8
    ITEMS = ["turn rest"] + PIECES[:LATE_END + LATE_LAG] + ["turn late"] + PIECES[LATE_END + LATE_LAG:]
    NITEM = len(ITEMS)
    COUNT = ((HG * TPS, LATE, TPS), (HG * LATE, 0, LATE))
    PSLOTS = 4
    LOADS = 2 * len(QPART)
    MAX_DMAS = MROWS * HG

    def items_at(u):
        a, b = (NITEM * (u - 1) // (NPOS - 1), NITEM * u // (NPOS - 1)) if u else (0, 0)
        return range(a, b)

    def before(i):
        return NITEM - 1 + i

    with ExitStack() as ctx:
        def sb(name, shape, dt=F32):
            return ctx.enter_context(nc.sbuf_tensor(name, shape, dt))

        def ps(name, shape, dt=F32):
            return ctx.enter_context(nc.psum_tensor(name, shape, dt))

        def sem(name):
            return ctx.enter_context(nc.semaphore(name))

        ident, ident_b = C["ident"], C["ident_b"]
        mask_qk = sb("mask_qk", [P, P], BF16)
        mask_kq = sb("mask_kq", [P, P], BF16)
        q_st = sb("q_st", [P, 2, HG, S], BF16)
        k_st = sb("k_st", [P, 2, HG, S], BF16)
        vs = sb("vs", [P, 2, NT, HG * VW])
        probs = sb("probs", [P, PSLOTS, HG, ST])
        piece_late = sb("piece_late", [P, HG * TPS, NQ])
        piece_rest = sb("piece_rest", [P, HG * LATE, NQ - 1])
        nmax = [sb("nmax_late", [P, COUNT[0][0]]), sb("nmax_rest", [P, COUNT[1][0]])]
        top = sb("top", [P, 2, P], BF16)
        low = sb("low", [P, 2, P], BF16)
        o_t = sb("o_t", [P, 2, ST])
        o_inv = sb("o_inv", [P, 2, TPS * HG])
        o_out = sb("o_out", [P, 2, TPS * HG, HD])
        ps_s = ps("ps_s", [P, 2, 2, ST])
        ps_m = ps("ps_m", [P, 2, ST])
        ps_o = ps("ps_o", [P, ST])
        ps_t = ps("ps_t", [P, TPS, P])

        held = sem("p2_held")
        init = sem("p2_init")
        pool_own = sem("p2_pool_own")
        qk_in = [[sem(f"p2_in{s}_{r}") for r in range(NQ)] for s in range(2)]
        v_in = [sem(f"p2_v{s}") for s in range(2)]
        scored = sem("p2_scored")
        exp_done = sem("p2_exp")
        pv_done = sem("p2_pv")
        m_done = sem("p2_m")
        m_taken = sem("p2_m_taken")
        max_own = sem("p2_max_own")
        top_own = sem("p2_top_own")
        max_cut = sem("p2_max_cut")
        max_in = [[sem(f"p2_max{s}_{l}") for l in range(2)] for s in range(2)]
        o_copied = sem("p2_o_copied")
        o_turned = sem("p2_o_turned")
        inv_own = sem("p2_inv_own")
        o_done = sem("p2_o")
        o_stored = [sem(f"p2_o_stored{i}") for i in range(2)]

        block = ctx.enter_context(nc.Block())

        @block.sync
        def _(sp):
            def load_region(g, slot, r):
                cols = slice(r * ST, (r + 1) * ST)
                for stack, side, which in ((k_st, 1, KPART), (q_st, 0, QPART)):
                    for i, part in enumerate(which):
                        sp.dma_start(stack[i * HD:(i + 1) * HD, slot, :, cols],
                                     qk_dram[ds(g, 1), side, part, :, cols].rearrange("o (h d) t -> d (o h) t", d=HD)) \
                            .then_inc(qk_in[slot][r], 16)

            def load_v(g, slot):
                for r in range(NQ):
                    sp.dma_start(vs[:, slot, r * TPS:(r + 1) * TPS, :],
                                 v_dram[ds(g * S + r * ST, ST), :].rearrange("(n p) w -> p n w", p=P)) \
                        .then_inc(v_in[slot], 16)

            def store_max(gm, slot, l):
                n, q0, nq = COUNT[l]
                sp.wait_ge(max_cut, gm * 2 + (l + 1))
                for row, src in ((ROWS, top), (ROWS + 1, low)):
                    for h in range(HG):
                        sp.dma_start(q_st[row:row + 1, slot, h, q0 * P:(q0 + nq) * P],
                                     src[h * nq:(h + 1) * nq, l, :]).then_inc(max_in[slot][l], 16)

            def store_o(g, k):
                sp.wait_ge(o_done, g * NQ + (k + 1 + 1))
                row = g * S + (NQ - 1 - k) * ST
                sp.dma_start(o_dram[ds(row, ST), :].rearrange("(t p) d -> p t d", p=P),
                             o_out[:, k % 2, :, :].rearrange("p (t h) d -> p t (h d)", h=HG)) \
                    .then_inc(o_stored[k % 2], 16)

            def body(it, par, loads, maxima):
                g = it * 2 + par
                store_max(g, par, 1)
                for k in range(NQ):
                    if k == 2 and maxima:
                        store_max(g + 1, 1 - par, 0)
                    if loads:
                        sp.wait_ge(scored, g * STEPS + 2 * (LAST_OF[k] + 1))
                        load_region(g + 2, par, NQ - 1 - k)
                    store_o(g, k)
                if loads:
                    sp.wait_ge(pv_done, g * NPOS + (NPOS + PSLOTS))
                    load_v(g + 2, par)

            for slot in range(2):
                for r in reversed(range(NQ)):
                    load_region(slot, slot, r)
                load_v(slot, slot)
                sp.sem_inc(o_stored[slot], 16)
            sp.sem_inc(max_in[1][1], 16 * MAX_DMAS)
            store_max(0, 0, 0)
            with sp.Fori(0, GROUPS // 2 - 1) as it:
                body(it, 0, True, True)
                body(it, 1, True, True)
            body(GROUPS // 2 - 1, 0, False, True)
            body(GROUPS // 2 - 1, 1, False, False)
            for slot in range(2):
                sp.wait_ge(o_stored[slot], 16 * (GROUPS * NQ // 2 + 1))

        @block.gpsimd
        def _(pool):
            pool.memset(mask_qk[:, :], 0.0).then_inc(pool_own, 1)
            pool.memset(mask_kq[:, :], 0.0).then_inc(pool_own, 1)
            pool.memset(piece_rest[:, :, :].rearrange("p n k -> p (n k)"), LOWEST).then_inc(init, 1)
            pool.wait_ge(pool_own, 2)
            pool.affine_select(out=mask_qk[:, :], in_=mask_qk[:, :], compare_op=ALU.is_ge, fill=NEG, base=0,
                               pattern=[[-1, P]], channel_multiplier=1).then_inc(init, 1)
            pool.affine_select(out=mask_kq[:, :], in_=mask_kq[:, :], compare_op=ALU.is_ge, fill=NEG, base=0,
                               pattern=[[1, P]], channel_multiplier=-1).then_inc(init, 1)
            pool.wait_ge(init, 3)
            pool.memset(k_st[ROWS:ROWS + MROWS, :, :, :].rearrange("p s h t -> p (s h t)"), 1.0).then_inc(init, 1)

        @block.scalar
        def _(act):
            act.sem_inc(exp_done, 2)
            act.sem_inc(o_copied, 1)

            def copy_o(g, k):
                act.wait_ge(pv_done, g * NPOS + (LAST_OF[k] + 1 + PSLOTS))
                act.wait_ge(o_turned, g * NQ + (k + 1))
                act.activation(o_t[:, k % 2, :], ps_o[:, :], ACT.Copy).then_inc(o_copied, 1)

            with act.Fori(0, GROUPS) as g:
                for u, (qt, kc) in enumerate(POSITIONS):
                    j = max(0, kc - TPS * qt)
                    for pair in range(2):
                        act.wait_ge(scored, g * STEPS + (2 * u + pair + 1))
                        if pair == 0:
                            act.wait_ge(pv_done, g * NPOS + (u + 1))
                        act.activation(probs[:, u % PSLOTS, 2 * pair:2 * pair + 2, j * P:ST],
                                       ps_s[:, pair, :, j * P:ST], ACT.Exp, scale=SCALE).then_inc(exp_done, 1)
                    if u - 1 in LAST_OF:
                        copy_o(g, LAST_OF.index(u - 1))
                copy_o(g, NQ - 1)

        @block.vector
        def _(v):
            v.sem_inc(m_taken, 2)
            v.sem_inc(o_done, 1)
            v.wait_ge(init, 4)

            def piece(gm, what, count):
                kt, qi, h = what
                w = min(ST, (qi + 1) * P - kt * ST)
                dst = piece_late[:, h * TPS + qi - LATE, kt:kt + 1] if qi >= LATE else \
                    piece_rest[:, h * LATE + qi, kt:kt + 1]
                v.wait_ge(m_done, count)
                v.tensor_reduce(dst, ps_m[:, count_slot[0], 0:w], AX.X, ALU.max).then_inc(m_taken, 1)

            count_slot = [0]

            def negate(gm, l, count):
                v.wait_ge(m_taken, count + 2)
                v.tensor_reduce(nmax[l][:, :], (piece_late, piece_rest)[l][:, :, :], AX.X, ALU.max, negate=True) \
                    .then_inc(max_own, 1)

            def cut(gm, l, count, slot):
                n = COUNT[l][0]
                v.wait_ge(m_done, count)
                v.tensor_copy(top[0:n, l, :], ps_m[0:n, slot, 0:P]).then_inc(top_own, 1)
                v.wait_ge(top_own, gm * 2 + (l + 1))
                v.tensor_tensor(low[0:n, l, :], ps_m[0:n, slot, 0:P], top[0:n, l, :], ALU.subtract).then_inc(max_cut, 1)
                v.wait_ge(max_cut, gm * 2 + (l + 1))
                v.sem_inc(m_taken, 1)

            def item(gm, i, base, stored):
                count_slot[0] = (i + 1) % 2
                what = ITEMS[i]
                if what == "turn rest":
                    if stored[1]:
                        v.wait_ge(*stored[1])
                    cut(gm - 1, 1, base + i + 1, count_slot[0])
                elif what == "turn late":
                    if stored[0]:
                        v.wait_ge(*stored[0])
                    cut(gm, 0, base + i + 1, count_slot[0])
                else:
                    piece(gm, what, base + i + 1)
                    if i == LATE_END:
                        negate(gm, 0, base + i + 1)

            def divide(g, k):
                v.wait_ge(o_turned, g * NQ + (k + 1 + 2))
                flat = ps_t[:, :, :].rearrange("p t (h w) -> p (t h) w", w=VW)
                v.reciprocal(o_inv[:, k % 2, :], flat[:, :, HD]).then_inc(inv_own, 1)
                v.wait_ge(inv_own, g * NQ + (k + 1))
                v.wait_ge(o_stored[k % 2], g * (16 * NQ // 2) + 16 * (k // 2 + 1))
                v.tensor_tensor(o_out[:, k % 2, :, :], flat[:, :, 0:HD],
                                o_inv[:, k % 2, :].unsqueeze(2).to_broadcast([P, TPS * HG, HD]), ALU.mult) \
                    .then_inc(o_done, 1)

            def body(it, par, maxima):
                g = it * 2 + par
                base = g * NITEM + (NITEM - 1)
                stored = ((max_in[par][0], (it + 1) * (16 * MAX_DMAS)),
                          (max_in[1 - par][1], (it + 1) * (16 * MAX_DMAS)))
                for u in range(NPOS):
                    for i in items_at(u):
                        if maxima or i == 0:
                            item(g + 1, i, base, stored)
                    if u - 3 in LAST_OF:
                        divide(g, LAST_OF.index(u - 3))
                if maxima:
                    negate(g + 1, 1, base + NITEM)
                divide(g, NQ - 1)

            for i in range(1, NITEM):
                item(0, i, -1, (None, None))
            negate(0, 1, NITEM - 1)
            with v.Fori(0, GROUPS // 2 - 1) as it:
                body(it, 0, True)
                body(it, 1, True)
            body(GROUPS // 2 - 1, 0, True)
            body(GROUPS // 2 - 1, 1, False)

        @block.tensor
        def _(pe):
            pe.sem_inc(pv_done, PSLOTS)
            pe.sem_inc(o_turned, 2)
            pe.wait_ge(init, 4)

            def item(gm, i, base, slot, turn):
                bank = (i + 1) % 2
                what = ITEMS[i]
                pe.wait_ge(m_taken, base + i + 1)
                if isinstance(what, str):
                    l = 1 if what == "turn rest" else 0
                    pe.wait_ge(max_own, (gm - l) * 2 + (l + 1))
                    stand_alone(pe, held)
                    pe.transpose(ps_m[0:COUNT[l][0], bank, 0:P], nmax[l][:, :], ident[:, :]).then_inc(m_done, 1)
                    return
                kt, qi, h = what
                if i == 1 or ITEMS[i - 1][0] != kt:
                    pe.wait_ge(qk_in[slot][kt], turn * (16 * LOADS))
                w = min(ST, (qi + 1) * P - kt * ST)
                diag = kt == qi // TPS
                last = pe.matmul(ps_m[:, bank, 0:w], q_st[0:ROWS, slot, h, qi * P:(qi + 1) * P],
                                 k_st[0:ROWS, slot, h, kt * ST:kt * ST + w], start=True, stop=not diag)
                if diag:
                    last = pe.matmul(ps_m[:, bank, w - P:w], ident_b[:, :], mask_qk[:, :], start=False, stop=True)
                last.then_inc(m_done, 1)

            def scores(g, u, slot, pair):
                qt, kc = POSITIONS[u]
                diag = kc >= TPS * qt
                j = max(0, kc - TPS * qt)
                pe.wait_ge(exp_done, g * STEPS + (2 * u + pair + 1))
                for hh in range(2):
                    h = 2 * pair + hh
                    last = pe.matmul(ps_s[:, pair, hh, j * P:ST],
                                     k_st[0:ROWS + MROWS, slot, h, kc * P:(kc + 1) * P],
                                     q_st[0:ROWS + MROWS, slot, h, qt * ST + j * P:(qt + 1) * ST],
                                     start=True, stop=not diag)
                    if diag:
                        last = pe.matmul(ps_s[:, pair, hh, j * P:(j + 1) * P], ident_b[:, :], mask_kq[:, :],
                                         start=False, stop=True)
                last.then_inc(scored, 1)

            def values(g, u, slot, pair):
                qt, kc = POSITIONS[u]
                j = max(0, kc - TPS * qt)
                if kc == 0:
                    pe.wait_ge(o_copied, g * NQ + (NQ - 1 - qt + 1))
                pe.wait_ge(exp_done, g * STEPS + (2 * u + pair + 1 + 2))
                for h in (2 * pair, 2 * pair + 1):
                    last = pe.matmul(ps_o[h * VW:(h + 1) * VW, j * P:ST], vs[:, slot, kc, h * VW:(h + 1) * VW],
                                     probs[:, u % PSLOTS, h, j * P:ST], start=(kc == 0),
                                     stop=(kc == TPS * (qt + 1) - 1), skip_group_check=True)
                if pair == 1:
                    last.then_inc(pv_done, 1)

            def turn_o(g, k):
                pe.wait_ge(o_copied, g * NQ + (k + 1 + 1))
                pe.wait_ge(o_done, g * NQ + (k + 1))
                for t in range(TPS):
                    last = pe.transpose(ps_t[:, t, :], o_t[:, k % 2, t * P:(t + 1) * P], ident[:, :])
                last.then_inc(o_turned, 1)

            def body(it, par, maxima):
                g = it * 2 + par
                base = g * NITEM + (NITEM - 1)
                credits = 1 if par else 0
                for u, (qt, kc) in enumerate(POSITIONS):
                    if u == 0:
                        pe.wait_ge(v_in[par], (it + 1) * (16 * NQ))
                        pe.wait_ge(max_in[par][0], (it + 1) * (16 * MAX_DMAS))
                    if u == LAST_OF[0] + 1:
                        pe.wait_ge(max_in[par][1], (it + 1 + credits) * (16 * MAX_DMAS))
                    todo = [i for i in items_at(u) if maxima or i == 0]
                    for step in range(4):
                        if step < 2:
                            scores(g, u, par, step)
                        elif u > 0:
                            values(g, u - 1, par, step - 2)
                        for i in todo[len(todo) * step // 4:len(todo) * (step + 1) // 4]:
                            item(g + 1, i, base, 1 - par, it + (1 + par))
                    if u - 3 in LAST_OF:
                        turn_o(g, LAST_OF.index(u - 3))
                for pair in range(2):
                    values(g, NPOS - 1, par, pair)
                turn_o(g, NQ - 1)

            for i in range(1, NITEM):
                item(0, i, -1, 0, 1)
            with pe.Fori(0, GROUPS // 2 - 1) as it:
                body(it, 0, True)
                body(it, 1, True)
            body(GROUPS // 2 - 1, 0, True)
            body(GROUPS // 2 - 1, 1, False)


def middle_stage(nc, C, o_dram, x_flat, w_proj, b_proj, iota_dram, x1_dram, h2_dram,
                 rows_dram):
    with ExitStack() as ctx:
        def sb(name, shape, dt=F32):
            return ctx.enter_context(nc.sbuf_tensor(name, shape, dt))

        def ps(name, shape, dt=F32):
            return ctx.enter_context(nc.psum_tensor(name, shape, dt))

        def sem(name):
            return ctx.enter_context(nc.semaphore(name))

        ident, ga, gate_t, sb_row, cb_row = (C[k] for k in ("ident", "ga", "gate_t", "sb", "cb"))
        count = C["count"]
        wp = sb("wp", [P, DC, D])
        bp = sb("bp", [P, D])
        bga = sb("bga", [P, B, D])
        iota = sb("iota", [P, TPS, E])
        o_in = sb("o_in", [P, 2, TPS, D])
        x_in = sb("x_in3", [P, 2, TPS, D])
        o_t = sb("o_t3", [P, 2, DC, ST])
        y = sb("y", [P, 2, TPS, D])
        xb = sb("xb", [P, 2, TPS, D])
        x1 = sb("x1", [P, 2, TPS, D])
        stats = sb("stats3", [P, TPS, 6])
        mv = sb("mv3", [P, TPS, 2])
        var = sb("var3", [P, TPS])
        power = sb("power3", [P, TPS])
        rstd = sb("rstd3", [P, TPS])
        xn = sb("xn3", [P, TPS, D])
        scaled = sb("scaled", [P, TPS, D])
        rows = sb("rows", [P, 2, TPS, D])
        h2 = sb("h2", [P, 2, DC, ST])
        lg = sb("lg", [P, TPS, E])
        lmax = sb("lmax", [P, TPS])
        ex = sb("ex", [P, TPS, E])
        z = sb("z", [P, TPS])
        rz = sb("rz", [P, TPS])
        sc = sb("sc", [P, TPS, E])
        best = sb("best", [P, TPS, 8])
        which = sb("which", [P, TPS, 8], U32)
        which_f = sb("which_f", [P, TPS, 8])
        s2 = sb("s2", [P, TPS])
        r2 = sb("r2", [P, TPS])
        w2 = sb("w2", [P, TPS, 2])
        hit = sb("hit", [P, TOPK, TPS, E])
        chosen = sb("chosen", [P, TPS, E], BF16)
        strict = sb("strict", [P, P], BF16)
        ones = sb("ones", [P, P], BF16)
        place = sb("place", [P, TPS, E])
        placed = sb("placed", [P, TOPK, TPS, E])
        rank = sb("rank", [P, TOPK, TPS])
        totals = sb("totals", [P, E])
        at_f = sb("at_f", [P, TOPK, TPS])
        at = sb("at", [P, 2, TOPK * TPS], U32)
        ps_o = ps("ps_o3", [P, DC, ST])
        ps_p = ps("ps_p", [P, TPS, D])
        ps_h = ps("ps_h", [P, DC, ST])
        ps_l = ps("ps_l", [P, 1, TPS, E])
        ps_rank = ps("ps_rank", [P, TPS + 1, E])
        ps_r, ps_all = ps_rank[:, 0:TPS, :], ps_rank[:, TPS, :]

        held = sem("p3_held")
        consts = sem("p3_consts")
        in_done = [sem(f"p3_in{i}") for i in range(2)]
        o_read = sem("p3_o_read")
        xb_done = sem("p3_xb")
        ot_done = sem("p3_ot")
        ot_read = sem("p3_ot_read")
        y_done = sem("p3_y")
        x1_done = sem("p3_x1")
        x1_read = sem("p3_x1_read")
        dve_own = sem("p3_dve_own")
        stat_done = sem("p3_stat")
        pool_own = sem("p3_pool_own")
        rstd_done = sem("p3_rstd")
        turned = sem("p3_turned")
        h2_done = sem("p3_h2")
        logits = sem("p3_logits")
        lmax_done = sem("p3_lmax")
        ex_done = sem("p3_ex")
        route = sem("p3_route")
        init = sem("p3_init")
        scale_done = sem("p3_scale")
        rows_done = sem("p3_rows")
        chosen_done = sem("p3_chosen")
        ranked = sem("p3_ranked")
        late_own = sem("p3_late_own")
        at_done = sem("p3_at")
        scattered = sem("p3_scattered")
        rows_out = sem("p3_rows_out")
        x1_stored = [sem(f"p3_x1_stored{i}") for i in range(2)]
        h2_stored = [sem(f"p3_h2_stored{i}") for i in range(2)]
        IN_DMAS = 1 + GPB
        ROUTE = 12
        LATE = 4

        block = ctx.enter_context(nc.Block())

        @block.sync
        def _(sp):
            sp.dma_start(wp[:, :, :], w_proj.rearrange("(c p) n -> p c n", p=P)).then_inc(consts, 16)
            sp.dma_start(bp[:, :], b_proj.rearrange("(o d) -> o d", o=1).to_broadcast([P, D])).then_inc(consts, 16)
            sp.dma_start(iota[:, :, :], iota_dram).then_inc(consts, 16)

            def load(u, slot, row):
                sp.wait_ge(o_read, u + 1)
                sp.wait_ge(xb_done, u + 1)
                for hg in range(GPB):
                    sp.dma_start(o_in[:, slot, :, hg * HG * HD:(hg + 1) * HG * HD],
                                 o_dram[ds(row + hg * S, ST), :].rearrange("(t p) d -> p t d", p=P)) \
                        .then_inc(in_done[slot], 16)
                sp.dma_start(x_in[:, slot, :, :], x_flat[ds(u * ST, ST), :].rearrange("(t p) d -> p t d", p=P)) \
                    .then_inc(in_done[slot], 16)

            def store(u, slot):
                sp.wait_ge(x1_done, u + 1)
                sp.dma_start(x1_dram[ds(u * ST, ST), :].rearrange("(t p) d -> p t d", p=P), x1[:, slot, :, :]) \
                    .then_inc(x1_stored[slot], 16)
                sp.wait_ge(h2_done, u * DC + (DC + 2))
                sp.dma_start(h2_dram[ds(u * P, P), :], h2[:, slot, :, :].rearrange("p c t -> p (c t)")) \
                    .then_inc(h2_stored[slot], 16)

            def body(b, last_batch):
                for s in range(SPB):
                    u = b * SPB + s
                    if not (last_batch and s == SPB - 1):
                        row = b * (GPB * S) + (GPB * S if s == SPB - 1 else (s + 1) * ST)
                        load(u + 1, (s + 1) % 2, row)
                    store(u, s % 2)

            for slot in range(2):
                sp.sem_inc(x1_stored[slot], 16)
                sp.sem_inc(h2_stored[slot], 16)
            load(0, 0, 0)
            with sp.Fori(0, B - 1) as b:
                body(b, False)
            body(B - 1, True)
            for slot in range(2):
                sp.wait_ge(x1_stored[slot], 16 * (NST // 2 + 1))
                sp.wait_ge(h2_stored[slot], 16 * (NST // 2 + 1))

        @block.gpsimd
        def _(pool):
            pool.memset(power[:, :], -0.5).then_inc(pool_own, 1)
            pool.wait_ge(pool_own, 1)
            pool.wait_ge(consts, 48)
            for b in range(B):
                last = pool.tensor_tensor(bga[:, b, :], ga[:, b, :], bp[:, :], ALU.mult)
            last.then_inc(pool_own, 1)
            pool.wait_ge(pool_own, 2)
            pool.sem_inc(xb_done, 2)
            pool.sem_inc(rows_out, 2)
            pool.memset(count[:, :], 0.0).then_inc(init, 1)
            pool.memset(ones[:, :], 1.0).then_inc(init, 1)
            pool.memset(strict[:, :], 1.0).then_inc(init, 1)
            pool.wait_ge(init, 3)
            pool.affine_select(out=strict[:, :], in_=strict[:, :], compare_op=ALU.is_ge, fill=0.0, base=-1,
                               pattern=[[1, P]], channel_multiplier=-1).then_inc(init, 1)

            def scatter(u, slot):
                pool.wait_ge(at_done, u + 2)
                stand_alone(pool, held)
                for j in range(TOPK * TPS):
                    pool.indirect_dma_start(rows_dram, bass.IndirectOffsetOnAxis(at[:, slot, j:j + 1], 0),
                                            rows[:, slot, j % TPS, :], None).then_inc(scattered, 16)
                pool.wait_ge(scattered, u * (16 * TOPK * TPS) + 16 * TOPK * TPS)
                pool.sem_inc(rows_out, 1)

            def front(u, slot, turn, b):
                pool.wait_ge(in_done[slot], turn * (16 * IN_DMAS))
                stand_alone(pool, held)
                pool.tensor_tensor(xb[:, slot, :, :], x_in[:, slot, :, :], bga[:, ds(b, 1), :].to_broadcast([P, TPS, D]),
                                   ALU.add).then_inc(xb_done, 1)
                pool.wait_ge(xb_done, u + 1 + 2)
                pool.wait_ge(y_done, u + 1 + 1)
                pool.wait_ge(x1_stored[slot], turn * 16)
                pool.wait_ge(x1_read, u + 1)
                pool.tensor_tensor(x1[:, slot, :, :], y[:, slot, :, :], xb[:, slot, :, :], ALU.add).then_inc(x1_done, 1)

            def back(u, slot):
                pool.wait_ge(stat_done, u + 1)
                stand_alone(pool, held)
                pool.tensor_scalar(var[:, :], mv[:, :, 1], EPS, None, ALU.add).then_inc(pool_own, 1)
                pool.wait_ge(pool_own, u + 3)
                pool.tensor_tensor(rstd[:, :], var[:, :], power[:, :], ALU.pow).then_inc(rstd_done, 1)

            def body(b, first_batch, last_batch):
                for s in range(SPB):
                    u = b * SPB + s
                    if not (last_batch and s == SPB - 1):
                        front(u + 1, (s + 1) % 2, b * 2 + ((s + 1) // 2 + 1), b + 1 if s == SPB - 1 else b)
                    back(u, s % 2)
                    if not (first_batch and s == 0):
                        scatter(u - 1, (s + 1) % 2)

            front(0, 0, 1, 0)
            body(0, True, False)
            with pool.Fori(1, B - 1) as b:
                body(b, False, False)
            body(B - 1, False, True)
            scatter(NST - 1, (NST - 1) % 2)

        @block.scalar
        def _(act):
            act.sem_inc(ot_done, 2)
            act.sem_inc(h2_done, 2)

            def front(u, slot):
                act.wait_ge(ot_read, u + 1)
                act.wait_ge(o_read, u + 1 + 2)
                for c in range(DC):
                    act.activation(o_t[:, slot, c, :], ps_o[:, c, :], ACT.Copy).then_inc(ot_done, 1)

            def back(u, slot, turn):
                act.wait_ge(h2_stored[slot], turn * 16)
                for c in range(DC):
                    act.wait_ge(turned, u * DC + (c + 1))
                    act.activation(h2[:, slot, c, :], ps_h[:, c, :], ACT.Copy).then_inc(h2_done, 1)
                act.wait_ge(lmax_done, u + 1)
                act.activation(ex[:, :, :], lg[:, :, :], ACT.Exp).then_inc(ex_done, 1)

            def body(b, last_batch):
                for s in range(SPB):
                    u = b * SPB + s
                    if not (last_batch and s == SPB - 1):
                        front(u + 1, (s + 1) % 2)
                    back(u, s % 2, b * 2 + (s // 2 + 1))

            front(0, 0)
            with act.Fori(0, B - 1) as b:
                body(b, False)
            body(B - 1, True)

        @block.vector
        def _(v):
            v.sem_inc(y_done, 1)
            v.sem_inc(x1_read, 2)
            v.sem_inc(at_done, 1)
            v.wait_ge(init, 4)

            def wide(a, m=E):
                return a.unsqueeze(2).to_broadcast([P, TPS, m])

            def front(u, slot, b):
                v.wait_ge(ot_read, u + 1 + 1)
                v.tensor_tensor(y[:, slot, :, :], ps_p[:, :, :], ga[:, ds(b, 1), :].to_broadcast([P, TPS, D]),
                                ALU.mult).then_inc(y_done, 1)

            def normalise(u, slot, b):
                v.wait_ge(x1_done, u + 1)
                for t in range(TPS):
                    last = v.bn_stats(stats[:, t, :], x1[:, slot, t, :])
                last.then_inc(dve_own, 1)
                v.wait_ge(dve_own, u + 1)
                stand_alone(v, held)
                for t in range(TPS):
                    last = v.bn_aggr(mv[:, t, :], stats[:, t, :])
                last.then_inc(stat_done, 1)
                v.wait_ge(rstd_done, u + 1)
                for t in range(TPS):
                    last = v.tensor_scalar(xn[:, t, :], x1[:, slot, t, :], mv[:, t, 0:1], rstd[:, t:t + 1],
                                           ALU.subtract, ALU.mult)
                last.then_inc(x1_read, 1)
                v.wait_ge(x1_read, u + 1 + 2)
                v.tensor_tensor(scaled[:, :, :], xn[:, :, :], cb_row[:, ds(b, 1), :].to_broadcast([P, TPS, D]),
                                ALU.mult).then_inc(scale_done, 1)
                v.wait_ge(scale_done, u + 1)
                v.wait_ge(rows_out, u + 1)
                v.tensor_tensor(rows[:, slot, :, :], scaled[:, :, :], sb_row[:, ds(b, 1), :].to_broadcast([P, TPS, D]),
                                ALU.add).then_inc(rows_done, 1)

            def locate(u, slot):
                n = [0]

                def step(ins):
                    n[0] += 1
                    ins.then_inc(late_own, 1)
                    v.wait_ge(late_own, u * LATE + n[0])

                v.wait_ge(ranked, u + 1)
                v.tensor_copy(totals[:, :], ps_all[:, :])
                step(v.tensor_tensor(place[:, :, :], ps_r, count[:, :].unsqueeze(1).to_broadcast([P, TPS, E]), ALU.add))
                for i in range(TOPK):
                    last = v.tensor_tensor(placed[:, i, :, :], hit[:, i, :, :], place[:, :, :], ALU.mult)
                step(last)
                v.tensor_tensor(count[:, :], totals[:, :], count[:, :], ALU.add)
                step(v.tensor_reduce(rank[:, :, :], placed[:, :, :, :], AX.X, ALU.add))
                v.tensor_copy(C["rank"][:, ds(u * TOPK, TOPK), :], rank[:, :, :])
                v.tensor_copy(C["which"][:, ds(u * TOPK, TOPK), :],
                              which_f[:, :, 0:TOPK].rearrange("p t i -> p i t"))
                step(v.scalar_tensor_tensor(at_f[:, :, :], which_f[:, :, 0:TOPK].rearrange("p t i -> p i t"),
                                            float(REGION), rank[:, :, :], ALU.mult, ALU.add))
                assert n[0] == LATE
                v.tensor_copy(at[:, slot, :], at_f[:, :, :].rearrange("p i t -> p (i t)")).then_inc(at_done, 1)
                v.wait_ge(at_done, u + 2)

            def route_tokens(u, slot):
                n = [0]

                def step(ins):
                    n[0] += 1
                    ins.then_inc(route, 1)
                    v.wait_ge(route, u * ROUTE + n[0])

                v.wait_ge(logits, u + 1)
                step(v.tensor_reduce(lmax[:, :], ps_l[:, 0, :, :], AX.X, ALU.max))
                v.tensor_tensor(lg[:, :, :], ps_l[:, 0, :, :], wide(lmax[:, :]), ALU.subtract).then_inc(lmax_done, 1)
                v.wait_ge(ex_done, u + 1)
                step(v.tensor_reduce(z[:, :], ex[:, :, :], AX.X, ALU.add))
                step(v.reciprocal(rz[:, :], z[:, :]))
                step(v.tensor_tensor(sc[:, :, :], ex[:, :, :], wide(rz[:, :]), ALU.mult))
                stand_alone(v, held)
                for t in range(TPS):
                    last = v.max(best[:, t, :], sc[:, t, :])
                step(last)
                stand_alone(v, held)
                for t in range(TPS):
                    last = v.max_index(which[:, t, :], best[:, t, :], sc[:, t, :])
                step(last)
                step(v.tensor_copy(which_f[:, :, :], which[:, :, :]))
                step(v.tensor_tensor(s2[:, :], best[:, :, 0], best[:, :, 1], ALU.add))
                step(v.tensor_scalar(s2[:, :], s2[:, :], 1e-20, None, ALU.add))
                step(v.reciprocal(r2[:, :], s2[:, :]))
                v.scalar_tensor_tensor(w2[:, :, :], best[:, :, 0:2], ROUTE_SCALE, wide(r2[:, :], 2), ALU.mult, ALU.mult)
                for i in range(TOPK):
                    last = v.tensor_tensor(hit[:, i, :, :], iota[:, :, :], wide(which_f[:, :, i]), ALU.is_equal)
                step(last)
                step(v.tensor_copy(C["weight"][:, ds(u * TPS, TPS), :], w2[:, :, :]))
                v.tensor_tensor(chosen[:, :, :], hit[:, 0, :, :], hit[:, 1, :, :], ALU.add).then_inc(chosen_done, 1)
                assert n[0] == ROUTE

            def body(b, first_batch, last_batch):
                for s in range(SPB):
                    u = b * SPB + s
                    if not (last_batch and s == SPB - 1):
                        front(u + 1, (s + 1) % 2, b + 1 if s == SPB - 1 else b)
                    normalise(u, s % 2, b)
                    if not (first_batch and s == 0):
                        locate(u - 1, (s + 1) % 2)
                    route_tokens(u, s % 2)

            v.wait_ge(consts, 48)
            front(0, 0, 0)
            body(0, True, False)
            with v.Fori(1, B - 1) as b:
                body(b, False, False)
            body(B - 1, False, True)
            locate(NST - 1, (NST - 1) % 2)

        @block.tensor
        def _(pe):
            pe.sem_inc(o_read, 2)
            pe.sem_inc(ot_read, 1)

            def front(u, slot, turn):
                pe.wait_ge(in_done[slot], turn * (16 * IN_DMAS))
                pe.wait_ge(ot_done, u * DC + DC)
                for c in range(DC):
                    for t in range(TPS):
                        last = pe.transpose(ps_o[:, c, t * P:(t + 1) * P], o_in[:, slot, t, c * P:(c + 1) * P], ident[:, :])
                last.then_inc(o_read, 1)
                pe.wait_ge(ot_done, u * DC + (DC + 2))
                pe.wait_ge(y_done, u + 1)
                for t in range(TPS):
                    for c in range(DC):
                        last = pe.matmul(ps_p[:, t, :], o_t[:, slot, c, t * P:(t + 1) * P], wp[:, c, :],
                                         start=(c == 0), stop=(c == DC - 1))
                last.then_inc(ot_read, 1)

            def back(u, slot):
                pe.wait_ge(rows_done, u + 1)
                pe.wait_ge(h2_done, u * DC + DC)
                for c in range(DC):
                    for t in range(TPS):
                        last = pe.transpose(ps_h[:, c, t * P:(t + 1) * P], rows[:, slot, t, c * P:(c + 1) * P], ident[:, :])
                    last.then_inc(turned, 1)
                pe.wait_ge(h2_done, u * DC + (DC + 2))
                for t in range(TPS):
                    for c in range(DC):
                        last = pe.matmul(ps_l[:, 0, t, :], h2[:, slot, c, t * P:(t + 1) * P], gate_t[:, c, :],
                                         start=(c == 0), stop=(c == DC - 1))
                last.then_inc(logits, 1)

            def ranks(u):
                pe.wait_ge(chosen_done, u + 1)
                pe.wait_ge(at_done, u + 1)
                for t in range(TPS + 1):
                    terms = [(ones, before) for before in range(t)] + ([(strict, t)] if t < TPS else [])
                    for i, (lhs, tile) in enumerate(terms):
                        last = pe.matmul(ps_rank[:, t, :], lhs[:, :], chosen[:, tile, :], start=(i == 0),
                                         stop=(i == len(terms) - 1))
                last.then_inc(ranked, 1)

            def body(b, first_batch, last_batch):
                for s in range(SPB):
                    u = b * SPB + s
                    if not (last_batch and s == SPB - 1):
                        front(u + 1, (s + 1) % 2, b * 2 + ((s + 1) // 2 + 1))
                    if not (first_batch and s == 0):
                        ranks(u - 1)
                    back(u, s % 2)

            pe.wait_ge(consts, 48)
            pe.wait_ge(init, 4)
            front(0, 0, 1)
            body(0, True, False)
            with pe.Fori(1, B - 1) as b:
                body(b, False, False)
            body(B - 1, False, True)
            ranks(NST - 1)


def expert_stage(nc, C, rows_dram, made_dram, steps_dram, plan_dram, w_gate, w_up, w_down):
    CHUNKS = [(f, min(P, F - f)) for f in range(0, F, P)]
    NC = len(CHUNKS)
    full = F // P
    WDMAS = 2 * DC + 2
    with ExitStack() as ctx:
        def sb(name, shape, dt=F32):
            return ctx.enter_context(nc.sbuf_tensor(name, shape, dt))

        def ps(name, shape, dt=F32):
            return ctx.enter_context(nc.psum_tensor(name, shape, dt))

        def sem(name):
            return ctx.enter_context(nc.semaphore(name))

        ident, count = C["ident"], C["count"]
        steps = sb("steps", [P, E, MOST])
        tables = sb("tables", [P, 3, NB, E])
        over = sb("over", [P, E, MOST])
        blocks = sb("blocks", [P, E])
        ends = sb("ends", [P, 4, E])
        start = sb("start", [P, E])
        start_row = sb("start_row", [P, E])
        past = sb("past", [P, 2, NB, E])
        inside = sb("inside", [P, NB, E])
        row_e = sb("row_e", [P, 2, NB, E])
        plan_f = sb("plan_f", [P, 2, NB])
        plan = sb("plan", [P, 2, NB], U32)
        pad_f = sb("pad_f", [P, E])
        pad_at = sb("pad_at", [P, E], U32)
        mine = sb("mine", [P, NST * TOPK * TPS, E])
        made_f = sb("made_f", [P, NST * TOPK * TPS])
        zeros = sb("zeros", [P, TPS, D])
        x_r = sb("x_r", [P, 2, TPS, D])
        x_t = sb("x_t", [P, 2, DC, ST])
        wg = sb("wg", [P, 2, DC, F])
        wu = sb("wu", [P, 2, DC, F])
        wd = sb("wd", [P, 2, NC, D])
        act_g = sb("act_g", [P, 2, ST])
        hid = sb("hid", [P, NC, ST])
        made = sb("made", [P, 2, TPS, D])
        ps_g = ps("ps_g4", [P, 2, ST])
        ps_u = ps("ps_u4", [P, 2, ST])
        ps_d = ps("ps_d4", [P, TPS, D])
        ps_x = ps("ps_x4", [P, DC, ST])

        tables_in = sem("p4_tables")
        zeroed = sem("p4_zeroed")
        step_done = sem("p4_step")
        planned = sem("p4_planned")
        padded = sem("p4_padded")
        x_in = [sem(f"p4_x_in{i}") for i in range(2)]
        w_in = [sem(f"p4_w_in{i}") for i in range(2)]
        x_turned = sem("p4_x_turned")
        xt_done = sem("p4_xt")
        gu_done = sem("p4_gu")
        silu_done = sem("p4_silu")
        hid_done = sem("p4_hid")
        down_done = sem("p4_down")
        made_done = sem("p4_made")
        made_stored = [sem(f"p4_stored{i}") for i in range(2)]

        block = ctx.enter_context(nc.Block())

        @block.sync
        def _(sp):
            sp.dma_start(steps[:, :, :], steps_dram).then_inc(tables_in, 16)
            sp.dma_start(tables[:, :, :, :].rearrange("p k n e -> p (k n e)"),
                         plan_dram.rearrange("p k n e -> p (k n e)")).then_inc(tables_in, 16)
            sp.wait_ge(planned, 1)
            sp.wait_ge(zeroed, 1)
            for e in range(E):
                row = sp.value_load(pad_at[0:1, e:e + 1], min_val=0, max_val=E * REGION - ST)
                sp.dma_start(rows_dram[ds(row, ST), :].rearrange("(t p) d -> p t d", p=P), zeros[:, :, :]) \
                    .then_inc(padded, 16)
            for slot in range(2):
                sp.sem_inc(made_stored[slot], 16)

            def load(j, slot, reused):
                row = sp.value_load(plan[0:1, 0, ds(j, 1)], min_val=0, max_val=E * REGION - ST)
                e = sp.value_load(plan[0:1, 1, ds(j, 1)], min_val=0, max_val=E - 1)
                if reused:
                    sp.wait_ge(down_done, j * NC)
                for c in range(DC):
                    for w, src in ((wg, w_gate), (wu, w_up)):
                        sp.dma_start(w[:, slot, c, :], src[ds(e, 1), c * P:(c + 1) * P, :]
                                     .rearrange("o p f -> (o p) f")).then_inc(w_in[slot], 16)
                sp.dma_start(wd[:, slot, 0:full, :], w_down[ds(e, 1), 0:full * P, :]
                             .rearrange("o (j p) n -> p (o j) n", p=P)).then_inc(w_in[slot], 16)
                sp.dma_start(wd[0:F - full * P, slot, full, :], w_down[ds(e, 1), full * P:F, :]
                             .rearrange("o p n -> (o p) n")).then_inc(w_in[slot], 16)
                if reused:
                    sp.wait_ge(x_turned, j * DC)
                sp.dma_start(x_r[:, slot, :, :], rows_dram[ds(row, ST), :].rearrange("(t p) d -> p t d", p=P)) \
                    .then_inc(x_in[slot], 16)

            def body(it, slots, last):
                for slot in slots:
                    j = it * 2 + slot
                    if not last:
                        load(j + 1, 1 - slot, True)
                    sp.wait_ge(made_done, j + 2)
                    sp.dma_start(made_dram[ds(j * ST, ST), :].rearrange("(t p) d -> p t d", p=P), made[:, slot, :, :]) \
                        .then_inc(made_stored[slot], 16)

            sp.wait_ge(padded, 16 * E)
            load(0, 0, False)
            with sp.Fori(0, NB // 2) as it:
                body(it, (0, 1), False)
            body(NB // 2, (0,), True)
            for slot in range(2):
                sp.wait_ge(made_stored[slot], 16 * ((NB + 1 - slot) // 2 + 1))

        @block.gpsimd
        def _(pool):
            pool.memset(zeros[:, :, :].rearrange("p t d -> p (t d)"), 0.0).then_inc(zeroed, 1)

        @block.scalar
        def _(act):
            act.sem_inc(silu_done, 2)
            act.sem_inc(xt_done, DC)

            def copy_x(j, slot):
                for c in range(DC):
                    act.wait_ge(x_turned, j * DC + (c + 1 + DC))
                    act.activation(x_t[:, slot, c, :], ps_x[:, c, :], ACT.Copy).then_inc(xt_done, 1)

            def body(it, slots, last):
                for slot in slots:
                    j = it * 2 + slot
                    for i, (f, m) in enumerate(CHUNKS):
                        half = (slot + i) % 2
                        act.wait_ge(gu_done, j * NC + (i + 1))
                        act.wait_ge(hid_done, j * NC + (i + 1))
                        act.activation(act_g[0:m, half, :], ps_g[0:m, half, :], ACT.Silu).then_inc(silu_done, 1)
                        if i == 1 and not last:
                            copy_x(j + 1, 1 - slot)

            copy_x(0, 0)
            with act.Fori(0, NB // 2) as it:
                body(it, (0, 1), False)
            body(NB // 2, (0,), True)

        @block.vector
        def _(v):
            v.sem_inc(hid_done, 2)
            v.sem_inc(made_done, 1)
            n = [0]

            def step(ins):
                n[0] += 1
                ins.then_inc(step_done, 1)
                v.wait_ge(step_done, n[0])

            def each(a):
                return a.unsqueeze(1).to_broadcast([P, NB, E])

            v.wait_ge(tables_in, 32)
            step(v.tensor_tensor(over[:, :, :], count[:, :].unsqueeze(2).to_broadcast([P, E, MOST]), steps[:, :, :],
                                 ALU.is_gt))
            step(v.tensor_reduce(blocks[:, :], over[:, :, :], AX.X, ALU.add))
            step(v.tensor_copy(ends[:, 0, :], blocks[:, :]))
            for k in range(3):
                by = 1 << k
                v.tensor_copy(ends[:, k + 1, 0:by], ends[:, k, 0:by])
                step(v.tensor_tensor(ends[:, k + 1, by:E], ends[:, k, by:E], ends[:, k, 0:E - by], ALU.add))
            end = ends[:, 3, :]
            step(v.tensor_tensor(start[:, :], end, blocks[:, :], ALU.subtract))
            step(v.tensor_scalar(start_row[:, :], start[:, :], float(ST), None, ALU.mult))
            v.tensor_tensor(past[:, 0, :, :], tables[:, 0, :, :], each(start[:, :]), ALU.is_ge)
            step(v.tensor_tensor(past[:, 1, :, :], tables[:, 0, :, :], each(end), ALU.is_ge))
            v.tensor_tensor(row_e[:, 0, :, :], tables[:, 1, :, :], each(start_row[:, :]), ALU.subtract)
            step(v.tensor_tensor(inside[:, :, :], past[:, 0, :, :], past[:, 1, :, :], ALU.subtract))
            v.tensor_tensor(row_e[:, 0, :, :], row_e[:, 0, :, :], inside[:, :, :], ALU.mult)
            step(v.tensor_tensor(row_e[:, 1, :, :], tables[:, 2, :, :], inside[:, :, :], ALU.mult))
            step(v.tensor_reduce(plan_f[:, :, :], row_e[:, :, :, :], AX.X, ALU.add))
            v.tensor_tensor(pad_f[:, :], tables[:, 1, 0, :], count[:, :], ALU.add)
            step(v.tensor_copy(plan[:, :, :], plan_f[:, :, :]))
            v.tensor_copy(pad_at[:, :], pad_f[:, :]).then_inc(planned, 1)
            every = [P, NST * TOPK * TPS, E]
            flat = "p a t -> p (a t)"
            step(v.tensor_tensor(mine[:, :, :], C["which"][:, :, :].rearrange(flat).unsqueeze(2).to_broadcast(every),
                                 tables[:, 2, 0, :].unsqueeze(1).to_broadcast(every), ALU.is_equal))
            step(v.tensor_tensor(mine[:, :, :], mine[:, :, :], start_row[:, :].unsqueeze(1).to_broadcast(every),
                                 ALU.mult))
            step(v.tensor_reduce(made_f[:, :], mine[:, :, :], AX.X, ALU.add))
            step(v.tensor_tensor(made_f[:, :], made_f[:, :], C["rank"][:, :, :].rearrange(flat), ALU.add))
            v.tensor_copy(C["made_at"][:, :, :].rearrange(flat), made_f[:, :])

            def body(it, slots):
                for slot in slots:
                    j = it * 2 + slot
                    for i, (f, m) in enumerate(CHUNKS):
                        half = (slot + i) % 2
                        v.wait_ge(silu_done, j * NC + (i + 1 + 2))
                        v.wait_ge(down_done, j * NC + (i + 1))
                        v.tensor_tensor(hid[0:m, i, :], act_g[0:m, half, :], ps_u[0:m, half, :], ALU.mult) \
                            .then_inc(hid_done, 1)
                    v.wait_ge(down_done, j * NC + 2 * NC)
                    v.wait_ge(made_stored[slot], it * 16 + 16)
                    v.tensor_copy(made[:, slot, :, :], ps_d[:, :, :]).then_inc(made_done, 1)

            with v.Fori(0, NB // 2) as it:
                body(it, (0, 1))
            body(NB // 2, (0,))

        @block.tensor
        def _(pe):
            pe.sem_inc(x_turned, DC)
            pe.sem_inc(down_done, NC)

            def turn(j, slot, turn_no):
                pe.wait_ge(x_in[slot], turn_no * 16)
                pe.wait_ge(xt_done, j * DC + DC)
                for c in range(DC):
                    for t in range(TPS):
                        last = pe.transpose(ps_x[:, c, t * P:(t + 1) * P], x_r[:, slot, t, c * P:(c + 1) * P], ident[:, :])
                    last.then_inc(x_turned, 1)

            def up(j, i, slot, turn_no):
                f, m = CHUNKS[i]
                half = (slot + i) % 2
                if i == 0:
                    pe.wait_ge(w_in[slot], turn_no * (16 * WDMAS))
                    pe.wait_ge(xt_done, j * DC + 2 * DC)
                pe.wait_ge(silu_done, j * NC + (i + 1))
                pe.wait_ge(hid_done, j * NC + (i + 1))
                for w, dst in ((wg, ps_g), (wu, ps_u)):
                    for c in range(DC):
                        last = pe.matmul(dst[0:m, half, :], w[:, slot, c, f:f + m], x_t[:, slot, c, :],
                                         start=(c == 0), stop=(c == DC - 1))
                last.then_inc(gu_done, 1)

            def down(j, i, slot):
                f, m = CHUNKS[i]
                if i == 0:
                    pe.wait_ge(made_done, j + 1)
                pe.wait_ge(hid_done, j * NC + (i + 1 + 2))
                for t in range(TPS):
                    last = pe.matmul(ps_d[:, t, :], hid[0:m, i, t * P:(t + 1) * P], wd[0:m, slot, i, :],
                                     start=(i == 0 and t % 2 == 0), stop=(i == NC - 1), skip_group_check=True)
                last.then_inc(down_done, 1)

            def body(it, slots, last):
                for slot in slots:
                    j = it * 2 + slot
                    for i in range(NC):
                        up(j, i, slot, it + 1)
                        if i > 0:
                            down(j, i - 1, slot)
                        if i == 1 and not last:
                            turn(j + 1, 1 - slot, it + (1 + slot))
                    down(j, NC - 1, slot)

            turn(0, 0, 1)
            with pe.Fori(0, NB // 2) as it:
                body(it, (0, 1), False)
            body(NB // 2, (0,), True)


def shared_stage(nc, C, h2_dram, x1_dram, made_dram, sw_gate, sw_up, sw_down, out_flat):
    CHUNKS = [(f, min(P, FS - f)) for f in range(0, FS, P)]
    NC = len(CHUNKS)
    full = FS // P
    GS = 3
    PICKS = TOPK * TPS
    with ExitStack() as ctx:
        def sb(name, shape, dt=F32):
            return ctx.enter_context(nc.sbuf_tensor(name, shape, dt))

        def ps(name, shape, dt=F32):
            return ctx.enter_context(nc.psum_tensor(name, shape, dt))

        def sem(name):
            return ctx.enter_context(nc.semaphore(name))

        gb, weight, made_at = C["gb"], C["weight"], C["made_at"]
        wg = sb("sg_w", [P, DC, FS])
        wu = sb("su_w", [P, DC, FS])
        wd = sb("sd_w", [P, NC, D])
        h2 = sb("h2_5", [P, 2, DC, ST])
        x1 = sb("x1_5", [P, 2, TPS, D])
        at_now = sb("at_now", [P, 2, PICKS], U32)
        got = sb("got", [P, 2, PICKS, D])
        act_g = sb("act_g5", [P, 2, ST])
        hid = sb("hid5", [P, GS, ST])
        first = sb("first", [P, TPS, D])
        mix = sb("mix", [P, TPS, D])
        total = sb("total", [P, TPS, D])
        gated = sb("gated", [P, TPS, D])
        y_out = sb("y_out", [P, TPS, D])
        weight_now = sb("weight_now", [P, 2 * TPS, TOPK])
        gb_now = sb("gb_now", [P, D])
        ps_g = ps("ps_g5", [P, 2, ST])
        ps_u = ps("ps_u5", [P, 2, ST])
        ps_d = ps("ps_d5", [P, 2, TPS, D])

        held = sem("p5_held")
        w_in = sem("p5_weights")
        in_done = [sem(f"p5_in{i}") for i in range(2)]
        at_copied = sem("p5_at")
        gathered = [sem(f"p5_gathered{i}") for i in range(2)]
        got_used = sem("p5_got_used")
        h2_read = sem("p5_h2_read")
        out_done = sem("p5_out")
        gu_done = sem("p5_gu")
        silu_done = sem("p5_silu")
        hid_done = sem("p5_hid")
        down_done = sem("p5_down")
        now = sem("p5_now")
        first_done = sem("p5_first")
        mixed = sem("p5_mixed")
        summed = sem("p5_summed")
        gated_done = sem("p5_gated")
        stored = sem("p5_stored")
        W_DMAS = 4

        block = ctx.enter_context(nc.Block())

        @block.sync
        def _(sp):
            sp.dma_start(wg[:, :, :], sw_gate.rearrange("(c p) f -> p c f", p=P)).then_inc(w_in, 16)
            sp.dma_start(wu[:, :, :], sw_up.rearrange("(c p) f -> p c f", p=P)).then_inc(w_in, 16)
            sp.dma_start(wd[:, 0:full, :], sw_down[0:full * P, :].rearrange("(j p) n -> p j n", p=P)).then_inc(w_in, 16)
            sp.dma_start(wd[0:FS - full * P, full, :], sw_down[full * P:FS, :]).then_inc(w_in, 16)

            def load(u, slot):
                sp.wait_ge(h2_read, u + 1)
                sp.wait_ge(out_done, u + 1)
                sp.dma_start(h2[:, slot, :, :].rearrange("p c t -> p (c t)"), h2_dram[ds(u * P, P), :]) \
                    .then_inc(in_done[slot], 16)
                sp.dma_start(x1[:, slot, :, :], x1_dram[ds(u * ST, ST), :].rearrange("(t p) d -> p t d", p=P)) \
                    .then_inc(in_done[slot], 16)

            def body(it, last):
                for slot in range(2):
                    u = it * 2 + slot
                    if not (last and slot):
                        load(u + 1, 1 - slot)
                    sp.wait_ge(out_done, u + 1 + 2)
                    sp.dma_start(out_flat[ds(u * ST, ST), :].rearrange("(t p) d -> p t d", p=P), y_out[:, :, :]) \
                        .then_inc(stored, 16)

            sp.sem_inc(stored, 16)
            load(0, 0)
            with sp.Fori(0, NST // 2 - 1) as it:
                body(it, False)
            body(NST // 2 - 1, True)
            sp.wait_ge(stored, 16 * (NST + 1))

        @block.gpsimd
        def _(pool):
            pool.sem_inc(out_done, 2)

            def gather(u, slot):
                pool.wait_ge(got_used, u + 1)
                stand_alone(pool, held)
                pool.tensor_copy(at_now[:, slot, :].rearrange("p (i t) -> p i t", i=TOPK),
                                 made_at[:, ds(u * TOPK, TOPK), :]).then_inc(at_copied, 1)
                pool.wait_ge(at_copied, u + 1)
                stand_alone(pool, held)
                for j in range(PICKS):
                    pool.indirect_dma_start(got[:, slot, j, :], None, made_dram,
                                            bass.IndirectOffsetOnAxis(at_now[:, slot, j:j + 1], 0)) \
                        .then_inc(gathered[slot], 16)

            def body(it, last):
                for slot in range(2):
                    u = it * 2 + slot
                    if not (last and slot):
                        gather(u + 1, 1 - slot)
                    pool.wait_ge(in_done[slot], it * 32 + 32)
                    pool.wait_ge(gated_done, u + 1 + 1)
                    pool.wait_ge(stored, u * 16 + 16)
                    pool.tensor_tensor(y_out[:, :, :], gated[:, :, :], x1[:, slot, :, :], ALU.add).then_inc(out_done, 1)

            gather(0, 0)
            with pool.Fori(0, NST // 2 - 1) as it:
                body(it, False)
            body(NST // 2 - 1, True)

        @block.scalar
        def _(act):
            act.sem_inc(silu_done, 2)
            with act.Fori(0, NST // 2) as it:
                for slot in range(2):
                    u = it * 2 + slot
                    for i, (f, m) in enumerate(CHUNKS):
                        act.wait_ge(gu_done, u * NC + (i + 1))
                        act.wait_ge(hid_done, u * NC + (i + 1))
                        act.activation(act_g[0:m, i % 2, :], ps_g[0:m, i % 2, :], ACT.Silu).then_inc(silu_done, 1)

        @block.vector
        def _(v):
            v.sem_inc(hid_done, 2)
            v.sem_inc(got_used, 2)
            v.sem_inc(gated_done, 1)
            v.sem_inc(summed, 2)

            def mix_experts(u, slot, it):
                v.wait_ge(gathered[slot], it * (16 * PICKS) + 16 * PICKS)
                for t in range(TPS):
                    last = v.tensor_scalar(first[:, t, :], got[:, slot, t, :], weight_now[:, slot * TPS + t, 0:1], None,
                                           ALU.mult)
                last.then_inc(first_done, 1)
                v.wait_ge(first_done, u + 1)
                v.wait_ge(summed, u + 2)
                for t in range(TPS):
                    last = v.scalar_tensor_tensor(mix[:, t, :], got[:, slot, TPS + t, :],
                                                  weight_now[:, slot * TPS + t, 1:2], first[:, t, :], ALU.mult, ALU.add)
                last.then_inc(got_used, 1)

            with v.Fori(0, NST // 2) as it:
                v.wait_ge(gated_done, it * 2 + 1)
                v.wait_ge(got_used, it * 2 + 2)
                v.tensor_copy(weight_now[:, :, :], weight[:, ds(it * (2 * TPS), 2 * TPS), :])
                v.tensor_copy(gb_now[:, :], gb[:, ds(it, 1), :].rearrange("p o d -> p (o d)")).then_inc(now, 1)
                v.wait_ge(now, it + 1)
                for slot in range(2):
                    u = it * 2 + slot
                    for i, (f, m) in enumerate(CHUNKS):
                        v.wait_ge(silu_done, u * NC + (i + 1 + 2))
                        v.wait_ge(down_done, u * NC + (i + 1))
                        v.tensor_tensor(hid[0:m, i % GS, :], act_g[0:m, i % 2, :], ps_u[0:m, i % 2, :], ALU.mult) \
                            .then_inc(hid_done, 1)
                        if i == NC - 3:
                            mix_experts(u, slot, it)
                    v.wait_ge(down_done, u * NC + (NC + GS))
                    v.wait_ge(got_used, u + 3)
                    v.wait_ge(gated_done, u + 1)
                    v.tensor_tensor(total[:, :, :], ps_d[:, slot, :, :], mix[:, :, :], ALU.add).then_inc(summed, 1)
                    v.wait_ge(summed, u + 3)
                    v.wait_ge(out_done, u + 2)
                    v.tensor_tensor(gated[:, :, :], total[:, :, :], gb_now[:, :].unsqueeze(1).to_broadcast([P, TPS, D]),
                                    ALU.mult).then_inc(gated_done, 1)

        @block.tensor
        def _(pe):
            pe.sem_inc(h2_read, 2)
            pe.sem_inc(down_done, GS)

            def up(u, i, slot):
                f, m = CHUNKS[i]
                pe.wait_ge(silu_done, u * NC + (i + 1))
                pe.wait_ge(hid_done, u * NC + (i + 1))
                for w, dst in ((wg, ps_g), (wu, ps_u)):
                    for c in range(DC):
                        last = pe.matmul(dst[0:m, i % 2, :], w[:, c, f:f + m], h2[:, slot, c, :],
                                         start=(c == 0), stop=(c == DC - 1))
                last.then_inc(gu_done, 1)

            def down(u, i, slot):
                f, m = CHUNKS[i]
                if i == 0:
                    pe.wait_ge(summed, u + 1)
                pe.wait_ge(hid_done, u * NC + (i + 1 + 2))
                for t in range(TPS):
                    last = pe.matmul(ps_d[:, slot, t, :], hid[0:m, i % GS, t * P:(t + 1) * P], wd[0:m, i, :],
                                     start=(i == 0 and t % 2 == 0), stop=(i == NC - 1), skip_group_check=True)
                last.then_inc(down_done, 1)
                if i == NC - 1:
                    pe.wait_ge(down_done, u * NC + (NC + GS))
                    pe.sem_inc(h2_read, 1)

            pe.wait_ge(w_in, 16 * W_DMAS)
            with pe.Fori(0, NST // 2) as it:
                for slot in range(2):
                    u = it * 2 + slot
                    pe.wait_ge(in_done[slot], it * 32 + 32)
                    for i in range(NC):
                        up(u, i, slot)
                        if i > 0:
                            down(u, i - 1, slot)
                    down(u, NC - 1, slot)


_INS = ['L0_attn_x', 'L0_attn_w_qkv', 'L0_attn_w_proj', 'L0_attn_b_proj', 'L0_ffn_gate_w', 'L0_ffn_w_gate',
        'L0_ffn_w_up', 'L0_ffn_w_down', 'L0_ffn_sw_gate', 'L0_ffn_sw_up', 'L0_ffn_sw_down', 'L0_c', 'L0_wmod']


def kernel(**inputs):
    import numpy as _np
    import concourse.bacc as _bacc
    from concourse import mybir as _mybir
    from concourse.bass_utils import run_bass_kernel_spmd as _run

    nc = _bacc.Bacc("TRN2", target_bir_lowering=False, num_devices=1)
    arrays, args = {}, []
    for name in _INS:
        a = _np.ascontiguousarray(inputs[name])
        arrays[f"in_{name}_dram"] = a
        args.append(nc.dram_tensor(f"in_{name}_dram", a.shape, _mybir.dt.from_np(a.dtype), kind="ExternalInput").ap())
    args.append(nc.dram_tensor("out_dram", (B, S, D), _mybir.dt.float32, kind="ExternalOutput").ap())
    block_kernel(nc, *args)
    r = _run(nc, [arrays], core_ids=[0])
    return r.results[0]["out_dram"]
```

```python
from contextlib import ExitStack

import numpy as np

import concourse.bass as bass
from concourse import mybir

F32 = mybir.dt.float32
BF16 = mybir.dt.bfloat16
F32R = mybir.dt.float32r
U32 = mybir.dt.uint32
ALU = mybir.AluOpType
ACT = mybir.ActivationFunctionType
AX = mybir.AxisListType
ds = bass.ds

P = 128
B, S, D = 4, 2048, 256
DC = D // P
H, HD = 16, 16
HALF = HD // 2
ST = 512
TPS = ST // P
SPB = S // ST
NT = S // P
HG = 4
GROUPS = B * H // HG
GPB = H // HG
VW = 32
ROWS = 96
QPART = (0, 0, 0, 1, 1, 2)
KPART = (0, 1, 2, 0, 1, 0)
PARTS = ("high", "low")
PRODUCTS = ((0, 0), (0, 1), (1, 0))
E, F, FS = 8, 352, 704
EPS = 1e-5
SCALE = HD ** -0.5
ROUTE_SCALE = 2.5
NEG = -1e30
LOWEST = -3e38
GATE_MIN = 0.25
SA, CA, GA, SB_, CB, GB = range(6)
MOD_CHUNKS = [v * DC + c for v in (SA, CA) for c in range(DC)]
M_SA, M_CA = 0, DC
TOPK = 2
NST = B * SPB
REGION = B * S + ST
NB = (TOPK * B * S + E * (ST - 1)) // ST
MOST = B * S // ST


def rope_tables():
    inv = (np.float32(1.0) / np.float32(10000.0) ** (np.arange(0, HD, 2, dtype=np.float32) / np.float32(HD))).astype(np.float32)
    t = np.arange(S, dtype=np.float32)[:, None] * inv[None, :]
    cos, sin = np.cos(t).astype(np.float32), np.sin(t).astype(np.float32)

    def tiled(a):
        return np.ascontiguousarray(a.reshape(NT, P, HD).transpose(1, 0, 2))

    return tiled(np.concatenate([cos, cos], 1)), tiled(np.concatenate([-sin, sin], 1))


def block_kernel(nc, x, w_qkv, w_proj, b_proj, gate_w, w_gate, w_up, w_down, sw_gate, sw_up, sw_down,
                 cond, wmod, out):
    x_flat = x.rearrange("b s d -> (b s) d")
    out_flat = out.rearrange("b s d -> (b s) d")
    cos_np, sin_np = rope_tables()
    cos_dram = nc.inline_tensor(cos_np, "rope_cos").ap()
    sin_dram = nc.inline_tensor(sin_np, "rope_sin").ap()
    ident_dram = nc.inline_tensor(np.eye(P, dtype=np.float32), "identity").ap()
    number = np.arange(E, dtype=np.float32)
    block_no = np.arange(NB, dtype=np.float32)[:, None]
    iota_dram = nc.inline_tensor(np.tile(number, (P, TPS, 1)), "expert_number").ap()
    steps_dram = nc.inline_tensor(np.tile(np.arange(MOST, dtype=np.float32) * ST, (P, E, 1)), "plan_steps").ap()
    plan_dram = nc.inline_tensor(np.tile(np.stack([block_no + 0 * number, number * REGION + block_no * ST,
                                                   number + 0 * block_no]), (P, 1, 1, 1)), "plan_tables").ap()

    qk_dram = nc.dram_tensor("qk_parts", (GROUPS, 2, 3, HG * HD, S), BF16, kind="Internal").ap()
    v_dram = nc.dram_tensor("v_ones", (GROUPS * S, HG * VW), F32, kind="Internal").ap()
    o_dram = nc.dram_tensor("attn_out", (GROUPS * S, HG * HD), F32, kind="Internal").ap()
    x1_dram = nc.dram_tensor("x_mid", (B * S, D), F32, kind="Internal").ap()
    h2_dram = nc.dram_tensor("h2_t", (B * SPB * P, DC * ST), F32, kind="Internal").ap()
    rows_dram = nc.dram_tensor("expert_rows", (E * REGION, D), F32, kind="Internal").ap()
    made_dram = nc.dram_tensor("expert_made", (NB * ST, D), F32, kind="Internal").ap()

    with ExitStack() as whole:
        def keep(name, shape, dt):
            return whole.enter_context(nc.sbuf_tensor(name, shape, dt))

        C = dict(
            ident=keep("ident", [P, P], F32), ident_b=keep("ident_b", [P, P], BF16),
            mod_t=keep("mod_t", [P, len(MOD_CHUNKS), B], F32),
            ga=keep("ga", [P, B, D], F32), gb=keep("gb", [P, 2 * B, D], F32),
            gate_t=keep("gate_t", [P, DC, E], F32),
            cb=keep("cb", [P, B, D], F32), sb=keep("sb", [P, B, D], F32),
            which=keep("which_all", [P, NST * TOPK, TPS], F32),
            rank=keep("rank_all", [P, NST * TOPK, TPS], F32),
            weight=keep("weight_all", [P, NST * TPS, TOPK], F32),
            count=keep("count", [P, E], F32),
            plan=keep("plan", [P, 2, NB], U32),
            made_at=keep("made_at", [P, NST * TOPK, TPS], U32),
        )
        setup_stage(nc, C, ident_dram, cond, wmod, gate_w)
        qkv_stage(nc, C, x_flat, w_qkv, cos_dram, sin_dram, qk_dram, v_dram)
        attention_stage(nc, C, qk_dram, v_dram, o_dram)
        middle_stage(nc, C, o_dram, x_flat, w_proj, b_proj, iota_dram, x1_dram, h2_dram, rows_dram,
                     steps_dram, plan_dram)
        expert_stage(nc, C, rows_dram, made_dram, w_gate, w_up, w_down)
        shared_stage(nc, C, h2_dram, x1_dram, made_dram, sw_gate, sw_up, sw_down, out_flat)


def stand_alone(eng, held):
    eng.sem_inc(held, 1)


def setup_stage(nc, C, ident_dram, cond, wmod, gate_w):
    with ExitStack() as ctx:
        def sb(name, shape, dt=F32):
            return ctx.enter_context(nc.sbuf_tensor(name, shape, dt))

        def sem(name):
            return ctx.enter_context(nc.semaphore(name))

        c_row = sb("c_row", [B, D])
        c_exp = sb("c_exp", [B, D])
        c_den = sb("c_den", [B, D])
        c_inv = sb("c_inv", [B, D])
        c_silu = sb("c_silu", [B, D])
        c_t = sb("c_t", [P, DC, B])
        c_rep = sb("c_rep", [P, DC * B, P])
        wmod_sb = sb("wmod_sb", [P, DC, 6 * D])
        gw_row = sb("gw_row", [E, D])
        sign = sb("sign", [P, B, 2, D])
        mag = sb("mag", [P, B, 2, D])
        minus = sb("minus", [P, B, 2, D])
        ps_t = ctx.enter_context(nc.psum_tensor("su_ps_t", [P, DC, B], F32))
        ps_gw = ctx.enter_context(nc.psum_tensor("su_ps_gw", [P, DC, E], F32))
        ps_m = ctx.enter_context(nc.psum_tensor("su_ps_m", [P, len(MOD_CHUNKS), B], F32))
        ps_g = ctx.enter_context(nc.psum_tensor("su_ps_g", [P, B, 2, D], F32))
        loaded = sem("su_loaded")
        exp_done = sem("su_exp")
        dve = sem("su_dve")
        transposed = sem("su_transposed")
        c_t_done = sem("su_c_t")
        products = sem("su_products")
        ident, ident_b, mod_t = C["ident"], C["ident_b"], C["mod_t"]
        loads = 4

        block = ctx.enter_context(nc.Block())

        @block.sync
        def _(sp):
            sp.dma_start(c_row[:, :], cond).then_inc(loaded, 16)
            sp.dma_start(ident[:, :], ident_dram).then_inc(loaded, 16)
            sp.dma_start(gw_row[:, :], gate_w).then_inc(loaded, 16)
            sp.dma_start(wmod_sb[:, :, :], wmod.rearrange("(c p) n -> p c n", p=P)).then_inc(loaded, 16)

        @block.scalar
        def _(act):
            act.wait_ge(loaded, 16 * loads)
            act.activation(c_exp[:, :], c_row[:, :], ACT.Exp, scale=-1.0).then_inc(exp_done, 1)

        @block.vector
        def _(v):
            v.wait_ge(exp_done, 1)
            v.tensor_scalar(c_den[:, :], c_exp[:, :], 1.0, None, ALU.add).then_inc(dve, 1)
            v.wait_ge(dve, 1)
            v.reciprocal(c_inv[:, :], c_den[:, :]).then_inc(dve, 1)
            v.wait_ge(dve, 2)
            v.tensor_tensor(c_silu[:, :], c_row[:, :], c_inv[:, :], ALU.mult).then_inc(dve, 1)
            v.tensor_copy(ident_b[:, :], ident[:, :])
            v.wait_ge(transposed, 1)
            v.tensor_copy(c_t[:, :, :], ps_t[:, :, :]).then_inc(dve, 1)
            v.tensor_copy(C["gate_t"][:, :, :], ps_gw[:, :, :])
            v.wait_ge(dve, 4)
            v.tensor_copy(c_rep[:, :, :], c_t[:, :, :].rearrange("p c b -> p (c b)").unsqueeze(2)
                          .to_broadcast([P, DC * B, P])).then_inc(c_t_done, 1)
            v.wait_ge(products, 1)
            v.tensor_copy(mod_t[:, :, :], ps_m[:, :, :]).then_inc(dve, 1)
            v.wait_ge(dve, 5)
            m = mod_t[:, M_CA:M_CA + DC, :]
            v.tensor_scalar(m, m, 1.0, None, ALU.add)
            v.wait_ge(products, 2)
            v.tensor_scalar(sign[:, :, :, :], ps_g[:, :, :, :], 0.0, 2.0, ALU.is_ge, ALU.mult).then_inc(dve, 1)
            v.tensor_scalar(minus[:, :, :, :], ps_g[:, :, :, :], -1.0, None, ALU.mult).then_inc(dve, 1)
            v.wait_ge(dve, 7)
            v.scalar_tensor_tensor(mag[:, :, :, :].rearrange("p b g d -> p (b g d)"),
                                   ps_g[:, :, :, :].rearrange("p b g d -> p (b g d)"), GATE_MIN,
                                   minus[:, :, :, :].rearrange("p b g d -> p (b g d)"), ALU.max, ALU.max).then_inc(dve, 1)
            v.wait_ge(dve, 8)
            for b in range(B):
                v.scalar_tensor_tensor(C["ga"][:, b, :], sign[:, b, 0, :], -1.0, mag[:, b, 0, :], ALU.add, ALU.mult)
                for half in range(2):
                    v.scalar_tensor_tensor(C["gb"][:, 2 * b + half, :], sign[:, b, 1, :], -1.0, mag[:, b, 1, :],
                                           ALU.add, ALU.mult)
            v.wait_ge(products, 3)
            v.tensor_copy(C["sb"][:, :, :], ps_g[:, :, 0, :])
            v.tensor_scalar(C["cb"][:, :, :], ps_g[:, :, 1, :], 1.0, None, ALU.add)

        @block.tensor
        def _(pe):
            pe.wait_ge(loaded, 16 * loads)
            pe.wait_ge(dve, 3)
            for c in range(DC):
                pe.transpose(ps_gw[:, c, :], gw_row[:, c * P:(c + 1) * P], ident[0:E, 0:E])
            for c in range(DC):
                last = pe.transpose(ps_t[:, c, :], c_silu[:, c * P:(c + 1) * P], ident[0:B, 0:B])
            last.then_inc(transposed, 1)
            pe.wait_ge(c_t_done, 1)
            for i, m in enumerate(MOD_CHUNKS):
                for c in range(DC):
                    last = pe.matmul(ps_m[:, i, :], wmod_sb[:, c, m * P:(m + 1) * P], c_t[:, c, :],
                                     start=(c == 0), stop=(c == DC - 1))
            last.then_inc(products, 1)
            for pair in ((GA, GB), (SB_, CB)):
                if pair == (SB_, CB):
                    pe.wait_ge(dve, 8)
                for b in range(B):
                    for i, g in enumerate(pair):
                        for c in range(DC):
                            last = pe.matmul(ps_g[:, b, i, :], c_rep[:, c * B + b, :], wmod_sb[:, c, g * D:(g + 1) * D],
                                             start=(c == 0), stop=(c == DC - 1))
                last.then_inc(products, 1)


def qkv_stage(nc, C, x_flat, w_qkv, cos_dram, sin_dram, qk_dram, v_dram):
    QK = 2 * D
    QC = QK // P

    def steps_of(run, engine):
        def around(b, s, has):
            def tile(t, k):
                back = 1 if t < k else 0
                v = s - back
                return (b * SPB + v, (t - k) % TPS, v % 2, b * 2 + (v // 2 + 1)) if has(-back) else None
            return tile

        def within(u):
            return lambda k: 0 <= u + k < NST

        for u in range(-1, SPB):
            run(u // SPB, u % SPB, within(u)(1), around(u // SPB, u % SPB, within(u)))
        with engine.Fori(1, B - 1) as b:
            for s in range(SPB):
                run(b, s, True, around(b, s, lambda k: True))
        for u in range((B - 1) * SPB, NST + 1):
            run(u // SPB, u % SPB, within(u)(1), around(u // SPB, u % SPB, within(u)))

    with ExitStack() as ctx:
        def sb(name, shape, dt=F32):
            return ctx.enter_context(nc.sbuf_tensor(name, shape, dt))

        def ps(name, shape, dt=F32):
            return ctx.enter_context(nc.psum_tensor(name, shape, dt))

        def sem(name):
            return ctx.enter_context(nc.semaphore(name))

        ident, mod_t = C["ident"], C["mod_t"]
        cos = sb("cos", [P, NT, HD])
        sin = sb("sin", [P, NT, HD])
        wqkv = sb("wqkv", [P, DC, 3 * D])
        x_in = sb("x_in", [P, SPB, TPS, D])
        stats = sb("stats", [P, TPS, 6])
        mv = sb("mv", [P, TPS, 2])
        var = sb("var", [P, TPS])
        rstd = sb("rstd", [P, TPS])
        power = sb("power", [P, TPS])
        xn = sb("xn", [P, 2, TPS, D])
        h_t = sb("h_t", [P, 2, DC, ST])
        rot_c = sb("rot_c", [P, TPS, QK])
        rot_s = sb("rot_s", [P, TPS, QK])
        qk = sb("qk", [P, TPS, QK])
        rest = sb("rest", [P, TPS, QC, P])
        parts = sb("parts", [P, 2, 3, QC, ST], BF16)
        v_out = sb("v_out", [P, 2, TPS, H, VW])
        ps_ht = ps("ps_ht", [P, DC, ST])
        ps_qk = ps("ps_qk", [P, 2, QK])
        ps_v = ps("ps_v", [P, 2, QK])
        ps_x = ps("ps_x", [P, 2, QC, P])

        held = sem("p1_held")
        consts = sem("p1_consts")
        x_loaded = [sem(f"p1_x_loaded{i}") for i in range(SPB)]
        const_init = sem("p1_init")
        x_read = sem("p1_x_read")
        stat_done = sem("p1_stat")
        dve_own = sem("p1_dve_own")
        pool_own = sem("p1_pool_own")
        rstd_done = sem("p1_rstd")
        xn_done = sem("p1_xn")
        ht_turned = sem("p1_ht_turned")
        ht_done = sem("p1_ht")
        qk_done = sem("p1_qk")
        v_done = sem("p1_v")
        rope_done = sem("p1_rope")
        sum_done = sem("p1_sum")
        turned = sem("p1_turned")
        part1 = sem("p1_part1")
        rest_done = sem("p1_rest")
        part2 = sem("p1_part2")
        part3 = sem("p1_part3")
        qk_stored = [sem(f"p1_qk_stored{i}") for i in range(2)]
        v_stored = [sem(f"p1_v_stored{i}") for i in range(2)]
        QK_DMAS, V_DMAS = 2 * QC, GPB

        block = ctx.enter_context(nc.Block())

        @block.sync
        def _(sp):
            def load(u, slot):
                sp.wait_ge(x_read, u + 1)
                sp.dma_start(x_in[:, slot, :, :], x_flat[ds(u * ST, ST), :].rearrange("(t p) d -> p t d", p=P)) \
                    .then_inc(x_loaded[slot], 16)

            def body(b, last_batch):
                for s in range(SPB):
                    u = b * SPB + s
                    if not (last_batch and s >= 1):
                        load(u + 3, (s + 3) % SPB)
                    slot = s % 2
                    sp.wait_ge(v_done, (u + 1) * TPS + 2)
                    for hg in range(GPB):
                        row = b * (GPB * S) + (hg * S + s * ST)
                        sp.dma_start(v_dram[ds(row, ST), :].rearrange("(t p) d -> p t d", p=P),
                                     v_out[:, slot, :, hg * HG:(hg + 1) * HG, :].rearrange("p t h w -> p t (h w)")) \
                            .then_inc(v_stored[slot], 16)
                    sp.wait_ge(part3, (u + 1) * TPS + TPS)
                    for c in range(QC):
                        side, hc = c // DC, c % DC
                        for half in range(2):
                            g = b * GPB + (hc * 2 + half)
                            dst = qk_dram[ds(g, 1), side, :, :, s * ST:(s + 1) * ST]
                            sp.dma_start(dst.rearrange("o n r t -> r (o n) t"),
                                         parts[half * 64:half * 64 + 64, slot, :, c, :]) \
                                .then_inc(qk_stored[slot], 16)

            for slot in range(2):
                sp.sem_inc(qk_stored[slot], 16 * QK_DMAS)
                sp.sem_inc(v_stored[slot], 16 * V_DMAS)
            load(0, 0)
            load(1, 1)
            load(2, 2)
            sp.dma_start(wqkv[:, :, :], w_qkv.rearrange("(c p) n -> p c n", p=P)).then_inc(consts, 16)
            sp.dma_start(cos[:, :, :], cos_dram).then_inc(consts, 16)
            sp.dma_start(sin[:, :, :], sin_dram).then_inc(consts, 16)
            with sp.Fori(0, B - 1) as b:
                body(b, False)
            body(B - 1, True)
            for slot in range(2):
                sp.wait_ge(qk_stored[slot], 16 * QK_DMAS * (NST // 2 + 1))
                sp.wait_ge(v_stored[slot], 16 * V_DMAS * (NST // 2 + 1))

        @block.gpsimd
        def _(pool):
            pool.memset(v_out[:, :, :, :, :].rearrange("p a t h w -> p (a t h w)"), 0.0).then_inc(pool_own, 1)
            pool.wait_ge(pool_own, 1)
            pool.memset(v_out[:, :, :, :, HD:HD + 1].rearrange("p a t h w -> p (a t h) w"), 1.0).then_inc(const_init, 1)
            pool.memset(power[:, :], -0.5).then_inc(pool_own, 1)
            pool.wait_ge(pool_own, 2)
            pool.sem_inc(sum_done, TPS)
            pool.sem_inc(part3, TPS)

            def rstds(u):
                pool.wait_ge(stat_done, u + 1)
                stand_alone(pool, held)
                pool.tensor_scalar(var[:, :], mv[:, :, 1], EPS, None, ALU.add).then_inc(pool_own, 1)
                pool.wait_ge(pool_own, u + 3)
                pool.tensor_tensor(rstd[:, :], var[:, :], power[:, :], ALU.pow).then_inc(rstd_done, 1)

            def add(u, t):
                n = u * TPS + t
                pool.wait_ge(rope_done, n + 1 + TPS)
                pool.wait_ge(turned, n + 1)
                pool.tensor_tensor(qk[:, t, :], rot_c[:, t, :], rot_s[:, t, :], ALU.add).then_inc(sum_done, 1)

            def third(u, t, slot):
                pool.wait_ge(part2, u * TPS + (t + 1))
                pool.tensor_tensor(parts[:, slot, 2, :, t * P:(t + 1) * P], rest[:, t, :, :],
                                   parts[:, slot, 1, :, t * P:(t + 1) * P], ALU.subtract).then_inc(part3, 1)

            def run(b, s, more, tile):
                for t in range(TPS):
                    if tile(t, 0):
                        add(b * SPB + s, t)
                    if t == 0 and more:
                        rstds(b * SPB + s + 1)
                    if tile(t, 3):
                        u, tt, slot, _ = tile(t, 3)
                        third(u, tt, slot)

            steps_of(run, pool)

        @block.vector
        def _(v):
            v.sem_inc(x_read, SPB)
            v.sem_inc(rope_done, TPS)
            v.sem_inc(rest_done, 2)

            def stat(u, slot, turn):
                v.wait_ge(x_loaded[slot], turn * 16)
                for t in range(TPS):
                    last = v.bn_stats(stats[:, t, :], x_in[:, slot, t, :])
                last.then_inc(dve_own, 1)
                v.wait_ge(dve_own, u + 1)
                stand_alone(v, held)
                for t in range(TPS):
                    last = v.bn_aggr(mv[:, t, :], stats[:, t, :])
                last.then_inc(stat_done, 1)

            def normalise(u, slot, x_slot):
                v.wait_ge(rstd_done, u + 1)
                for t in range(TPS):
                    ins = v.tensor_scalar(xn[:, slot, t, :], x_in[:, x_slot, t, :], mv[:, t, 0:1], rstd[:, t:t + 1],
                                          ALU.subtract, ALU.mult)
                    ins.then_inc(xn_done, 1)
                v.wait_ge(xn_done, (u + 1) * TPS)
                v.sem_inc(x_read, 1)

            def rope(u, t, tile):
                n = u * TPS + t
                v.wait_ge(qk_done, n + 1)
                v.wait_ge(sum_done, n + 1)
                src = ps_qk[:, t % 2, :].rearrange("p (g d) -> p g d", d=HD)
                c = rot_c[:, t, :].rearrange("p (g d) -> p g d", d=HD)
                s = rot_s[:, t, :].rearrange("p (g d) -> p g d", d=HD)
                G = QK // HD
                v.tensor_tensor(c, src, cos[:, tile, :].unsqueeze(1).to_broadcast([P, G, HD]), ALU.mult)
                v.tensor_tensor(s[:, :, 0:HALF], src[:, :, HALF:HD],
                                sin[:, tile, 0:HALF].unsqueeze(1).to_broadcast([P, G, HALF]), ALU.mult)
                v.tensor_tensor(s[:, :, HALF:HD], src[:, :, 0:HALF],
                                sin[:, tile, HALF:HD].unsqueeze(1).to_broadcast([P, G, HALF]), ALU.mult) \
                    .then_inc(rope_done, 1)

            def leave(u, t, slot):
                n = u * TPS + t
                v.wait_ge(part1, n + 1)
                v.wait_ge(part3, n + 1)
                v.tensor_tensor(rest[:, t, :, :], ps_x[:, t % 2, :, :],
                                parts[:, slot, 0, :, t * P:(t + 1) * P], ALU.subtract).then_inc(rest_done, 1)

            def run(b, s, more, tile):
                for t in range(TPS):
                    if tile(t, 0):
                        rope(b * SPB + s, t, s * TPS + t)
                    if t == 0 and more:
                        stat(b * SPB + s + 1, (s + 1) % SPB, b + ((s + 1) // SPB + 1))
                    if tile(t, 3):
                        u, tt, slot, _ = tile(t, 3)
                        leave(u, tt, slot)
                    if t == 1 and more:
                        normalise(b * SPB + s + 1, (s + 1) % 2, (s + 1) % SPB)

            v.wait_ge(consts, 16 * 3)
            steps_of(run, v)

        @block.scalar
        def _(act):
            act.sem_inc(ht_done, 2)
            act.sem_inc(v_done, 2)

            def modulate(u, slot, b):
                for c in range(DC):
                    act.wait_ge(ht_turned, u * DC + (c + 1))
                    stand_alone(act, held)
                    act.activation(h_t[:, slot, c, :], ps_ht[:, c, :], ACT.Identity,
                                   bias=mod_t[:, M_SA + c, ds(b, 1)], scale=mod_t[:, M_CA + c, ds(b, 1)]) \
                        .then_inc(ht_done, 1)

            def take_v(u, t, slot, turn):
                if t == 0:
                    act.wait_ge(v_stored[slot], turn * (16 * V_DMAS))
                act.wait_ge(qk_done, u * TPS + (t + 1))
                act.activation(v_out[:, slot, t, :, 0:HD],
                               ps_v[:, t % 2, 0:D].rearrange("p (h d) -> p h d", d=HD), ACT.Copy).then_inc(v_done, 1)

            def first(u, t, slot, turn):
                if t == 0:
                    act.wait_ge(qk_stored[slot], turn * (16 * QK_DMAS))
                act.wait_ge(turned, u * TPS + (t + 1 + TPS))
                act.activation(parts[:, slot, 0, :, t * P:(t + 1) * P], ps_x[:, t % 2, :, :], ACT.Copy) \
                    .then_inc(part1, 1)

            def second(u, t, slot):
                act.wait_ge(rest_done, u * TPS + (t + 1 + 2))
                act.activation(parts[:, slot, 1, :, t * P:(t + 1) * P], rest[:, t, :, :], ACT.Copy) \
                    .then_inc(part2, 1)

            def run(b, s, more, tile):
                for t in range(TPS):
                    if t == 2 and more:
                        modulate(b * SPB + s + 1, (s + 1) % 2, b + (s + 1) // SPB)
                    if tile(t, 0):
                        take_v(b * SPB + s, t, s % 2, b * 2 + (s // 2 + 1))
                    if tile(t, 2):
                        first(*tile(t, 2))
                    if tile(t, 3):
                        u, tt, slot, _ = tile(t, 3)
                        second(u, tt, slot)

            act.wait_ge(const_init, 1)
            steps_of(run, act)

        @block.tensor
        def _(pe):
            pe.sem_inc(turned, TPS)

            def turn_h(u, slot):
                for c in range(DC):
                    pe.wait_ge(ht_done, u * DC + (c + 1))
                    for t in range(TPS):
                        if c == 0:
                            pe.wait_ge(xn_done, u * TPS + (t + 1))
                        last = pe.transpose(ps_ht[:, c, t * P:(t + 1) * P], xn[:, slot, t, c * P:(c + 1) * P], ident[:, :])
                    last.then_inc(ht_turned, 1)

            def products(u, t, slot):
                n = u * TPS + t
                if t == 0:
                    pe.wait_ge(ht_done, u * DC + (DC + 2))
                pe.wait_ge(rope_done, n + TPS - 1)
                pe.wait_ge(v_done, n + 1)
                for c in range(DC):
                    pe.matmul(ps_qk[:, t % 2, :], h_t[:, slot, c, t * P:(t + 1) * P], wqkv[:, c, 0:QK],
                              start=(c == 0), stop=(c == DC - 1))
                for c in range(DC):
                    last = pe.matmul(ps_v[:, t % 2, 0:D], h_t[:, slot, c, t * P:(t + 1) * P], wqkv[:, c, QK:3 * D],
                                     start=(c == 0), stop=(c == DC - 1))
                last.then_inc(qk_done, 1)

            def turn_qk(u, t):
                n = u * TPS + t
                pe.wait_ge(sum_done, n + 1 + TPS)
                pe.wait_ge(rest_done, n + 1)
                for c in range(QC):
                    last = pe.transpose(ps_x[:, t % 2, c, :], qk[:, t, c * P:(c + 1) * P], ident[:, :])
                last.then_inc(turned, 1)

            def run(b, s, more, tile):
                for t in range(TPS):
                    if tile(t, 0):
                        products(b * SPB + s, t, s % 2)
                    if tile(t, 2):
                        u, tt, _, _ = tile(t, 2)
                        turn_qk(u, tt)
                    if t == 2 and more:
                        turn_h(b * SPB + s + 1, (s + 1) % 2)

            pe.wait_ge(consts, 16 * 3)
            steps_of(run, pe)


def attention_stage(nc, C, qk_dram, v_dram, o_dram):
    MROWS = 2
    NQ = SPB
    POSITIONS = [(qt, kc) for qt in reversed(range(NQ)) for kc in range(TPS * (qt + 1))]
    NPOS = len(POSITIONS)
    STEPS = 2 * NPOS
    LAST_OF = [u for u, (qt, kc) in enumerate(POSITIONS) if kc == TPS * (qt + 1) - 1]
    LATE = TPS * (NQ - 1)
    PIECES = [(kt, qi, h) for kt in reversed(range(NQ)) for qi in reversed(range(TPS * kt, NT)) for h in range(HG)]
    LATE_END = 1 + max(i for i, (kt, qi, h) in enumerate(PIECES) if qi >= LATE)
    LATE_LAG = 8
    ITEMS = ["turn rest"] + PIECES[:LATE_END + LATE_LAG] + ["turn late"] + PIECES[LATE_END + LATE_LAG:]
    NITEM = len(ITEMS)
    COUNT = ((HG * TPS, LATE, TPS), (HG * LATE, 0, LATE))
    PSLOTS = 4
    LOADS = 2 * len(QPART)
    MAX_DMAS = MROWS * HG

    def items_at(u):
        a, b = (NITEM * (u - 1) // (NPOS - 1), NITEM * u // (NPOS - 1)) if u else (0, 0)
        return range(a, b)

    with ExitStack() as ctx:
        def sb(name, shape, dt=F32):
            return ctx.enter_context(nc.sbuf_tensor(name, shape, dt))

        def ps(name, shape, dt=F32):
            return ctx.enter_context(nc.psum_tensor(name, shape, dt))

        def sem(name):
            return ctx.enter_context(nc.semaphore(name))

        ident, ident_b = C["ident"], C["ident_b"]
        mask_qk = sb("mask_qk", [P, P], BF16)
        mask_kq = sb("mask_kq", [P, P], BF16)
        q_st = sb("q_st", [P, 2, HG, S], BF16)
        k_st = sb("k_st", [P, 2, HG, S], BF16)
        vs = sb("vs", [P, 2, NT, HG * VW])
        probs = sb("probs", [P, PSLOTS, HG, ST])
        piece_late = sb("piece_late", [P, HG * TPS, NQ])
        piece_rest = sb("piece_rest", [P, HG * LATE, NQ - 1])
        nmax = [sb("nmax_late", [P, COUNT[0][0]]), sb("nmax_rest", [P, COUNT[1][0]])]
        top = sb("top", [P, 2, P], BF16)
        low = sb("low", [P, 2, P], BF16)
        o_t = sb("o_t", [P, 2, ST])
        o_inv = sb("o_inv", [P, 2, TPS * HG])
        o_out = sb("o_out", [P, 2, TPS * HG, HD])
        ps_s = ps("ps_s", [P, 2, 2, ST])
        ps_m = ps("ps_m", [P, 2, ST])
        ps_o = ps("ps_o", [P, ST])
        ps_t = ps("ps_t", [P, TPS, P])

        held = sem("p2_held")
        init = sem("p2_init")
        pool_own = sem("p2_pool_own")
        qk_in = [[sem(f"p2_in{s}_{r}") for r in range(NQ)] for s in range(2)]
        v_in = [sem(f"p2_v{s}") for s in range(2)]
        scored = sem("p2_scored")
        exp_done = sem("p2_exp")
        pv_done = sem("p2_pv")
        m_done = sem("p2_m")
        m_taken = sem("p2_m_taken")
        max_own = sem("p2_max_own")
        top_own = sem("p2_top_own")
        max_cut = sem("p2_max_cut")
        max_in = [[sem(f"p2_max{s}_{l}") for l in range(2)] for s in range(2)]
        o_copied = sem("p2_o_copied")
        o_turned = sem("p2_o_turned")
        inv_own = sem("p2_inv_own")
        o_done = sem("p2_o")
        o_stored = [sem(f"p2_o_stored{i}") for i in range(2)]

        block = ctx.enter_context(nc.Block())

        @block.sync
        def _(sp):
            def load_region(g, slot, r):
                cols = slice(r * ST, (r + 1) * ST)
                for stack, side, which in ((k_st, 1, KPART), (q_st, 0, QPART)):
                    for i, part in enumerate(which):
                        sp.dma_start(stack[i * HD:(i + 1) * HD, slot, :, cols],
                                     qk_dram[ds(g, 1), side, part, :, cols].rearrange("o (h d) t -> d (o h) t", d=HD)) \
                            .then_inc(qk_in[slot][r], 16)

            def load_v(g, slot):
                for r in range(NQ):
                    sp.dma_start(vs[:, slot, r * TPS:(r + 1) * TPS, :],
                                 v_dram[ds(g * S + r * ST, ST), :].rearrange("(n p) w -> p n w", p=P)) \
                        .then_inc(v_in[slot], 16)

            def store_max(gm, slot, l):
                n, q0, nq = COUNT[l]
                sp.wait_ge(max_cut, gm * 2 + (l + 1))
                for row, src in ((ROWS, top), (ROWS + 1, low)):
                    for h in range(HG):
                        sp.dma_start(q_st[row:row + 1, slot, h, q0 * P:(q0 + nq) * P],
                                     src[h * nq:(h + 1) * nq, l, :]).then_inc(max_in[slot][l], 16)

            def store_o(g, k):
                sp.wait_ge(o_done, g * NQ + (k + 1 + 1))
                row = g * S + (NQ - 1 - k) * ST
                sp.dma_start(o_dram[ds(row, ST), :].rearrange("(t p) d -> p t d", p=P),
                             o_out[:, k % 2, :, :].rearrange("p (t h) d -> p t (h d)", h=HG)) \
                    .then_inc(o_stored[k % 2], 16)

            def body(it, par, loads, maxima):
                g = it * 2 + par
                store_max(g, par, 1)
                for k in range(NQ):
                    if k == 2 and maxima:
                        store_max(g + 1, 1 - par, 0)
                    if loads:
                        sp.wait_ge(scored, g * STEPS + 2 * (LAST_OF[k] + 1))
                        load_region(g + 2, par, NQ - 1 - k)
                    store_o(g, k)
                if loads:
                    sp.wait_ge(pv_done, g * NPOS + (NPOS + PSLOTS))
                    load_v(g + 2, par)

            for slot in range(2):
                for r in reversed(range(NQ)):
                    load_region(slot, slot, r)
                load_v(slot, slot)
                sp.sem_inc(o_stored[slot], 16)
            sp.sem_inc(max_in[1][1], 16 * MAX_DMAS)
            store_max(0, 0, 0)
            with sp.Fori(0, GROUPS // 2 - 1) as it:
                body(it, 0, True, True)
                body(it, 1, True, True)
            body(GROUPS // 2 - 1, 0, False, True)
            body(GROUPS // 2 - 1, 1, False, False)
            for slot in range(2):
                sp.wait_ge(o_stored[slot], 16 * (GROUPS * NQ // 2 + 1))

        @block.gpsimd
        def _(pool):
            pool.memset(mask_qk[:, :], 0.0).then_inc(pool_own, 1)
            pool.memset(mask_kq[:, :], 0.0).then_inc(pool_own, 1)
            pool.memset(piece_rest[:, :, :].rearrange("p n k -> p (n k)"), LOWEST).then_inc(init, 1)
            pool.wait_ge(pool_own, 2)
            pool.affine_select(out=mask_qk[:, :], in_=mask_qk[:, :], compare_op=ALU.is_ge, fill=NEG, base=0,
                               pattern=[[-1, P]], channel_multiplier=1).then_inc(init, 1)
            pool.affine_select(out=mask_kq[:, :], in_=mask_kq[:, :], compare_op=ALU.is_ge, fill=NEG, base=0,
                               pattern=[[1, P]], channel_multiplier=-1).then_inc(init, 1)
            pool.wait_ge(init, 3)
            pool.memset(k_st[ROWS:ROWS + MROWS, :, :, :].rearrange("p s h t -> p (s h t)"), 1.0).then_inc(init, 1)

        @block.scalar
        def _(act):
            act.sem_inc(exp_done, 2)
            act.sem_inc(o_copied, 1)

            def copy_o(g, k):
                act.wait_ge(pv_done, g * NPOS + (LAST_OF[k] + 1 + PSLOTS))
                act.wait_ge(o_turned, g * NQ + (k + 1))
                act.activation(o_t[:, k % 2, :], ps_o[:, :], ACT.Copy).then_inc(o_copied, 1)

            with act.Fori(0, GROUPS) as g:
                for u, (qt, kc) in enumerate(POSITIONS):
                    j = max(0, kc - TPS * qt)
                    for pair in range(2):
                        act.wait_ge(scored, g * STEPS + (2 * u + pair + 1))
                        if pair == 0:
                            act.wait_ge(pv_done, g * NPOS + (u + 1))
                        act.activation(probs[:, u % PSLOTS, 2 * pair:2 * pair + 2, j * P:ST],
                                       ps_s[:, pair, :, j * P:ST], ACT.Exp, scale=SCALE).then_inc(exp_done, 1)
                    if u - 1 in LAST_OF:
                        copy_o(g, LAST_OF.index(u - 1))
                copy_o(g, NQ - 1)

        @block.vector
        def _(v):
            v.sem_inc(m_taken, 2)
            v.sem_inc(o_done, 1)
            v.wait_ge(init, 4)

            def piece(what, count, bank):
                kt, qi, h = what
                w = min(ST, (qi + 1) * P - kt * ST)
                dst = piece_late[:, h * TPS + qi - LATE, kt:kt + 1] if qi >= LATE else \
                    piece_rest[:, h * LATE + qi, kt:kt + 1]
                v.wait_ge(m_done, count)
                v.tensor_reduce(dst, ps_m[:, bank, 0:w], AX.X, ALU.max).then_inc(m_taken, 1)

            def negate(l, count):
                v.wait_ge(m_taken, count + 2)
                v.tensor_reduce(nmax[l][:, :], (piece_late, piece_rest)[l][:, :, :], AX.X, ALU.max, negate=True) \
                    .then_inc(max_own, 1)

            def cut(gm, l, count, bank):
                n = COUNT[l][0]
                v.wait_ge(m_done, count)
                v.tensor_copy(top[0:n, l, :], ps_m[0:n, bank, 0:P]).then_inc(top_own, 1)
                v.wait_ge(top_own, gm * 2 + (l + 1))
                v.tensor_tensor(low[0:n, l, :], ps_m[0:n, bank, 0:P], top[0:n, l, :], ALU.subtract).then_inc(max_cut, 1)
                v.wait_ge(max_cut, gm * 2 + (l + 1))
                v.sem_inc(m_taken, 1)

            def item(gm, i, base, stored):
                bank = (i + 1) % 2
                what = ITEMS[i]
                if what == "turn rest":
                    if stored[1]:
                        v.wait_ge(*stored[1])
                    cut(gm - 1, 1, base + i + 1, bank)
                elif what == "turn late":
                    if stored[0]:
                        v.wait_ge(*stored[0])
                    cut(gm, 0, base + i + 1, bank)
                else:
                    piece(what, base + i + 1, bank)
                    if i == LATE_END:
                        negate(0, base + i + 1)

            def divide(g, k):
                v.wait_ge(o_turned, g * NQ + (k + 1 + 2))
                flat = ps_t[:, :, :].rearrange("p t (h w) -> p (t h) w", w=VW)
                v.reciprocal(o_inv[:, k % 2, :], flat[:, :, HD]).then_inc(inv_own, 1)
                v.wait_ge(inv_own, g * NQ + (k + 1))
                v.wait_ge(o_stored[k % 2], g * (16 * NQ // 2) + 16 * (k // 2 + 1))
                v.tensor_tensor(o_out[:, k % 2, :, :], flat[:, :, 0:HD],
                                o_inv[:, k % 2, :].unsqueeze(2).to_broadcast([P, TPS * HG, HD]), ALU.mult) \
                    .then_inc(o_done, 1)

            def body(it, par, maxima):
                g = it * 2 + par
                base = g * NITEM + (NITEM - 1)
                stored = ((max_in[par][0], (it + 1) * (16 * MAX_DMAS)),
                          (max_in[1 - par][1], (it + 1) * (16 * MAX_DMAS)))
                for u in range(NPOS):
                    for i in items_at(u):
                        if maxima or i == 0:
                            item(g + 1, i, base, stored)
                    if u - 3 in LAST_OF:
                        divide(g, LAST_OF.index(u - 3))
                if maxima:
                    negate(1, base + NITEM)
                divide(g, NQ - 1)

            for i in range(1, NITEM):
                item(0, i, -1, (None, None))
            negate(1, NITEM - 1)
            with v.Fori(0, GROUPS // 2 - 1) as it:
                body(it, 0, True)
                body(it, 1, True)
            body(GROUPS // 2 - 1, 0, True)
            body(GROUPS // 2 - 1, 1, False)

        @block.tensor
        def _(pe):
            pe.sem_inc(pv_done, PSLOTS)
            pe.sem_inc(o_turned, 2)
            pe.wait_ge(init, 4)

            def item(gm, i, base, slot, turn):
                bank = (i + 1) % 2
                what = ITEMS[i]
                pe.wait_ge(m_taken, base + i + 1)
                if isinstance(what, str):
                    l = 1 if what == "turn rest" else 0
                    pe.wait_ge(max_own, (gm - l) * 2 + (l + 1))
                    stand_alone(pe, held)
                    pe.transpose(ps_m[0:COUNT[l][0], bank, 0:P], nmax[l][:, :], ident[:, :]).then_inc(m_done, 1)
                    return
                kt, qi, h = what
                if i == 1 or ITEMS[i - 1][0] != kt:
                    pe.wait_ge(qk_in[slot][kt], turn * (16 * LOADS))
                w = min(ST, (qi + 1) * P - kt * ST)
                diag = kt == qi // TPS
                last = pe.matmul(ps_m[:, bank, 0:w], q_st[0:ROWS, slot, h, qi * P:(qi + 1) * P],
                                 k_st[0:ROWS, slot, h, kt * ST:kt * ST + w], start=True, stop=not diag)
                if diag:
                    last = pe.matmul(ps_m[:, bank, w - P:w], ident_b[:, :], mask_qk[:, :], start=False, stop=True)
                last.then_inc(m_done, 1)

            def scores(g, u, slot, pair):
                qt, kc = POSITIONS[u]
                diag = kc >= TPS * qt
                j = max(0, kc - TPS * qt)
                pe.wait_ge(exp_done, g * STEPS + (2 * u + pair + 1))
                for hh in range(2):
                    h = 2 * pair + hh
                    last = pe.matmul(ps_s[:, pair, hh, j * P:ST],
                                     k_st[0:ROWS + MROWS, slot, h, kc * P:(kc + 1) * P],
                                     q_st[0:ROWS + MROWS, slot, h, qt * ST + j * P:(qt + 1) * ST],
                                     start=True, stop=not diag)
                    if diag:
                        last = pe.matmul(ps_s[:, pair, hh, j * P:(j + 1) * P], ident_b[:, :], mask_kq[:, :],
                                         start=False, stop=True)
                last.then_inc(scored, 1)

            def values(g, u, slot, pair):
                qt, kc = POSITIONS[u]
                j = max(0, kc - TPS * qt)
                if kc == 0:
                    pe.wait_ge(o_copied, g * NQ + (NQ - 1 - qt + 1))
                pe.wait_ge(exp_done, g * STEPS + (2 * u + pair + 1 + 2))
                for h in (2 * pair, 2 * pair + 1):
                    last = pe.matmul(ps_o[h * VW:(h + 1) * VW, j * P:ST], vs[:, slot, kc, h * VW:(h + 1) * VW],
                                     probs[:, u % PSLOTS, h, j * P:ST], start=(kc == 0),
                                     stop=(kc == TPS * (qt + 1) - 1), skip_group_check=True)
                if pair == 1:
                    last.then_inc(pv_done, 1)

            def turn_o(g, k):
                pe.wait_ge(o_copied, g * NQ + (k + 1 + 1))
                pe.wait_ge(o_done, g * NQ + (k + 1))
                for t in range(TPS):
                    last = pe.transpose(ps_t[:, t, :], o_t[:, k % 2, t * P:(t + 1) * P], ident[:, :])
                last.then_inc(o_turned, 1)

            def body(it, par, maxima):
                g = it * 2 + par
                base = g * NITEM + (NITEM - 1)
                credits = 1 if par else 0
                for u, (qt, kc) in enumerate(POSITIONS):
                    if u == 0:
                        pe.wait_ge(v_in[par], (it + 1) * (16 * NQ))
                    todo = [i for i in items_at(u) if maxima or i == 0]
                    for step in range(4):
                        if step >= 2:
                            values(g, u, par, step - 2)
                        elif u + 1 < NPOS:
                            if step == 0 and u == LAST_OF[0]:
                                pe.wait_ge(max_in[par][1], (it + 1 + credits) * (16 * MAX_DMAS))
                            scores(g, u + 1, par, step)
                        elif maxima:
                            if step == 0:
                                pe.wait_ge(max_in[1 - par][0], (it + 1 + par) * (16 * MAX_DMAS))
                            scores(g + 1, 0, 1 - par, step)
                        for i in todo[len(todo) * step // 4:len(todo) * (step + 1) // 4]:
                            item(g + 1, i, base, 1 - par, it + (1 + par))
                    if u - 2 in LAST_OF:
                        turn_o(g, LAST_OF.index(u - 2))
                turn_o(g, NQ - 1)

            for i in range(1, NITEM):
                item(0, i, -1, 0, 1)
            pe.wait_ge(max_in[0][0], 16 * MAX_DMAS)
            for pair in range(2):
                scores(0, 0, 0, pair)
            with pe.Fori(0, GROUPS // 2 - 1) as it:
                body(it, 0, True)
                body(it, 1, True)
            body(GROUPS // 2 - 1, 0, True)
            body(GROUPS // 2 - 1, 1, False)


def middle_stage(nc, C, o_dram, x_flat, w_proj, b_proj, iota_dram, x1_dram, h2_dram,
                 rows_dram, steps_dram, plan_dram):
    FIRST, LAST = -4, NST
    RSLOTS = 4

    def steps_of(run, engine):
        def within(u):
            return lambda k: 0 <= u + k < NST

        for u in range(FIRST, SPB):
            run(u // SPB, u % SPB, within(u))
        with engine.Fori(1, B - 1) as b:
            for s in range(SPB):
                run(b, s, lambda k: True)
        for u in range((B - 1) * SPB, LAST + 1):
            run(u // SPB, u % SPB, within(u))
    with ExitStack() as ctx:
        def sb(name, shape, dt=F32):
            return ctx.enter_context(nc.sbuf_tensor(name, shape, dt))

        def ps(name, shape, dt=F32):
            return ctx.enter_context(nc.psum_tensor(name, shape, dt))

        def sem(name):
            return ctx.enter_context(nc.semaphore(name))

        ident, ga, gate_t, sb_row, cb_row = (C[k] for k in ("ident", "ga", "gate_t", "sb", "cb"))
        count, plan = C["count"], C["plan"]
        wp = sb("wp", [P, DC, D])
        bp = sb("bp", [P, D])
        bga = sb("bga", [P, B, D])
        iota = sb("iota", [P, TPS, E])
        o_in = sb("o_in", [P, 2, TPS, D])
        x_in = sb("x_in3", [P, 2, TPS, D])
        o_t = sb("o_t3", [P, 2, DC, ST])
        y = sb("y", [P, 2, TPS, D])
        xb = sb("xb", [P, 2, TPS, D])
        x1 = sb("x1", [P, 2, TPS, D])
        stats = sb("stats3", [P, TPS, 6])
        mv = sb("mv3", [P, TPS, 2])
        var = sb("var3", [P, TPS])
        power = sb("power3", [P, TPS])
        rstd = sb("rstd3", [P, TPS])
        xn = sb("xn3", [P, TPS, D])
        scaled = sb("scaled", [P, TPS, D])
        rows = sb("rows", [P, RSLOTS, TPS, D])
        h2 = sb("h2", [P, 2, DC, ST])
        lg = sb("lg", [P, TPS, E])
        lmax = sb("lmax", [P, TPS])
        ex = sb("ex", [P, TPS, E])
        z = sb("z", [P, TPS])
        rz = sb("rz", [P, TPS])
        sc = sb("sc", [P, TPS, E])
        best = sb("best", [P, TPS, 8])
        which = sb("which", [P, TPS, 8], U32)
        which_f = sb("which_f", [P, TPS, 8])
        s2 = sb("s2", [P, TPS])
        r2 = sb("r2", [P, TPS])
        w2 = sb("w2", [P, TPS, 2])
        hit = sb("hit", [P, TOPK, TPS, E])
        chosen = sb("chosen", [P, TPS, E], BF16)
        strict = sb("strict", [P, P], BF16)
        ones = sb("ones", [P, P], BF16)
        place = sb("place", [P, TPS, E])
        placed = sb("placed", [P, TOPK, TPS, E])
        rank = sb("rank", [P, TOPK, TPS])
        totals = sb("totals", [P, E])
        at_f = sb("at_f", [P, TOPK, TPS])
        at = sb("at", [P, RSLOTS, TOPK * TPS], U32)
        steps = sb("steps", [P, E, MOST])
        tables = sb("tables", [P, 3, NB, E])
        over = sb("over", [P, E, MOST])
        blocks = sb("blocks", [P, E])
        ends = sb("ends", [P, 4, E])
        start = sb("start", [P, E])
        start_row = sb("start_row", [P, E])
        past = sb("past", [P, 2, NB, E])
        inside = sb("inside", [P, NB, E])
        row_e = sb("row_e", [P, 2, NB, E])
        plan_f = sb("plan_f", [P, 2, NB])
        pad_f = sb("pad_f", [P, E])
        pad_at = sb("pad_at", [P, E], U32)
        mine = sb("mine", [P, NST * TOPK * TPS, E])
        made_f = sb("made_f", [P, NST * TOPK * TPS])
        zeros = sb("zeros", [P, TPS, D])
        ps_o = ps("ps_o3", [P, DC, ST])
        ps_p = ps("ps_p", [P, TPS, D])
        ps_h = ps("ps_h", [P, DC, ST])
        ps_l = ps("ps_l", [P, TPS, E])
        ps_rank = ps("ps_rank", [P, TPS + 1, E])
        ps_r, ps_all = ps_rank[:, 0:TPS, :], ps_rank[:, TPS, :]

        held = sem("p3_held")
        consts = sem("p3_consts")
        in_done = [sem(f"p3_in{i}") for i in range(2)]
        o_read = sem("p3_o_read")
        xb_done = sem("p3_xb")
        ot_done = sem("p3_ot")
        ot_read = sem("p3_ot_read")
        y_done = sem("p3_y")
        x1_done = sem("p3_x1")
        x1_read = sem("p3_x1_read")
        dve_own = sem("p3_dve_own")
        stat_done = sem("p3_stat")
        pool_own = sem("p3_pool_own")
        rstd_done = sem("p3_rstd")
        turned = sem("p3_turned")
        h2_done = sem("p3_h2")
        logits = sem("p3_logits")
        lmax_done = sem("p3_lmax")
        ex_done = sem("p3_ex")
        max_own = sem("p3_max")
        route = sem("p3_route")
        init = sem("p3_init")
        scale_done = sem("p3_scale")
        rows_done = sem("p3_rows")
        chosen_done = sem("p3_chosen")
        ranked = sem("p3_ranked")
        locate_own = sem("p3_locate_own")
        at_done = sem("p3_at")
        scattered = sem("p3_scattered")
        rows_out = sem("p3_rows_out")
        x1_stored = [sem(f"p3_x1_stored{i}") for i in range(2)]
        h2_stored = [sem(f"p3_h2_stored{i}") for i in range(2)]
        tables_in = sem("p3_tables")
        zeroed = sem("p3_zeroed")
        step_done = sem("p3_step")
        planned = sem("p3_planned")
        padded = sem("p3_padded")
        IN_DMAS = 1 + GPB
        ROUTE = 11
        LOCATE = 4

        block = ctx.enter_context(nc.Block())

        @block.sync
        def _(sp):
            sp.dma_start(wp[:, :, :], w_proj.rearrange("(c p) n -> p c n", p=P)).then_inc(consts, 16)
            sp.dma_start(bp[:, :], b_proj.rearrange("(o d) -> o d", o=1).to_broadcast([P, D])).then_inc(consts, 16)
            sp.dma_start(iota[:, :, :], iota_dram).then_inc(consts, 16)

            def load(u, slot, b, part):
                sp.wait_ge(o_read, u + 1)
                sp.wait_ge(xb_done, u + 1)
                for hg in range(GPB):
                    sp.dma_start(o_in[:, slot, :, hg * HG * HD:(hg + 1) * HG * HD],
                                 o_dram[ds(b * (GPB * S) + (hg * S + part * ST), ST), :]
                                 .rearrange("(t p) d -> p t d", p=P)).then_inc(in_done[slot], 16)
                sp.dma_start(x_in[:, slot, :, :], x_flat[ds(u * ST, ST), :].rearrange("(t p) d -> p t d", p=P)) \
                    .then_inc(in_done[slot], 16)

            def run(b, s, has):
                u = b * SPB + s
                if has(4):
                    load(u + 4, s % 2, b + 1, s)
                if has(2):
                    sp.wait_ge(x1_done, u + 3)
                    sp.dma_start(x1_dram[ds((u + 2) * ST, ST), :].rearrange("(t p) d -> p t d", p=P), x1[:, s % 2, :, :]) \
                        .then_inc(x1_stored[s % 2], 16)
                if has(1):
                    sp.wait_ge(h2_done, u * DC + (2 * DC + 2))
                    sp.dma_start(h2_dram[ds((u + 1) * P, P), :], h2[:, (s + 1) % 2, :, :].rearrange("p c t -> p (c t)")) \
                        .then_inc(h2_stored[(s + 1) % 2], 16)

            for slot in range(2):
                sp.sem_inc(x1_stored[slot], 16)
                sp.sem_inc(h2_stored[slot], 16)
            sp.dma_start(steps[:, :, :], steps_dram).then_inc(tables_in, 16)
            sp.dma_start(tables[:, :, :, :].rearrange("p k n e -> p (k n e)"),
                         plan_dram.rearrange("p k n e -> p (k n e)")).then_inc(tables_in, 16)
            steps_of(run, sp)
            sp.wait_ge(planned, 1)
            sp.wait_ge(zeroed, 1)
            for e in range(E):
                row = sp.value_load(pad_at[0:1, e:e + 1], min_val=0, max_val=E * REGION - ST)
                sp.dma_start(rows_dram[ds(row, ST), :].rearrange("(t p) d -> p t d", p=P), zeros[:, :, :]) \
                    .then_inc(padded, 16)
            sp.wait_ge(padded, 16 * E)
            for slot in range(2):
                sp.wait_ge(x1_stored[slot], 16 * (NST // 2 + 1))
                sp.wait_ge(h2_stored[slot], 16 * (NST // 2 + 1))

        @block.gpsimd
        def _(pool):
            pool.memset(zeros[:, :, :].rearrange("p t d -> p (t d)"), 0.0).then_inc(zeroed, 1)
            pool.memset(power[:, :], -0.5).then_inc(pool_own, 1)
            pool.wait_ge(pool_own, 1)
            pool.wait_ge(consts, 48)
            for b in range(B):
                last = pool.tensor_tensor(bga[:, b, :], ga[:, b, :], bp[:, :], ALU.mult)
            last.then_inc(pool_own, 1)
            pool.wait_ge(pool_own, 2)
            pool.sem_inc(xb_done, 2)
            pool.sem_inc(rows_out, RSLOTS)
            pool.memset(count[:, :], 0.0).then_inc(init, 1)
            pool.memset(ones[:, :], 1.0).then_inc(init, 1)
            pool.memset(strict[:, :], 1.0).then_inc(init, 1)
            pool.wait_ge(init, 3)
            pool.affine_select(out=strict[:, :], in_=strict[:, :], compare_op=ALU.is_ge, fill=0.0, base=-1,
                               pattern=[[1, P]], channel_multiplier=-1).then_inc(init, 1)

            def scatter(u, rslot):
                pool.wait_ge(at_done, u + 2)
                stand_alone(pool, held)
                for j in range(TOPK * TPS):
                    pool.indirect_dma_start(rows_dram, bass.IndirectOffsetOnAxis(at[:, rslot, j:j + 1], 0),
                                            rows[:, rslot, j % TPS, :], None).then_inc(scattered, 16)
                pool.wait_ge(scattered, u * (16 * TOPK * TPS) + 16 * TOPK * TPS)
                pool.sem_inc(rows_out, 1)

            def run(b, s, has):
                u = b * SPB + s
                slot = s % 2
                turn = b * 2 + (s // 2 + 2)
                if has(2):
                    pool.wait_ge(in_done[slot], turn * (16 * IN_DMAS))
                    stand_alone(pool, held)
                    pool.tensor_tensor(xb[:, slot, :, :], x_in[:, slot, :, :],
                                       bga[:, ds(b + (s + 2) // SPB, 1), :].to_broadcast([P, TPS, D]), ALU.add) \
                        .then_inc(xb_done, 1)
                if has(1):
                    pool.wait_ge(stat_done, u + 2)
                    stand_alone(pool, held)
                    pool.tensor_scalar(var[:, :], mv[:, :, 1], EPS, None, ALU.add).then_inc(pool_own, 1)
                    pool.wait_ge(pool_own, u + 4)
                    pool.tensor_tensor(rstd[:, :], var[:, :], power[:, :], ALU.pow).then_inc(rstd_done, 1)
                if has(2):
                    pool.wait_ge(xb_done, u + 3 + 2)
                    pool.wait_ge(y_done, u + 3 + 1)
                    pool.wait_ge(x1_stored[slot], turn * 16)
                    pool.wait_ge(x1_read, u + 3)
                    pool.tensor_tensor(x1[:, slot, :, :], y[:, slot, :, :], xb[:, slot, :, :], ALU.add) \
                        .then_inc(x1_done, 1)
                if has(-1):
                    scatter(u - 1, (s - 1) % RSLOTS)

            steps_of(run, pool)

        @block.scalar
        def _(act):
            act.sem_inc(ot_done, 2)
            act.sem_inc(h2_done, 2)

            def run(b, s, has):
                u = b * SPB + s
                if has(3):
                    act.wait_ge(ot_read, u + 4)
                    act.wait_ge(o_read, u + 4 + 2)
                    for c in range(DC):
                        act.activation(o_t[:, (s + 1) % 2, c, :], ps_o[:, c, :], ACT.Copy).then_inc(ot_done, 1)
                if has(0):
                    act.wait_ge(lmax_done, u + 1)
                    act.activation(ex[:, :, :], lg[:, :, :], ACT.Exp).then_inc(ex_done, 1)
                if has(1):
                    act.wait_ge(h2_stored[(s + 1) % 2], b * 32 + (16 * ((s + 1) // 2) + 16))
                    for c in range(DC):
                        act.wait_ge(turned, u * DC + (c + 1 + DC))
                        act.activation(h2[:, (s + 1) % 2, c, :], ps_h[:, c, :], ACT.Copy).then_inc(h2_done, 1)

            steps_of(run, act)

        @block.vector
        def _(v):
            v.sem_inc(y_done, 1)
            v.sem_inc(x1_read, 2)
            v.sem_inc(at_done, 1)
            v.wait_ge(init, 4)

            def wide(a, m=E):
                return a.unsqueeze(2).to_broadcast([P, TPS, m])

            def gate_projection(u, slot, b):
                v.wait_ge(ot_read, u + 1 + 1)
                v.tensor_tensor(y[:, slot, :, :], ps_p[:, :, :], ga[:, ds(b, 1), :].to_broadcast([P, TPS, D]),
                                ALU.mult).then_inc(y_done, 1)

            def statistics(u, slot):
                v.wait_ge(x1_done, u + 1)
                for t in range(TPS):
                    last = v.bn_stats(stats[:, t, :], x1[:, slot, t, :])
                last.then_inc(dve_own, 1)
                v.wait_ge(dve_own, u + 1)
                stand_alone(v, held)
                for t in range(TPS):
                    last = v.bn_aggr(mv[:, t, :], stats[:, t, :])
                last.then_inc(stat_done, 1)

            def normalise(u, slot, rslot, b):
                v.wait_ge(rstd_done, u + 1)
                for t in range(TPS):
                    last = v.tensor_scalar(xn[:, t, :], x1[:, slot, t, :], mv[:, t, 0:1], rstd[:, t:t + 1],
                                           ALU.subtract, ALU.mult)
                last.then_inc(x1_read, 1)
                v.wait_ge(x1_read, u + 1 + 2)
                v.tensor_tensor(scaled[:, :, :], xn[:, :, :], cb_row[:, ds(b, 1), :].to_broadcast([P, TPS, D]),
                                ALU.mult).then_inc(scale_done, 1)
                v.wait_ge(scale_done, u + 1)
                v.wait_ge(rows_out, u + 1)
                v.tensor_tensor(rows[:, rslot, :, :], scaled[:, :, :], sb_row[:, ds(b, 1), :].to_broadcast([P, TPS, D]),
                                ALU.add).then_inc(rows_done, 1)

            def locate(u, rslot):
                n = [0]

                def step(ins):
                    n[0] += 1
                    ins.then_inc(locate_own, 1)
                    v.wait_ge(locate_own, u * LOCATE + n[0])

                v.wait_ge(ranked, u + 1)
                v.tensor_copy(totals[:, :], ps_all[:, :])
                step(v.tensor_tensor(place[:, :, :], ps_r, count[:, :].unsqueeze(1).to_broadcast([P, TPS, E]), ALU.add))
                for i in range(TOPK):
                    last = v.tensor_tensor(placed[:, i, :, :], hit[:, i, :, :], place[:, :, :], ALU.mult)
                step(last)
                v.tensor_tensor(count[:, :], totals[:, :], count[:, :], ALU.add)
                step(v.tensor_reduce(rank[:, :, :], placed[:, :, :, :], AX.X, ALU.add))
                v.tensor_copy(C["rank"][:, ds(u * TOPK, TOPK), :], rank[:, :, :])
                v.tensor_copy(C["which"][:, ds(u * TOPK, TOPK), :],
                              which_f[:, :, 0:TOPK].rearrange("p t i -> p i t"))
                step(v.scalar_tensor_tensor(at_f[:, :, :], which_f[:, :, 0:TOPK].rearrange("p t i -> p i t"),
                                            float(REGION), rank[:, :, :], ALU.mult, ALU.add))
                assert n[0] == LOCATE
                v.tensor_copy(at[:, rslot, :], at_f[:, :, :].rearrange("p i t -> p (i t)")).then_inc(at_done, 1)
                v.wait_ge(at_done, u + 2)

            def less_maximum(u):
                v.wait_ge(logits, u + 1)
                v.tensor_reduce(lmax[:, :], ps_l[:, :, :], AX.X, ALU.max).then_inc(max_own, 1)
                v.wait_ge(max_own, u + 1)
                v.tensor_tensor(lg[:, :, :], ps_l[:, :, :], wide(lmax[:, :]), ALU.subtract).then_inc(lmax_done, 1)

            def choose(u):
                n = [0]

                def step(ins):
                    n[0] += 1
                    ins.then_inc(route, 1)
                    v.wait_ge(route, u * ROUTE + n[0])

                v.wait_ge(ex_done, u + 1)
                step(v.tensor_reduce(z[:, :], ex[:, :, :], AX.X, ALU.add))
                step(v.reciprocal(rz[:, :], z[:, :]))
                step(v.tensor_tensor(sc[:, :, :], ex[:, :, :], wide(rz[:, :]), ALU.mult))
                stand_alone(v, held)
                for t in range(TPS):
                    last = v.max(best[:, t, :], sc[:, t, :])
                step(last)
                stand_alone(v, held)
                for t in range(TPS):
                    last = v.max_index(which[:, t, :], best[:, t, :], sc[:, t, :])
                step(last)
                step(v.tensor_copy(which_f[:, :, :], which[:, :, :]))
                step(v.tensor_tensor(s2[:, :], best[:, :, 0], best[:, :, 1], ALU.add))
                step(v.tensor_scalar(s2[:, :], s2[:, :], 1e-20, None, ALU.add))
                step(v.reciprocal(r2[:, :], s2[:, :]))
                v.scalar_tensor_tensor(w2[:, :, :], best[:, :, 0:2], ROUTE_SCALE, wide(r2[:, :], 2), ALU.mult, ALU.mult)
                for i in range(TOPK):
                    last = v.tensor_tensor(hit[:, i, :, :], iota[:, :, :], wide(which_f[:, :, i]), ALU.is_equal)
                step(last)
                step(v.tensor_copy(C["weight"][:, ds(u * TPS, TPS), :], w2[:, :, :]))
                v.tensor_tensor(chosen[:, :, :], hit[:, 0, :, :], hit[:, 1, :, :], ALU.add).then_inc(chosen_done, 1)
                assert n[0] == ROUTE

            def run(b, s, has):
                u = b * SPB + s
                if has(2):
                    gate_projection(u + 2, s % 2, b + (s + 2) // SPB)
                if has(1):
                    statistics(u + 1, (s + 1) % 2)
                if has(-1):
                    locate(u - 1, (s - 1) % RSLOTS)
                if has(0):
                    less_maximum(u)
                if has(1):
                    normalise(u + 1, (s + 1) % 2, (s + 1) % RSLOTS, b + (s + 1) // SPB)
                if has(0):
                    choose(u)

            v.wait_ge(consts, 48)
            steps_of(run, v)

            v.wait_ge(at_done, NST + 1)
            n = [0]

            def step(ins):
                n[0] += 1
                ins.then_inc(step_done, 1)
                v.wait_ge(step_done, n[0])

            def each(a):
                return a.unsqueeze(1).to_broadcast([P, NB, E])

            v.wait_ge(tables_in, 32)
            step(v.tensor_tensor(over[:, :, :], count[:, :].unsqueeze(2).to_broadcast([P, E, MOST]), steps[:, :, :],
                                 ALU.is_gt))
            step(v.tensor_reduce(blocks[:, :], over[:, :, :], AX.X, ALU.add))
            step(v.tensor_copy(ends[:, 0, :], blocks[:, :]))
            for k in range(3):
                by = 1 << k
                v.tensor_copy(ends[:, k + 1, 0:by], ends[:, k, 0:by])
                step(v.tensor_tensor(ends[:, k + 1, by:E], ends[:, k, by:E], ends[:, k, 0:E - by], ALU.add))
            end = ends[:, 3, :]
            step(v.tensor_tensor(start[:, :], end, blocks[:, :], ALU.subtract))
            step(v.tensor_scalar(start_row[:, :], start[:, :], float(ST), None, ALU.mult))
            v.tensor_tensor(past[:, 0, :, :], tables[:, 0, :, :], each(start[:, :]), ALU.is_ge)
            step(v.tensor_tensor(past[:, 1, :, :], tables[:, 0, :, :], each(end), ALU.is_ge))
            v.tensor_tensor(row_e[:, 0, :, :], tables[:, 1, :, :], each(start_row[:, :]), ALU.subtract)
            step(v.tensor_tensor(inside[:, :, :], past[:, 0, :, :], past[:, 1, :, :], ALU.subtract))
            v.tensor_tensor(row_e[:, 0, :, :], row_e[:, 0, :, :], inside[:, :, :], ALU.mult)
            step(v.tensor_tensor(row_e[:, 1, :, :], tables[:, 2, :, :], inside[:, :, :], ALU.mult))
            step(v.tensor_reduce(plan_f[:, :, :], row_e[:, :, :, :], AX.X, ALU.add))
            v.tensor_tensor(pad_f[:, :], tables[:, 1, 0, :], count[:, :], ALU.add)
            step(v.tensor_copy(plan[:, :, :], plan_f[:, :, :]))
            v.tensor_copy(pad_at[:, :], pad_f[:, :]).then_inc(planned, 1)
            every = [P, NST * TOPK * TPS, E]
            flat = "p a t -> p (a t)"
            step(v.tensor_tensor(mine[:, :, :], C["which"][:, :, :].rearrange(flat).unsqueeze(2).to_broadcast(every),
                                 tables[:, 2, 0, :].unsqueeze(1).to_broadcast(every), ALU.is_equal))
            step(v.tensor_tensor(mine[:, :, :], mine[:, :, :], start_row[:, :].unsqueeze(1).to_broadcast(every),
                                 ALU.mult))
            step(v.tensor_reduce(made_f[:, :], mine[:, :, :], AX.X, ALU.add))
            step(v.tensor_tensor(made_f[:, :], made_f[:, :], C["rank"][:, :, :].rearrange(flat), ALU.add))
            v.tensor_copy(C["made_at"][:, :, :].rearrange(flat), made_f[:, :])

        @block.tensor
        def _(pe):
            pe.sem_inc(o_read, 2)
            pe.sem_inc(ot_read, 1)

            def front(u, slot, turn):
                pe.wait_ge(in_done[slot], turn * (16 * IN_DMAS))
                pe.wait_ge(ot_done, u * DC + DC)
                for c in range(DC):
                    for t in range(TPS):
                        last = pe.transpose(ps_o[:, c, t * P:(t + 1) * P], o_in[:, slot, t, c * P:(c + 1) * P], ident[:, :])
                last.then_inc(o_read, 1)
                pe.wait_ge(ot_done, u * DC + (DC + 2))
                pe.wait_ge(y_done, u + 1)
                for t in range(TPS):
                    for c in range(DC):
                        last = pe.matmul(ps_p[:, t, :], o_t[:, slot, c, t * P:(t + 1) * P], wp[:, c, :],
                                         start=(c == 0), stop=(c == DC - 1))
                last.then_inc(ot_read, 1)

            def back(u, slot, rslot):
                pe.wait_ge(rows_done, u + 1)
                pe.wait_ge(h2_done, u * DC + DC)
                for c in range(DC):
                    for t in range(TPS):
                        last = pe.transpose(ps_h[:, c, t * P:(t + 1) * P], rows[:, rslot, t, c * P:(c + 1) * P], ident[:, :])
                    last.then_inc(turned, 1)
                pe.wait_ge(h2_done, u * DC + (DC + 2))
                for t in range(TPS):
                    for c in range(DC):
                        last = pe.matmul(ps_l[:, t, :], h2[:, slot, c, t * P:(t + 1) * P], gate_t[:, c, :],
                                         start=(c == 0), stop=(c == DC - 1))
                last.then_inc(logits, 1)

            def ranks(u):
                pe.wait_ge(chosen_done, u + 1)
                pe.wait_ge(at_done, u + 1)
                for t in range(TPS + 1):
                    terms = [(ones, before) for before in range(t)] + ([(strict, t)] if t < TPS else [])
                    for i, (lhs, tile) in enumerate(terms):
                        last = pe.matmul(ps_rank[:, t, :], lhs[:, :], chosen[:, tile, :], start=(i == 0),
                                         stop=(i == len(terms) - 1))
                last.then_inc(ranked, 1)

            def run(b, s, has):
                u = b * SPB + s
                if has(-1):
                    ranks(u - 1)
                if has(3):
                    front(u + 3, (s + 1) % 2, b * 2 + ((s + 3) // 2 + 1))
                if has(1):
                    back(u + 1, (s + 1) % 2, (s + 1) % RSLOTS)

            pe.wait_ge(consts, 48)
            pe.wait_ge(init, 4)
            steps_of(run, pe)


def expert_stage(nc, C, rows_dram, made_dram, w_gate, w_up, w_down):
    NC = -(-F // P)
    full = F // P
    WDMAS = 2 * DC + 2
    with ExitStack() as ctx:
        def sb(name, shape, dt=F32):
            return ctx.enter_context(nc.sbuf_tensor(name, shape, dt))

        def ps(name, shape, dt=F32):
            return ctx.enter_context(nc.psum_tensor(name, shape, dt))

        def sem(name):
            return ctx.enter_context(nc.semaphore(name))

        ident, plan = C["ident"], C["plan"]
        x_r = sb("x_r", [P, 2, TPS, D])
        wg = sb("wg", [P, 2, DC, NC * P])
        wu = sb("wu", [P, 2, DC, NC * P])
        wd = sb("wd", [P, 2, NC, D])
        x_t = [sb(f"x_t_{part}", [P, 2, DC, ST], F32R) for part in PARTS]
        wg_p = [sb(f"wg_{part}", [P, 2, DC, NC * P], F32R) for part in PARTS]
        wu_p = [sb(f"wu_{part}", [P, 2, DC, NC * P], F32R) for part in PARTS]
        wd_p = [sb(f"wd_{part}", [P, 2, NC, D], F32R) for part in PARTS]
        act_g = sb("act_g", [P, 2, ST])
        hid_f = sb("hid_f", [P, 2, ST])
        hid = [sb(f"hid_{part}", [P, NC, ST], F32R) for part in PARTS]
        made = sb("made", [P, 2, TPS, D])
        ps_g = ps("ps_g4", [P, 2, ST])
        ps_u = ps("ps_u4", [P, 2, ST])
        ps_d = ps("ps_d4", [P, TPS, D])
        ps_x = ps("ps_x4", [P, DC, ST])

        held = sem("p4_held")
        x_in = [sem(f"p4_x_in{i}") for i in range(2)]
        w_in = [sem(f"p4_w_in{i}") for i in range(2)]
        x_turned = sem("p4_x_turned")
        xt_high = sem("p4_xt_high")
        xt_done = sem("p4_xt")
        padded = sem("p4_padded")
        w_high = sem("p4_w_high")
        wg_done = sem("p4_wg")
        wu_done = sem("p4_wu")
        wd_done = sem("p4_wd")
        product = sem("p4_product")
        hid_high = sem("p4_hid_high")
        gu_done = sem("p4_gu")
        silu_done = sem("p4_silu")
        hid_done = sem("p4_hid")
        down_done = sem("p4_down")
        made_done = sem("p4_made")
        made_stored = [sem(f"p4_stored{i}") for i in range(2)]

        block = ctx.enter_context(nc.Block())

        @block.sync
        def _(sp):
            for slot in range(2):
                sp.sem_inc(made_stored[slot], 16)

            def load(j, slot, reused):
                row = sp.value_load(plan[0:1, 0, ds(j, 1)], min_val=0, max_val=E * REGION - ST)
                e = sp.value_load(plan[0:1, 1, ds(j, 1)], min_val=0, max_val=E - 1)
                if reused:
                    sp.wait_ge(wg_done, j)
                    sp.wait_ge(wu_done, j)
                    sp.wait_ge(wd_done, j)
                for c in range(DC):
                    for w, src in ((wg, w_gate), (wu, w_up)):
                        sp.dma_start(w[:, slot, c, 0:F], src[ds(e, 1), c * P:(c + 1) * P, :]
                                     .rearrange("o p f -> (o p) f")).then_inc(w_in[slot], 16)
                sp.dma_start(wd[:, slot, 0:full, :], w_down[ds(e, 1), 0:full * P, :]
                             .rearrange("o (j p) n -> p (o j) n", p=P)).then_inc(w_in[slot], 16)
                sp.dma_start(wd[0:F - full * P, slot, full, :], w_down[ds(e, 1), full * P:F, :]
                             .rearrange("o p n -> (o p) n")).then_inc(w_in[slot], 16)
                if reused:
                    sp.wait_ge(x_turned, j * DC)
                sp.dma_start(x_r[:, slot, :, :], rows_dram[ds(row, ST), :].rearrange("(t p) d -> p t d", p=P)) \
                    .then_inc(x_in[slot], 16)

            def body(it, slots, loads):
                for slot in slots:
                    j = it * 2 + slot
                    if slot in loads:
                        load(j + 2, slot, True)
                    sp.wait_ge(made_done, j + 2)
                    sp.dma_start(made_dram[ds(j * ST, ST), :].rearrange("(t p) d -> p t d", p=P), made[:, slot, :, :]) \
                        .then_inc(made_stored[slot], 16)

            sp.wait_ge(padded, 3)
            for slot in range(2):
                load(slot, slot, False)
            assert NB % 2 == 1
            with sp.Fori(0, NB // 2 - 1) as it:
                body(it, (0, 1), (0, 1))
            body(NB // 2 - 1, (0, 1), (0,))
            body(NB // 2, (0,), ())
            for slot in range(2):
                sp.wait_ge(made_stored[slot], 16 * ((NB + 1 - slot) // 2 + 1))

        @block.gpsimd
        def _(pool):
            for w in (wg, wu):
                pool.memset(w[:, :, :, F:NC * P], 0.0).then_inc(padded, 1)
            pool.wait_ge(padded, 2)
            pool.memset(wd[F - full * P:P, :, full, :], 0.0).then_inc(padded, 1)
            pool.wait_ge(padded, 3)
            pool.sem_inc(wu_done, 1)
            pool.sem_inc(wd_done, 1)

            def low_weights(j, slot):
                pool.wait_ge(w_high, j * 3 + 2)
                stand_alone(pool, held)
                pool.tensor_tensor(wu_p[1][:, slot, :, :], wu[:, slot, :, :], wu_p[0][:, slot, :, :], ALU.subtract) \
                    .then_inc(wu_done, 1)
                pool.wait_ge(w_high, j * 3 + 3)
                stand_alone(pool, held)
                pool.tensor_tensor(wd_p[1][:, slot, :, :], wd[:, slot, :, :], wd_p[0][:, slot, :, :], ALU.subtract) \
                    .then_inc(wd_done, 1)

            with pool.Fori(0, NB // 2) as it:
                for slot in range(2):
                    low_weights(it * 2 + slot, slot)
            low_weights(NB - 1, 0)

        @block.scalar
        def _(act):
            act.sem_inc(silu_done, 2)
            act.wait_ge(padded, 3)

            def high_rows(j, slot):
                for c in range(DC):
                    act.wait_ge(x_turned, j * DC + (c + 1 + DC))
                    act.activation(x_t[0][:, slot, c, :], ps_x[:, c, :], ACT.Copy).then_inc(xt_high, 1)

            def high_weights(j, slot, turn_no):
                act.wait_ge(w_in[slot], turn_no * (16 * WDMAS))
                act.wait_ge(down_done, j * NC + 1)
                for src, dst in ((wg, wg_p), (wu, wu_p)):
                    act.activation(dst[0][:, slot, :, :], src[:, slot, :, :], ACT.Copy).then_inc(w_high, 1)

            def high_down(slot):
                act.activation(wd_p[0][:, slot, :, :], wd[:, slot, :, :], ACT.Copy).then_inc(w_high, 1)

            def body(it, slots, last):
                for slot in slots:
                    j = it * 2 + slot
                    for i in range(NC):
                        half = (slot + i) % 2
                        act.wait_ge(gu_done, j * NC + (i + 1))
                        act.wait_ge(product, j * NC + (i + 1))
                        act.activation(act_g[:, half, :], ps_g[:, half, :], ACT.Silu).then_inc(silu_done, 1)
                        if i == 1 and not last:
                            high_rows(j + 1, 1 - slot)
                            high_weights(j + 1, 1 - slot, it + (1 + slot))
                        if i == 2 and not last:
                            high_down(1 - slot)

            high_weights(0, 0, 1)
            high_down(0)
            high_rows(0, 0)
            with act.Fori(0, NB // 2) as it:
                body(it, (0, 1), False)
            body(NB // 2, (0,), True)

        @block.vector
        def _(v):
            v.sem_inc(hid_done, 2)
            v.sem_inc(product, 2)
            v.sem_inc(made_done, 1)
            v.sem_inc(xt_done, DC)
            v.sem_inc(wg_done, 1)

            def low_rows(j, slot):
                for c in range(DC):
                    v.wait_ge(xt_high, j * DC + (c + 1))
                    v.tensor_tensor(x_t[1][:, slot, c, :], ps_x[:, c, :], x_t[0][:, slot, c, :], ALU.subtract) \
                        .then_inc(xt_done, 1)

            def low_gate(j, slot):
                v.wait_ge(w_high, j * 3 + 1)
                v.tensor_tensor(wg_p[1][:, slot, :, :], wg[:, slot, :, :], wg_p[0][:, slot, :, :], ALU.subtract) \
                    .then_inc(wg_done, 1)

            def hidden(j, i, half):
                n = j * NC + i
                v.wait_ge(silu_done, n + 1 + 2)
                v.wait_ge(hid_done, n + 1)
                v.tensor_tensor(hid_f[:, half, :], act_g[:, half, :], ps_u[:, half, :], ALU.mult).then_inc(product, 1)
                v.wait_ge(product, n + 1 + 2)
                v.wait_ge(down_done, n + 1)
                v.tensor_copy(hid[0][:, i, :], hid_f[:, half, :]).then_inc(hid_high, 1)
                v.wait_ge(hid_high, n + 1)
                v.tensor_tensor(hid[1][:, i, :], hid_f[:, half, :], hid[0][:, i, :], ALU.subtract).then_inc(hid_done, 1)

            def body(it, slots, last):
                for slot in slots:
                    j = it * 2 + slot
                    for i in range(NC):
                        hidden(j, i, (slot + i) % 2)
                        if i == 1 and not last:
                            low_rows(j + 1, 1 - slot)
                            low_gate(j + 1, 1 - slot)
                    v.wait_ge(down_done, j * NC + 2 * NC)
                    v.wait_ge(made_stored[slot], it * 16 + 16)
                    v.tensor_copy(made[:, slot, :, :], ps_d[:, :, :]).then_inc(made_done, 1)

            low_gate(0, 0)
            low_rows(0, 0)
            with v.Fori(0, NB // 2) as it:
                body(it, (0, 1), False)
            body(NB // 2, (0,), True)

        @block.tensor
        def _(pe):
            pe.sem_inc(x_turned, DC)
            pe.sem_inc(down_done, NC)

            def turn(j, slot, turn_no):
                pe.wait_ge(x_in[slot], turn_no * 16)
                pe.wait_ge(xt_done, j * DC + DC)
                for c in range(DC):
                    for t in range(TPS):
                        last = pe.transpose(ps_x[:, c, t * P:(t + 1) * P], x_r[:, slot, t, c * P:(c + 1) * P], ident[:, :])
                    last.then_inc(x_turned, 1)

            def up(j, i, slot):
                half = (slot + i) % 2
                if i == 0:
                    pe.wait_ge(wg_done, j + 2)
                    pe.wait_ge(wu_done, j + 2)
                    pe.wait_ge(xt_done, j * DC + 2 * DC)
                pe.wait_ge(silu_done, j * NC + (i + 1))
                pe.wait_ge(product, j * NC + (i + 1))
                for w, dst in ((wg_p, ps_g), (wu_p, ps_u)):
                    for k, (c, (a, b)) in enumerate((c, parts) for c in range(DC) for parts in PRODUCTS):
                        last = pe.matmul(dst[:, half, :], w[a][:, slot, c, i * P:(i + 1) * P], x_t[b][:, slot, c, :],
                                         start=(k == 0), stop=(k == DC * len(PRODUCTS) - 1))
                last.then_inc(gu_done, 1)

            def down(j, i, slot):
                if i == 0:
                    pe.wait_ge(wd_done, j + 2)
                    pe.wait_ge(made_done, j + 1)
                pe.wait_ge(hid_done, j * NC + (i + 1 + 2))
                for t in range(TPS):
                    for k, (a, b) in enumerate(PRODUCTS):
                        last = pe.matmul(ps_d[:, t, :], hid[a][:, i, t * P:(t + 1) * P], wd_p[b][:, slot, i, :],
                                         start=(i == 0 and t % 2 == 0 and k == 0),
                                         stop=(i == NC - 1 and k == len(PRODUCTS) - 1), skip_group_check=True)
                last.then_inc(down_done, 1)

            def body(it, slots, last):
                for slot in slots:
                    j = it * 2 + slot
                    for i in range(NC):
                        up(j, i, slot)
                        if i > 0:
                            down(j, i - 1, slot)
                        if i == 1 and not last:
                            turn(j + 1, 1 - slot, it + (1 + slot))
                    down(j, NC - 1, slot)

            turn(0, 0, 1)
            with pe.Fori(0, NB // 2) as it:
                body(it, (0, 1), False)
            body(NB // 2, (0,), True)


def shared_stage(nc, C, h2_dram, x1_dram, made_dram, sw_gate, sw_up, sw_down, out_flat):
    NC = -(-FS // P)
    full = FS // P
    GS = 3
    PICKS = TOPK * TPS
    with ExitStack() as ctx:
        def sb(name, shape, dt=F32):
            return ctx.enter_context(nc.sbuf_tensor(name, shape, dt))

        def ps(name, shape, dt=F32):
            return ctx.enter_context(nc.psum_tensor(name, shape, dt))

        def sem(name):
            return ctx.enter_context(nc.semaphore(name))

        gb, weight, made_at = C["gb"], C["weight"], C["made_at"]
        wg = sb("sg_w", [P, DC, NC * P])
        wu = sb("su_w", [P, DC, NC * P])
        wd = sb("sd_w", [P, NC, D])
        wg_p = [sb(f"sg_{part}", [P, DC, NC * P], F32R) for part in PARTS]
        wu_p = [sb(f"su_{part}", [P, DC, NC * P], F32R) for part in PARTS]
        wd_p = [sb(f"sd_{part}", [P, NC, D], F32R) for part in PARTS]
        h2_p = [sb(f"h2_{part}", [P, 2, DC, ST], F32R) for part in PARTS]
        h2 = sb("h2_5", [P, 2, DC, ST])
        x1 = sb("x1_5", [P, 2, TPS, D])
        at_now = sb("at_now", [P, 2, PICKS], U32)
        got = sb("got", [P, 2, PICKS, D])
        act_g = sb("act_g5", [P, 2, ST])
        hid_f = sb("hid_f5", [P, 2, ST])
        hid = [sb(f"hid5_{part}", [P, GS, ST], F32R) for part in PARTS]
        first = sb("first", [P, TPS, D])
        mix = sb("mix", [P, TPS, D])
        total = sb("total", [P, TPS, D])
        gated = sb("gated", [P, TPS, D])
        y_out = sb("y_out", [P, TPS, D])
        weight_now = sb("weight_now", [P, 2 * TPS, TOPK])
        gb_now = sb("gb_now", [P, D])
        ps_g = ps("ps_g5", [P, 2, ST])
        ps_u = ps("ps_u5", [P, 2, ST])
        ps_d = ps("ps_d5", [P, 2, TPS, D])

        held = sem("p5_held")
        padded = sem("p5_padded")
        w_in = sem("p5_weights")
        w_high = sem("p5_w_high")
        w_done = sem("p5_w")
        h2_high = sem("p5_h2_high")
        h2_done = sem("p5_h2")
        product = sem("p5_product")
        hid_high = sem("p5_hid_high")
        in_done = [sem(f"p5_in{i}") for i in range(2)]
        at_copied = sem("p5_at")
        gathered = [sem(f"p5_gathered{i}") for i in range(2)]
        got_used = sem("p5_got_used")
        h2_read = sem("p5_h2_read")
        out_done = sem("p5_out")
        gu_done = sem("p5_gu")
        silu_done = sem("p5_silu")
        hid_done = sem("p5_hid")
        down_done = sem("p5_down")
        now = sem("p5_now")
        first_done = sem("p5_first")
        mixed = sem("p5_mixed")
        summed = sem("p5_summed")
        gated_done = sem("p5_gated")
        stored = sem("p5_stored")
        W_DMAS = 4

        block = ctx.enter_context(nc.Block())

        @block.sync
        def _(sp):
            sp.wait_ge(padded, 3)
            sp.dma_start(wg[:, :, 0:FS], sw_gate.rearrange("(c p) f -> p c f", p=P)).then_inc(w_in, 16)
            sp.dma_start(wu[:, :, 0:FS], sw_up.rearrange("(c p) f -> p c f", p=P)).then_inc(w_in, 16)
            sp.dma_start(wd[:, 0:full, :], sw_down[0:full * P, :].rearrange("(j p) n -> p j n", p=P)).then_inc(w_in, 16)
            sp.dma_start(wd[0:FS - full * P, full, :], sw_down[full * P:FS, :]).then_inc(w_in, 16)

            def load(u, slot):
                sp.wait_ge(h2_done, u + 1)
                sp.wait_ge(out_done, u + 1)
                sp.dma_start(h2[:, slot, :, :].rearrange("p c t -> p (c t)"), h2_dram[ds(u * P, P), :]) \
                    .then_inc(in_done[slot], 16)
                sp.dma_start(x1[:, slot, :, :], x1_dram[ds(u * ST, ST), :].rearrange("(t p) d -> p t d", p=P)) \
                    .then_inc(in_done[slot], 16)

            def body(it, last):
                for slot in range(2):
                    u = it * 2 + slot
                    if not (last and slot):
                        load(u + 1, 1 - slot)
                    sp.wait_ge(out_done, u + 1 + 2)
                    sp.dma_start(out_flat[ds(u * ST, ST), :].rearrange("(t p) d -> p t d", p=P), y_out[:, :, :]) \
                        .then_inc(stored, 16)

            sp.sem_inc(stored, 16)
            load(0, 0)
            with sp.Fori(0, NST // 2 - 1) as it:
                body(it, False)
            body(NST // 2 - 1, True)
            sp.wait_ge(stored, 16 * (NST + 1))

        @block.gpsimd
        def _(pool):
            for w in (wg, wu):
                pool.memset(w[:, :, FS:NC * P], 0.0).then_inc(padded, 1)
            pool.wait_ge(padded, 2)
            pool.memset(wd[FS - full * P:P, full, :], 0.0).then_inc(padded, 1)
            pool.wait_ge(padded, 3)
            pool.sem_inc(out_done, 2)

            def gather(u, slot):
                pool.wait_ge(got_used, u + 1)
                stand_alone(pool, held)
                pool.tensor_copy(at_now[:, slot, :].rearrange("p (i t) -> p i t", i=TOPK),
                                 made_at[:, ds(u * TOPK, TOPK), :]).then_inc(at_copied, 1)
                pool.wait_ge(at_copied, u + 1)
                stand_alone(pool, held)
                for j in range(PICKS):
                    pool.indirect_dma_start(got[:, slot, j, :], None, made_dram,
                                            bass.IndirectOffsetOnAxis(at_now[:, slot, j:j + 1], 0)) \
                        .then_inc(gathered[slot], 16)

            def body(it, last):
                for slot in range(2):
                    u = it * 2 + slot
                    if not (last and slot):
                        gather(u + 1, 1 - slot)
                    pool.wait_ge(in_done[slot], it * 32 + 32)
                    pool.wait_ge(gated_done, u + 1 + 1)
                    pool.wait_ge(stored, u * 16 + 16)
                    pool.tensor_tensor(y_out[:, :, :], gated[:, :, :], x1[:, slot, :, :], ALU.add).then_inc(out_done, 1)

            gather(0, 0)
            with pool.Fori(0, NST // 2 - 1) as it:
                body(it, False)
            body(NST // 2 - 1, True)

        @block.scalar
        def _(act):
            act.sem_inc(silu_done, 2)

            def high_rows(u, slot, turn_no):
                act.wait_ge(in_done[slot], turn_no * 32)
                act.wait_ge(h2_read, u + 1)
                act.activation(h2_p[0][:, slot, :, :], h2[:, slot, :, :], ACT.Copy).then_inc(h2_high, 1)

            def body(it, last):
                for slot in range(2):
                    u = it * 2 + slot
                    for i in range(NC):
                        act.wait_ge(gu_done, u * NC + (i + 1))
                        act.wait_ge(product, u * NC + (i + 1))
                        act.activation(act_g[:, i % 2, :], ps_g[:, i % 2, :], ACT.Silu).then_inc(silu_done, 1)
                        if i == 2 and not (last and slot):
                            high_rows(u + 1, 1 - slot, it + (1 + slot))

            act.wait_ge(w_in, 16 * W_DMAS)
            act.wait_ge(padded, 3)
            for src, dst in ((wg, wg_p), (wu, wu_p), (wd, wd_p)):
                act.activation(dst[0][:, :, :], src[:, :, :], ACT.Copy).then_inc(w_high, 1)
            high_rows(0, 0, 1)
            with act.Fori(0, NST // 2 - 1) as it:
                body(it, False)
            body(NST // 2 - 1, True)

        @block.vector
        def _(v):
            v.sem_inc(hid_done, 2)
            v.sem_inc(product, 2)
            v.sem_inc(h2_done, 2)
            v.sem_inc(got_used, 2)
            v.sem_inc(gated_done, 1)
            v.sem_inc(summed, 2)

            def mix_experts(u, slot, it):
                v.wait_ge(gathered[slot], it * (16 * PICKS) + 16 * PICKS)
                for t in range(TPS):
                    last = v.tensor_scalar(first[:, t, :], got[:, slot, t, :], weight_now[:, slot * TPS + t, 0:1], None,
                                           ALU.mult)
                last.then_inc(first_done, 1)
                v.wait_ge(first_done, u + 1)
                v.wait_ge(summed, u + 2)
                for t in range(TPS):
                    last = v.scalar_tensor_tensor(mix[:, t, :], got[:, slot, TPS + t, :],
                                                  weight_now[:, slot * TPS + t, 1:2], first[:, t, :], ALU.mult, ALU.add)
                last.then_inc(got_used, 1)

            def hidden(u, i):
                n = u * NC + i
                v.wait_ge(silu_done, n + 1 + 2)
                v.wait_ge(hid_done, n + 1)
                v.tensor_tensor(hid_f[:, i % 2, :], act_g[:, i % 2, :], ps_u[:, i % 2, :], ALU.mult).then_inc(product, 1)
                v.wait_ge(product, n + 1 + 2)
                v.wait_ge(down_done, n + 1)
                v.tensor_copy(hid[0][:, i % GS, :], hid_f[:, i % 2, :]).then_inc(hid_high, 1)
                v.wait_ge(hid_high, n + 1)
                v.tensor_tensor(hid[1][:, i % GS, :], hid_f[:, i % 2, :], hid[0][:, i % GS, :], ALU.subtract) \
                    .then_inc(hid_done, 1)

            def low_rows(u, slot):
                v.wait_ge(h2_high, u + 1)
                v.tensor_tensor(h2_p[1][:, slot, :, :], h2[:, slot, :, :], h2_p[0][:, slot, :, :], ALU.subtract) \
                    .then_inc(h2_done, 1)

            def body(it, last):
                v.wait_ge(gated_done, it * 2 + 1)
                v.wait_ge(got_used, it * 2 + 2)
                v.tensor_copy(weight_now[:, :, :], weight[:, ds(it * (2 * TPS), 2 * TPS), :])
                v.tensor_copy(gb_now[:, :], gb[:, ds(it, 1), :].rearrange("p o d -> p (o d)")).then_inc(now, 1)
                v.wait_ge(now, it + 1)
                for slot in range(2):
                    u = it * 2 + slot
                    for i in range(NC):
                        hidden(u, i)
                        if i == 2 and not (last and slot):
                            low_rows(u + 1, 1 - slot)
                        if i == NC - 3:
                            mix_experts(u, slot, it)
                    v.wait_ge(down_done, u * NC + (NC + GS))
                    v.wait_ge(got_used, u + 3)
                    v.wait_ge(gated_done, u + 1)
                    v.tensor_tensor(total[:, :, :], ps_d[:, slot, :, :], mix[:, :, :], ALU.add).then_inc(summed, 1)
                    v.wait_ge(summed, u + 3)
                    v.wait_ge(out_done, u + 2)
                    v.tensor_tensor(gated[:, :, :], total[:, :, :], gb_now[:, :].unsqueeze(1).to_broadcast([P, TPS, D]),
                                    ALU.mult).then_inc(gated_done, 1)

            for k, (src, dst) in enumerate(((wg, wg_p), (wu, wu_p), (wd, wd_p))):
                v.wait_ge(w_high, k + 1)
                v.tensor_tensor(dst[1][:, :, :], src[:, :, :], dst[0][:, :, :], ALU.subtract).then_inc(w_done, 1)
            low_rows(0, 0)
            with v.Fori(0, NST // 2 - 1) as it:
                body(it, False)
            body(NST // 2 - 1, True)

        @block.tensor
        def _(pe):
            pe.sem_inc(h2_read, 2)
            pe.sem_inc(down_done, GS)

            def up(u, i, slot):
                pe.wait_ge(silu_done, u * NC + (i + 1))
                pe.wait_ge(product, u * NC + (i + 1))
                for w, dst in ((wg_p, ps_g), (wu_p, ps_u)):
                    for k, (c, (a, b)) in enumerate((c, parts) for c in range(DC) for parts in PRODUCTS):
                        last = pe.matmul(dst[:, i % 2, :], w[a][:, c, i * P:(i + 1) * P], h2_p[b][:, slot, c, :],
                                         start=(k == 0), stop=(k == DC * len(PRODUCTS) - 1))
                last.then_inc(gu_done, 1)

            def down(u, i, slot):
                if i == 0:
                    pe.wait_ge(summed, u + 1)
                pe.wait_ge(hid_done, u * NC + (i + 1 + 2))
                for t in range(TPS):
                    for k, (a, b) in enumerate(PRODUCTS):
                        last = pe.matmul(ps_d[:, slot, t, :], hid[a][:, i % GS, t * P:(t + 1) * P], wd_p[b][:, i, :],
                                         start=(i == 0 and t % 2 == 0 and k == 0),
                                         stop=(i == NC - 1 and k == len(PRODUCTS) - 1), skip_group_check=True)
                last.then_inc(down_done, 1)
                if i == NC - 1:
                    pe.wait_ge(down_done, u * NC + (NC + GS))
                    pe.sem_inc(h2_read, 1)

            pe.wait_ge(w_done, 3)
            with pe.Fori(0, NST // 2) as it:
                for slot in range(2):
                    u = it * 2 + slot
                    pe.wait_ge(h2_done, u + 3)
                    for i in range(NC):
                        up(u, i, slot)
                        if i > 0:
                            down(u, i - 1, slot)
                    down(u, NC - 1, slot)


_INS = ['L0_attn_x', 'L0_attn_w_qkv', 'L0_attn_w_proj', 'L0_attn_b_proj', 'L0_ffn_gate_w', 'L0_ffn_w_gate',
        'L0_ffn_w_up', 'L0_ffn_w_down', 'L0_ffn_sw_gate', 'L0_ffn_sw_up', 'L0_ffn_sw_down', 'L0_c', 'L0_wmod']


def kernel(**inputs):
    import numpy as _np
    import concourse.bacc as _bacc
    from concourse import mybir as _mybir
    from concourse.bass_utils import run_bass_kernel_spmd as _run

    nc = _bacc.Bacc("TRN2", target_bir_lowering=False, num_devices=1)
    arrays, args = {}, []
    for name in _INS:
        a = _np.ascontiguousarray(inputs[name])
        arrays[f"in_{name}_dram"] = a
        args.append(nc.dram_tensor(f"in_{name}_dram", a.shape, _mybir.dt.from_np(a.dtype), kind="ExternalInput").ap())
    args.append(nc.dram_tensor("out_dram", (B, S, D), _mybir.dt.float32, kind="ExternalOutput").ap())
    block_kernel(nc, *args)
    r = _run(nc, [arrays], core_ids=[0])
    return r.results[0]["out_dram"]
```
